# Optimizing a Trainium2 kernel written in Bass

```python
import numpy as np
import jax
import jax.numpy as jnp

def _softmax(x, axis=-1):
    return jax.nn.softmax(x, axis=axis)

def _gelu(x):
    return jax.nn.gelu(x, approximate=True)

def _silu(x):
    return jax.nn.silu(x)

def _sigmoid(x):
    return jax.nn.sigmoid(x)

def _layernorm(x, axis=-1, eps=1e-05):
    m = jnp.mean(x, axis=axis, keepdims=True)
    v = jnp.var(x, axis=axis, keepdims=True)
    return (x - m) / jnp.sqrt(v + eps)

def _scatter_add(tgt, idx, src, axis=0):
    return tgt.at[idx].add(src)

def _segment_sum(src, seg, n):
    return jax.ops.segment_sum(src, seg, n)
kernel_name = 'mk_perceiver_d1_seqx_r2_716467'

def setup_inputs(seed: int=0):
    np.random.seed(seed)
    _w = jnp.asarray

    def _rec_inputs():
        import jax
        import jax.numpy as jnp
        _rk = jax.random.key(seed)
        x = -0.0005207 + 1.001 * jax.random.normal(jax.random.fold_in(_rk, 1), (8, 64, 1024), jnp.float32)
        _lenS = 64 - jax.random.randint(jax.random.fold_in(_rk, 7), (8,), 0, max(1, 64 // 4) + 1, jnp.int32)
        _lenS2 = 1601 - jax.random.randint(jax.random.fold_in(_rk, 8), (8,), 0, max(1, 1601 // 4) + 1, jnp.int32)
        _ctx_2048P = jax.random.normal(jax.random.fold_in(_rk, 12), (8, 16, 1024), jnp.float32)
        _ctx_2048c = jax.random.dirichlet(jax.random.fold_in(_rk, 512), 0.3 * jnp.ones((16,), jnp.float32), (8, 1601))
        _ctx_2048t = jnp.einsum('bsk,bkd->bsd', _ctx_2048c, _ctx_2048P)
        _ctx_2048t = _ctx_2048t * jax.lax.rsqrt(jnp.mean(jnp.square(_ctx_2048t)) + 1e-12) * 0.953939
        ctx_2048 = -5.72187e-05 + 0.999849 * (_ctx_2048t + 0.3 * jax.random.normal(jax.random.fold_in(_rk, 612), (8, 1601, 1024), jnp.float32))
        _validS = jnp.arange(64)[None, :] < _lenS[:, None]
        _validS2 = jnp.arange(1601)[None, :] < _lenS2[:, None]
        _causal = jnp.tril(jnp.ones((64, 64), dtype=bool))
        mask_BxSx4224_bf0 = jnp.logical_not(jnp.ones((8, 64, 2112), dtype=bool))
        return (x, ctx_2048, mask_BxSx4224_bf0)
    x, ctx_2048, mask_BxSx4224_bf0 = _rec_inputs()

    def _L0_xattn_setup():
        import jax, jax.numpy as jnp
        import numpy as np
        import math
        DIM = 1024
        B, Q_LEN, KV_LEN = (8, 128, 2048)
        key = jax.random.key(seed)
        ks = jax.random.split(key, 8)
        x = jax.random.normal(ks[0], (B, Q_LEN, DIM), dtype=jnp.float32)
        mask = jnp.zeros((B, Q_LEN, KV_LEN + Q_LEN), dtype=bool)
        k_cache = jax.random.normal(ks[1], (B, KV_LEN, DIM), dtype=jnp.float32)
        v_cache = jax.random.normal(ks[2], (B, KV_LEN, DIM), dtype=jnp.float32)
        scale = 1.0 / math.sqrt(DIM)
        wq = jax.random.normal(ks[3], (DIM, DIM), dtype=jnp.float32) * scale
        wk = jax.random.normal(ks[4], (DIM, DIM), dtype=jnp.float32) * scale
        wv = jax.random.normal(ks[5], (DIM, DIM), dtype=jnp.float32) * scale
        wo = jax.random.normal(ks[6], (DIM, DIM), dtype=jnp.float32) * scale
        return {'x': x, 'mask': mask, 'k_cache': k_cache, 'v_cache': v_cache, 'wq': wq, 'wk': wk, 'wv': wv, 'wo': wo}
    _L0_xattn_all = _L0_xattn_setup()
    _L0_xattn_in = {k: v for k, v in _L0_xattn_all.items() if k in ('wq', 'wk', 'wv', 'wo')}
    del _L0_xattn_all

    def _L0_attn_setup():
        import jax, jax.numpy as jnp
        import numpy as np
        B, S, E = (2, 1024, 1024)
        N_HEAD = 16
        HEAD_DIM = E // N_HEAD
        MP_NUM = 4
        ROTARY_DIM = 64

        def _rotate_every_two(x):
            x1 = x[..., 0::2]
            x2 = x[..., 1::2]
            return jnp.stack((-x2, x1), axis=-1).reshape(x.shape)
        key = jax.random.key(seed)
        k1, k2, k3 = jax.random.split(key, 3)
        return {'hidden_states': jax.random.normal(k1, (B, S, E), jnp.float32) * 0.02, 'w_qkv': jax.random.normal(k2, (3 * E, E), jnp.float32) * 0.02, 'w_out': jax.random.normal(k3, (E, E), jnp.float32) * 0.02}
    _L0_attn_all = _L0_attn_setup()
    _L0_attn_in = {k: v for k, v in _L0_attn_all.items() if k in ('w_qkv', 'w_out')}
    del _L0_attn_all

    def _L0_ffn_setup():
        import jax, jax.numpy as jnp
        import numpy as np
        GOLDEN_CENTER = 1.0 / np.e
        GOLDEN_LOWER = 0.5 - np.log(4.0 / 3.0)
        GOLDEN_UPPER = 0.5

        def _golden_weights(x, Wr, temperature):
            inh = jax.nn.sigmoid(x @ Wr / temperature)
            in_zone = (inh >= GOLDEN_LOWER) & (inh <= GOLDEN_UPPER)
            distance = jnp.abs(inh - GOLDEN_CENTER)
            weights = jnp.exp(-distance / 0.1) * in_zone.astype(x.dtype)
            wsum = jnp.sum(weights, axis=-1, keepdims=True)
            no_expert = wsum < 1e-08
            fb = jnp.exp(-distance / 0.3)
            _, top2 = jax.lax.top_k(fb, 2)
            fb_mask = jnp.sum(jax.nn.one_hot(top2, weights.shape[-1], dtype=x.dtype), axis=-2)
            fb_w = fb * fb_mask
            fb_w = fb_w / jnp.maximum(jnp.sum(fb_w, axis=-1, keepdims=True), 1e-08)
            weights = jnp.where(no_expert, fb_w, weights)
            weights = weights / jnp.maximum(jnp.sum(weights, axis=-1, keepdims=True), 1e-08)
            return weights
        key = jax.random.key(seed)
        ks = jax.random.split(key, 5)
        B, T, D, E, F = (2, 1024, 1024, 8, 1024)
        s_in = 1.0 / np.sqrt(D)
        s_f = 1.0 / np.sqrt(F)
        return {'x': jax.random.normal(ks[0], (B, T, D), dtype=jnp.float32), 'Wg': jax.random.normal(ks[1], (E, D, F), dtype=jnp.float32) * s_in, 'Wu': jax.random.normal(ks[2], (E, D, F), dtype=jnp.float32) * s_in, 'Wd': jax.random.normal(ks[3], (E, F, D), dtype=jnp.float32) * s_f, 'Wr': jax.random.normal(ks[4], (D, E), dtype=jnp.float32) * s_in, 'temperature': jnp.ones((1,), dtype=jnp.float32)}
    _L0_ffn_all = _L0_ffn_setup()
    _L0_ffn_in = {k: v for k, v in _L0_ffn_all.items() if k in ('Wg', 'Wu', 'Wd', 'Wr', 'temperature')}
    del _L0_ffn_all
    return {'x': x, 'ctx_2048': ctx_2048, 'mask_BxSx4224_bf0': mask_BxSx4224_bf0, 'L0_xattn_wq': _L0_xattn_in['wq'], 'L0_xattn_wk': _L0_xattn_in['wk'], 'L0_xattn_wv': _L0_xattn_in['wv'], 'L0_xattn_wo': _L0_xattn_in['wo'], 'L0_attn_w_qkv': _L0_attn_in['w_qkv'], 'L0_attn_w_out': _L0_attn_in['w_out'], 'L0_ffn_Wg': _L0_ffn_in['Wg'], 'L0_ffn_Wu': _L0_ffn_in['Wu'], 'L0_ffn_Wd': _L0_ffn_in['Wd'], 'L0_ffn_Wr': _L0_ffn_in['Wr'], 'L0_ffn_temperature': _L0_ffn_in['temperature']}

def reference(x, ctx_2048, mask_BxSx4224_bf0, L0_xattn_wq, L0_xattn_wk, L0_xattn_wv, L0_xattn_wo, L0_attn_w_qkv, L0_attn_w_out, L0_ffn_Wg, L0_ffn_Wu, L0_ffn_Wd, L0_ffn_Wr, L0_ffn_temperature):
    import jax
    import jax.numpy as jnp

    def _L0_xattn_ref(x, mask, k_cache, v_cache, wq, wk, wv, wo):
        import jax, jax.numpy as jnp
        import numpy as np
        import math
        DIM = 1024
        B, Q_LEN, KV_LEN = (8, 128, 2048)
        q = jnp.einsum('bsd,ed->bse', x, wq)
        k_new = jnp.einsum('bsd,ed->bse', x, wk)
        v_new = jnp.einsum('bsd,ed->bse', x, wv)
        k = jnp.concatenate([k_cache, k_new], axis=1)
        v = jnp.concatenate([v_cache, v_new], axis=1)
        scale = 1.0 / math.sqrt(q.shape[-1])
        scores = jnp.einsum('bqd,bkd->bqk', q, k) * scale
        attn = jax.nn.softmax(scores, axis=-1)
        out = jnp.einsum('bqk,bkd->bqd', attn, v)
        return jnp.einsum('bqd,ed->bqe', out, wo)

    def _L0_attn_ref(hidden_states, w_qkv, w_out):
        import jax, jax.numpy as jnp
        import numpy as np
        B, S, E = (2, 1024, 1024)
        N_HEAD = 16
        HEAD_DIM = E // N_HEAD
        MP_NUM = 4
        ROTARY_DIM = 64

        def _rotate_every_two(x):
            x1 = x[..., 0::2]
            x2 = x[..., 1::2]
            return jnp.stack((-x2, x1), axis=-1).reshape(x.shape)
        b, s, e = hidden_states.shape
        local = e // MP_NUM
        qkv = jnp.einsum('bse,fe->bsf', hidden_states, w_qkv)
        qkv = qkv.reshape(b, s, MP_NUM, 3 * local)
        q = qkv[..., :local].reshape(b, s, N_HEAD, HEAD_DIM)
        v = qkv[..., local:2 * local].reshape(b, s, N_HEAD, HEAD_DIM)
        k = qkv[..., 2 * local:].reshape(b, s, N_HEAD, HEAD_DIM)
        inv_freq = 1.0 / 10000.0 ** (jnp.arange(0, ROTARY_DIM, 2, dtype=jnp.float32) / ROTARY_DIM)
        freqs = jnp.arange(s, dtype=jnp.float32)[:, None] * inv_freq[None, :]
        sin = jnp.repeat(jnp.sin(freqs), 2, axis=-1)[None, :, None, :]
        cos = jnp.repeat(jnp.cos(freqs), 2, axis=-1)[None, :, None, :]

        def rope(x):
            x_rot = x[..., :ROTARY_DIM]
            x_pass = x[..., ROTARY_DIM:]
            x_rot = x_rot * cos + _rotate_every_two(x_rot) * sin
            return jnp.concatenate([x_rot, x_pass], axis=-1)
        q = rope(q)
        k = rope(k)
        q = q.transpose(0, 2, 1, 3)
        k = k.transpose(0, 2, 1, 3)
        v = v.transpose(0, 2, 1, 3)
        scale = jnp.sqrt(jnp.asarray(HEAD_DIM, dtype=q.dtype))
        scores = jnp.einsum('bhqd,bhkd->bhqk', q, k) / scale
        causal = jnp.tril(jnp.ones((s, s), dtype=bool))
        scores = jnp.where(causal[None, None, :, :], scores, jnp.finfo(scores.dtype).min)
        attn = jax.nn.softmax(scores, axis=-1)
        out = jnp.einsum('bhqk,bhkd->bhqd', attn, v)
        out = out.transpose(0, 2, 1, 3).reshape(b, s, e)
        return jnp.einsum('bse,fe->bsf', out, w_out)

    def _L0_ffn_ref(x, Wg, Wu, Wd, Wr, temperature):
        import jax, jax.numpy as jnp
        import numpy as np
        GOLDEN_CENTER = 1.0 / np.e
        GOLDEN_LOWER = 0.5 - np.log(4.0 / 3.0)
        GOLDEN_UPPER = 0.5

        def _golden_weights(x, Wr, temperature):
            inh = jax.nn.sigmoid(x @ Wr / temperature)
            in_zone = (inh >= GOLDEN_LOWER) & (inh <= GOLDEN_UPPER)
            distance = jnp.abs(inh - GOLDEN_CENTER)
            weights = jnp.exp(-distance / 0.1) * in_zone.astype(x.dtype)
            wsum = jnp.sum(weights, axis=-1, keepdims=True)
            no_expert = wsum < 1e-08
            fb = jnp.exp(-distance / 0.3)
            _, top2 = jax.lax.top_k(fb, 2)
            fb_mask = jnp.sum(jax.nn.one_hot(top2, weights.shape[-1], dtype=x.dtype), axis=-2)
            fb_w = fb * fb_mask
            fb_w = fb_w / jnp.maximum(jnp.sum(fb_w, axis=-1, keepdims=True), 1e-08)
            weights = jnp.where(no_expert, fb_w, weights)
            weights = weights / jnp.maximum(jnp.sum(weights, axis=-1, keepdims=True), 1e-08)
            return weights
        weights = _golden_weights(x, Wr, temperature)
        gate = jnp.einsum('btd,edf->betf', x, Wg)
        up = jnp.einsum('btd,edf->betf', x, Wu)
        h = jax.nn.silu(gate) * up
        e_out = jnp.einsum('betf,efd->betd', h, Wd)
        out = jnp.einsum('bte,betd->btd', weights, e_out)
        return out
    x = x + _L0_xattn_ref(_layernorm(x, axis=-1), mask_BxSx4224_bf0, ctx_2048, ctx_2048, L0_xattn_wq, L0_xattn_wk, L0_xattn_wv, L0_xattn_wo)
    x = x + _L0_attn_ref(_layernorm(x, axis=-1), L0_attn_w_qkv, L0_attn_w_out)
    x = x + _L0_ffn_ref(_layernorm(x, axis=-1), L0_ffn_Wg, L0_ffn_Wu, L0_ffn_Wd, L0_ffn_Wr, L0_ffn_temperature)
    return x

_drawn_inputs = setup_inputs


def setup_inputs(seed=0):
    import zlib

    import numpy as np

    out = dict(_drawn_inputs(seed))
    spreads = {}
    factors = {'L0_xattn_wk': 2.896, 'L0_xattn_wv': 2.676}
    for name, (base, spread) in spreads.items():
        noise = np.random.default_rng([zlib.crc32(name.encode()), seed]).standard_normal(out[name].shape)
        drawn = base * np.exp(spread * noise) if base else spread * noise
        out[name] = jnp.asarray(drawn.astype(out[name].dtype))
    for name, factor in factors.items():
        out[name] = (out[name] * factor).astype(out[name].dtype)
    return out
```

```python
import concourse.bass as bass
from concourse import mybir
from contextlib import ExitStack

F32 = mybir.dt.float32
F32R = mybir.dt.float32r
ALU = mybir.AluOpType
ACT = mybir.ActivationFunctionType
AX = mybir.AxisListType

P = 128
B, QL, D, KV = 8, 64, 1024, 1601
C = D // P
TOK = B * QL
TT = TOK // P
H, DH = 16, 64
NE, F = 8, 1024
HALF = 512
UNIT = 2048
RING = 4
AHEAD = RING - 1
KFULL = 3 * HALF
KREM = KV - KFULL
KTAIL = KREM + 1
KEYS = KV + QL
NCH = 14
EPS = 1e-5

U_Q, U_K, U_V = 0, 4, 8
U_KEYS0 = 12
PER_BATCH = 14
U_WO = U_KEYS0 + B * PER_BATCH
U_QKV = U_WO + 4
U_WOUT = U_QKV + 12
U_FFN = U_WOUT + 4
PER_EXPERT = 12
O_LN1 = 0
O_QK = O_LN1 + 8
O_V = O_QK + 16
O_WO = O_V + 8
O_LN2 = O_WO + 8
O_QKV = O_LN2 + 8
O_WOUT = O_QKV + 24
O_LN3 = O_WOUT + 8
O_FFN = O_LN3 + 8
OUT_PER_EXPERT = 16

CONSTS = 3 * DH + P
SCALE = 1.0 / 32.0
HEAD_SCALE = 0.125
CENTER = 0.36787944117144233
LOWER = 0.21231792754821915
UPPER = 0.5


def released():
    silent, table = 0, []

    def unit(sem, value):
        nonlocal silent
        if sem is None:
            silent += 1
            sem, value = "unit_used", silent
        table.append((sem, value))

    def projection(base, groups):
        for g in range(groups):
            unit(None, 0)
            unit("out_ready", base + 4 * (g + 1))

    for k in range(8):
        unit("out_ready", O_QK + 2 * (k + 1))
    projection(O_V, 2)
    for s in range(B + 1):
        if s < B:
            for u in range(7):
                unit(*(("s_ready", 4 * s + (u + 1) // 2 + (u == 6)) if u % 2 or u == 6 else (None, 0)))
        if s > 0:
            for u in range(7):
                unit(*(("o_ready", s) if u == 6 else (None, 0)))
    projection(O_WO, 2)
    projection(O_QKV, 6)
    projection(O_WOUT, 2)
    for e in range(NE):
        for f in range(8):
            unit("out_ready", O_FFN + OUT_PER_EXPERT * e + f + 1)
        projection(O_FFN + OUT_PER_EXPERT * e + 8, 2)
    return table


class Steps:

    def __init__(self, engine, sem):
        self.engine, self.sem, self.n, self.k, self.i, self.per = engine, sem, 0, 0, 0, 0

    def done(self, ins):
        ins.then_inc(self.sem, 1)
        self.k += 1

    def wait(self):
        self.engine.wait_ge(self.sem, self.n + self.k + self.per * self.i)

    def loop(self, i, per):
        self.n, self.k, self.i, self.per = self.n + self.k, 0, i, per

    def end(self, turns):
        assert self.k == self.per, (self.k, self.per)
        self.n, self.k, self.i, self.per = self.n + self.per * turns, 0, 0, 0


def perceiver_block(nc, x_d, ctx_d, keys_d, tail_d, w_d, wr_d, temp_d, const_d, out_d):
    with ExitStack() as ctx:
        def sb(name, shape, dt=F32):
            return ctx.enter_context(nc.sbuf_tensor(name, shape, dt))

        def sem(name):
            return ctx.enter_context(nc.semaphore(name))

        new_k_d = nc.dram_tensor("new_keys_t", (P, C, TOK), F32).ap()
        x_mid_d = nc.dram_tensor("x_mid", (P, TT * D), F32).ap()
        new_v_d = nc.dram_tensor("new_values", (TOK, D), F32).ap()

        ps = ctx.enter_context(nc.psum_tensor("ps", [P, 8, HALF], F32))
        raw = sb("raw", [P, RING, UNIT])
        hi = sb("hi", [P, RING, UNIT], F32R)
        lo = sb("lo", [P, RING, UNIT], F32R)
        xq = sb("xq", [P, (B + 1) * C * QL])
        act_hi = sb("act_hi", [P, C, TOK], F32R)
        act_lo = sb("act_lo", [P, C, TOK], F32R)
        consts = sb("consts_sb", [P, CONSTS])
        wr_raw = sb("wr_raw", [P, C, NE])
        wr_hi = sb("wr_hi", [P, C, NE], F32R)
        wr_lo = sb("wr_lo", [P, C, NE], F32R)
        temp = sb("temp", [P, 1])
        eps = sb("eps", [P, 1])
        stats = sb("stats", [P, TT, 2, 6])
        mv = sb("mv", [P, TT, 2])
        std = sb("std", [P, TT])
        rstd = sb("rstd", [P, TT])
        small = sb("small", [P, 16, TT * NE])
        wts = sb("wts", [P, TT, NE])
        x = xq[:, 0:TT * D].rearrange("p (t d) -> p t d", t=TT)
        q = xq[:, :].rearrange("p (b c n) -> p b c n", b=B + 1, c=C)
        cos_t = consts[:, 0:DH]
        sin_t = consts[:, DH:2 * DH]
        mask_t = consts[:, 2 * DH:3 * DH]
        ident = consts[:, 3 * DH:]

        x_loaded = [sem(f"x_loaded{t}") for t in range(TT)]
        x_reloaded = sem("x_reloaded")
        x_mid_stored = sem("x_mid_stored")
        x_mid_loaded = sem("x_mid_loaded")
        consts_loaded = sem("consts_loaded")
        router_loaded = sem("router_loaded")
        temp_loaded = sem("temp_loaded")
        landed = [sem(f"landed{s}") for s in range(RING)]
        new_landed = sem("new_landed")
        hi_done = sem("hi_done")
        lo_done = sem("lo_done")
        unit_used = sem("unit_used")
        out_ready = sem("out_ready")
        evacuated = sem("evacuated")
        dve_step = sem("dve_step")
        eps_set = sem("eps_set")
        stats_ready = sem("stats_ready")
        std_ready = sem("std_ready")
        xn_ready = sem("xn_ready")
        ln_hi = sem("ln_hi")
        kv_stored = [sem(f"kv_stored{s}") for s in range(2)]
        q_hi_done = sem("q_hi_done")
        q_split = sem("q_split")
        s_ready = sem("s_ready")
        lorow_ready = sem("lorow_ready")
        s_evac = sem("s_evac")
        negmax_ready = sem("negmax_ready")
        p_ready = sem("p_ready")
        pt_ready = sem("pt_ready")
        pt_hi_done = sem("pt_hi_done")
        pt_split = sem("pt_split")
        o_ready = sem("o_ready")
        olo_ready = sem("olo_ready")
        o_evac = sem("o_evac")
        o_norm = sem("o_norm")
        ot_ready = sem("ot_ready")
        ot_hi_done = sem("ot_hi_done")
        ot_split = sem("ot_split")
        tq_ready = sem("tq_ready")
        tq_evac = sem("tq_evac")
        hs_ready = sem("hs_ready")
        hs_used = sem("hs_used")
        hs_shifted = sem("hs_shifted")
        hs_exp = sem("hs_exp")
        hp_ready = sem("hp_ready")
        hpt_ready = sem("hpt_ready")
        hpt_evac = sem("hpt_evac")
        ho_ready = sem("ho_ready")
        ho_hi = sem("ho_hi")
        ho_split = sem("ho_split")
        wr_hi_done = sem("wr_hi_done")
        wr_split = sem("wr_split")
        logits_ready = sem("logits_ready")
        logits_used = sem("logits_used")
        z_ready = sem("z_ready")
        ez_ready = sem("ez_ready")
        dist_ready = sem("dist_ready")
        edist_ready = sem("edist_ready")
        silu_done = sem("silu_done")
        out_stored = sem("out_stored")

        with ExitStack() as phase:
            def pb(name, shape, dt=F32):
                return phase.enter_context(nc.sbuf_tensor(name, shape, dt))

            qs = pb("qs", [P, 2, C, P], F32R)
            pt = pb("pt", [P, NCH, P], F32R)
            S = pb("scores", [P, 2, KEYS])
            lorow = pb("lorow", [QL, 2, HALF])
            olo = pb("olo", [QL, D])
            O = pb("attended", [QL, D])
            cols = pb("cols", [QL, 4, 2])
            mx, nb, sums, rinv = (cols[:, j, :] for j in range(4))
            kvs = pb("kvs", [P, 2, HALF])
            xn1 = S[:, :, 0:D]
        with ExitStack() as phase:
            qk = pb("qk", [P, TT, 2 * D])
            sc = pb("head_scores", [P, 2, D])
            qkt = pb("qkt", [P, 2 * C, P])
            pth = pb("pth", [P, H, QL])
            heads = pb("heads", [P, 3, H])
            hmx, hsum, hinv = (heads[:, j, :] for j in range(3))
            rope_a, rope_b = sc[:, 0, :].rearrange("p (s n) -> p s n", s=2), sc[:, 1, :].rearrange("p (s n) -> p s n", s=2)
            xn2 = sc[:, :, :]
        with ExitStack() as phase:
            h_hi = pb("h_hi", [P, C, TOK], F32R)
            h_lo = pb("h_lo", [P, C, TOK], F32R)
            work = pb("work", [P, 2, 2, TOK])
            silu, h32 = work[:, 0, :, :], work[:, 1, :, :]
            xn3 = work[:, :, :, :].rearrange("p a b n -> p a (b n)")
        xn_of = (xn1, xn2, xn3)
        v = x

        free = released()
        release = {"out_ready": out_ready, "unit_used": unit_used, "s_ready": s_ready, "o_ready": o_ready}
        assert len(free) == U_FFN + NE * PER_EXPERT

        block = ctx.enter_context(nc.Block())

        @block.sync
        def _(sp):
            def load(k, src, per=0, i=0, dst=None):
                if k >= RING:
                    sp.wait_ge(lo_done, k - RING + 1 + per * i)
                sp.dma_start(raw[:, k % RING, :] if dst is None else dst, src).then_inc(landed[k % RING], 16)

            def load_keys(k, b, per=0, i=0, first=False):
                for u in range(6):
                    load(k + u, keys_d[b, u], per, i)
                view = raw[:, (k + 6) % RING, 0:C * (KTAIL + QL)].rearrange("p (c n) -> p c n", c=C)
                load(k + 6, tail_d[b], per, i, view[:, :, 0:KTAIL])
                if first:
                    for s in range(2):
                        sp.wait_ge(kv_stored[s], 16 * 8)
                sp.dma_start(view[:, :, KTAIL:], new_k_d[:, :, bass.ds(b * QL, QL)]).then_inc(new_landed, 16)

            def load_values(k, b, per=0, i=0):
                for u in range(6):
                    load(k + u, ctx_d[b, 2 * P * u:2 * P * (u + 1), :].rearrange("(j p) d -> p j d", p=P), per, i,
                         raw[:, (k + u) % RING, :].rearrange("p (j d) -> p j d", j=2))
                load(k + 6, ctx_d[b, KFULL:KV, :], per, i, raw[0:KREM, (k + 6) % RING, 0:D])
                sp.dma_start(raw[0:QL, (k + 6) % RING, D:2 * D],
                             new_v_d[bass.ds(b * QL, QL), :]).then_inc(new_landed, 16)

            for t in range(TT):
                sp.dma_start(x[:, t, :], x_d[t * P:(t + 1) * P, :]).then_inc(x_loaded[t], 16)
                if t == 0:
                    sp.dma_start(consts[:, :], const_d).then_inc(consts_loaded, 16)
            for k in range(RING):
                load(k, w_d[k])
            sp.dma_start(wr_raw[:, :, :], wr_d).then_inc(router_loaded, 16)
            sp.dma_start(temp[:, :], temp_d).then_inc(temp_loaded, 16)
            with sp.Fori(0, 2) as i:
                for k in range(RING):
                    load(RING + k, w_d[4 * i + RING + k], RING, i)
            load_keys(U_KEYS0, 0, first=True)
            k0 = U_KEYS0 + 7
            load_keys(k0, 1)
            load_values(k0 + 7, 0)
            with sp.Fori(0, 3) as i:
                for s in range(2):
                    k = k0 + PER_BATCH * (1 + s)
                    load_keys(k, 2 * i + (s + 2), 2 * PER_BATCH, i)
                    load_values(k + 7, 2 * i + (s + 1), 2 * PER_BATCH, i)
            load_values(k0 + 7 * PER_BATCH, B - 1)
            with sp.Fori(0, (U_FFN + NE * PER_EXPERT - U_WO) // RING) as i:
                for k in range(RING):
                    load(U_WO + k, w_d[4 * i + (U_KEYS0 + k)], RING, i)
            for t in range(TT):
                sp.wait_ge(evacuated, O_FFN + NE * OUT_PER_EXPERT - TT + t + 1)
                sp.dma_start(out_d[t * P:(t + 1) * P, :], x[:, t, :]).then_inc(out_stored, 16)
            sp.wait_ge(out_stored, 16 * TT)

        @block.gpsimd
        def _(pool):
            for f in range(C):
                pool.wait_ge(evacuated, O_QK + C + f + 1)
                pool.dma_start(new_k_d[:, f, :], kvs[:, f % 2, :]).then_inc(kv_stored[f % 2], 16)
            for n in range(8):
                g, t = n // TT, n % TT
                pool.wait_ge(evacuated, O_V + n + 1)
                pool.dma_start(new_v_d[t * P:(t + 1) * P, g * HALF:(g + 1) * HALF],
                               kvs[:, n % 2, :]).then_inc(kv_stored[n % 2], 16)
            pool.wait_ge(q_split, B + 1)
            pool.dma_start(x[:, :, :], x_d.rearrange("(t p) d -> p t d", p=P)).then_inc(x_reloaded, 16)
            pool.wait_ge(xn_ready, 2 * TT)
            pool.dma_start(x_mid_d, xq[:, 0:TT * D]).then_inc(x_mid_stored, 16)
            pool.wait_ge(ho_ready, TT)
            pool.wait_ge(x_mid_stored, 16)
            pool.dma_start(xq[:, 0:TT * D], x_mid_d).then_inc(x_mid_loaded, 16)

        KEY_LAST, VALUE_LAST = "keys", "values"

        def part(buf, k, kind):
            if kind == KEY_LAST:
                return buf[:, k % RING, 0:C * (KTAIL + QL)]
            if kind == VALUE_LAST:
                return buf[0:KREM, k % RING, :]
            return buf[:, k % RING, :]

        def kind_of(pos):
            return {6: KEY_LAST, 13: VALUE_LAST}.get(pos % PER_BATCH)

        @block.scalar
        def _(act):
            def split(k, per=0, i=0, kind=None):
                act.wait_ge(landed[k % RING], 16 * (k // RING + 1) + 16 * (per // RING) * i)
                if kind:
                    b2 = (k - U_KEYS0 - 6) // 7
                    act.wait_ge(new_landed, 16 * (b2 + 1) + 16 * (per // 7) * i)
                if k >= RING:
                    name, value = free[k - RING + per]
                    grows = free[k - RING + 2 * per][1] - value
                    act.wait_ge(release[name], value - grows + grows * i if per else value)
                act.activation(part(hi, k, kind), part(raw, k, kind), ACT.Copy).then_inc(hi_done, 1)

            def norm(n, base):
                act.wait_ge(stats_ready, TT * (n + 1))
                act.activation(std[:, :], mv[:, :, 1], ACT.Sqrt, bias=eps[:, 0:1]).then_inc(std_ready, 1)
                for j in range(2 * TT):
                    t, h = j // 2, j % 2
                    act.wait_ge(out_ready, base + j + 1)
                    act.activation(act_hi[:, 4 * h:4 * h + 4, t * P:(t + 1) * P],
                                   ps[:, j, :].rearrange("p (c n) -> p c n", c=4), ACT.Copy).then_inc(ln_hi, 1)

            act.wait_ge(router_loaded, 16)
            act.activation(wr_hi[:, :, :], wr_raw[:, :, :], ACT.Copy).then_inc(wr_hi_done, 1)
            act.wait_ge(eps_set, 1)
            for k in range(AHEAD):
                split(k)
            norm(0, O_LN1)
            for k in range(U_Q, U_KEYS0):
                split(k + AHEAD)

            def q_hi(s, b, i=0):
                if s >= 2:
                    act.wait_ge(s_ready, 4 * (s - 1) + 8 * i)
                act.activation(qs[:, s % 2, :, 0:QL], q[:, b, :, :], ACT.Copy).then_inc(q_hi_done, 1)

            def score_rows(s, j, i=0):
                n = 4 * s + j
                w = HALF if j < 3 else KTAIL + QL
                act.wait_ge(s_ready, n + 1 + 8 * i)
                if n >= 2:
                    act.wait_ge(s_evac, n - 1 + 8 * i)
                act.activation(lorow[:, j % 2, 0:w], ps[QL:P, j, 0:w], ACT.Copy).then_inc(lorow_ready, 1)

            def exps(s, i=0):
                act.wait_ge(negmax_ready, s + 1 + 2 * i)
                act.activation(S[0:QL, s % 2, :], S[0:QL, s % 2, :], ACT.Exp, bias=nb[:, s % 2:s % 2 + 1], scale=SCALE,
                               accum_out=sums[:, s % 2:s % 2 + 1]).then_inc(p_ready, 1)

            def ot_hi(s, b, i=0):
                act.wait_ge(ot_ready, s + 1 + 2 * i)
                act.activation(act_hi[:, :, bass.ds(b * QL, QL)], ps[:, 6, :].rearrange("p (c n) -> p c n", c=C),
                               ACT.Copy).then_inc(ot_hi_done, 1)

            def step(s, i=0, loop=False, nxt=True):
                per = 2 * PER_BATCH if loop else 0
                k0 = U_KEYS0 + 7 + PER_BATCH * s
                for pos in range(0 if nxt else 7, PER_BATCH):
                    k = k0 + pos - (0 if nxt else 7)
                    split(k + AHEAD, per, i, kind_of(pos + AHEAD) if nxt or pos + AHEAD < PER_BATCH else None)
                    if pos == 1:
                        score_rows(s + 1, 0, i)
                        if s > 0:
                            ot_hi(s - 1, 2 * i + (s - 1), i)
                    if pos in (3, 5):
                        score_rows(s + 1, pos // 2, i)
                    if pos == 6:
                        score_rows(s + 1, 3, i)
                    if pos == (6 if nxt else 7):
                        if not nxt:
                            ot_hi(s - 1, s - 1)
                        for h, (a, e) in enumerate(((0, 8), (8, NCH))):
                            act.wait_ge(pt_ready, 2 * s + h + 1 + 4 * i)
                            act.activation(pt[:, a:e, 0:QL],
                                           ps[:, 4 + h, 0:(e - a) * QL].rearrange("p (k n) -> p k n", n=QL),
                                           ACT.Copy).then_inc(pt_hi_done, 1)
                        if nxt:
                            exps(s + 1, i)
                    if pos == 8 and nxt:
                        q_hi(s + 2, 2 * i + (s + 2), i)
                    if pos == 13:
                        act.wait_ge(o_ready, s + 1 + 2 * i)
                        act.activation(olo[:, :], ps[QL:P, 6:8, :].rearrange("p a n -> p (a n)"),
                                       ACT.Copy).then_inc(olo_ready, 1)

            act.wait_ge(evacuated, O_QK + C)
            q_hi(0, 0)
            q_hi(1, 1)
            for pos in range(7):
                split(U_KEYS0 + pos + AHEAD, kind=KEY_LAST if pos + AHEAD == 6 else None)
                if pos in (1, 3, 5, 6):
                    score_rows(0, (pos + 1) // 2 - (pos < 6) if pos < 6 else 3)
            exps(0)
            step(0)
            with act.Fori(0, 3) as i:
                step(1, i, True)
                step(2, i, True)
            step(7, nxt=False)
            ot_hi(7, 7)

            for k in range(U_WO, U_QKV):
                split(k + AHEAD)
            norm(1, O_LN2)
            with act.Fori(0, 3) as i:
                for k in range(RING):
                    split(U_QKV + k + AHEAD, RING, i)

            def heads_t(t):
                for w in range(2):
                    act.wait_ge(tq_ready, 2 * t + w + 1)
                    act.activation(qkt[:, C * w:C * (w + 1), :].rearrange("p c n -> p (c n)"),
                                   ps[:, 2 * w:2 * w + 2, :].rearrange("p a n -> p (a n)"),
                                   ACT.Copy).then_inc(tq_evac, 1)

            def heads_exp(t):
                act.wait_ge(hs_shifted, t + 1)
                act.activation(sc[:, t % 2, :], sc[:, t % 2, :], ACT.Exp).then_inc(hs_exp, 1)

            heads_t(0)
            heads_exp(0)
            for t in range(TT):
                if t + 1 < TT:
                    heads_t(t + 1)
                    heads_exp(t + 1)
                act.wait_ge(hpt_ready, t + 1)
                for b in range(2):
                    act.activation(pth[b * QL:(b + 1) * QL, :, :],
                                   ps[0:QL, 0:4, :].rearrange("p a (j n) -> p (a j) n", n=P)[:, :, b * QL:(b + 1) * QL],
                                   ACT.Copy).then_inc(hpt_evac, 1)
                act.wait_ge(ho_ready, t + 1)
                act.activation(act_hi[:, :, t * P:(t + 1) * P].rearrange("p c (b n) -> p b c n", b=2),
                               ps[:, 6:8, :].rearrange("p b (c n) -> p b c n", c=C), ACT.Copy).then_inc(ho_hi, 1)

            for k in range(U_WOUT, U_FFN):
                split(k + AHEAD)
            norm(2, O_LN3)

            act.wait_ge(z_ready, 1)
            act.activation(small[:, 1, :], small[:, 0, :], ACT.Exp, scale=-1.0).then_inc(ez_ready, 1)
            act.wait_ge(dist_ready, 1)
            act.activation(small[:, 5, :], small[:, 4, :], ACT.Exp, scale=-1.0 / 0.1).then_inc(edist_ready, 1)
            act.activation(small[:, 6, :], small[:, 4, :], ACT.Exp, scale=-1.0 / 0.3).then_inc(edist_ready, 1)

            def expert(e, per, last):
                for k in range(PER_EXPERT):
                    if not last or k + AHEAD < PER_EXPERT:
                        split(U_FFN + k + AHEAD + (0 if per else (NE - 1) * PER_EXPERT), per, e)
                    if k < 8:
                        act.wait_ge(out_ready, O_FFN + k + 1 + OUT_PER_EXPERT * e)
                        act.activation(silu[:, k % 2, :], ps[:, 4 + 2 * (k % 2), :], ACT.Silu).then_inc(silu_done, 1)

            with act.Fori(0, NE - 1) as e:
                expert(e, PER_EXPERT, False)
            expert(NE - 1, 0, True)

        @block.vector
        def _(dve):
            steps = Steps(dve, dve_step)

            def split(k, per=0, i=0, kind=None):
                dve.wait_ge(hi_done, k + 1 + per * i)
                dve.tensor_tensor(part(lo, k, kind), part(raw, k, kind), part(hi, k, kind),
                                  ALU.subtract).then_inc(lo_done, 1)

            def norm(n, base):
                for t in range(TT):
                    if n == 0:
                        dve.wait_ge(x_loaded[t], 16)
                    for h in range(2):
                        steps.done(dve.bn_stats(stats[:, t, h, :], x[:, t, h * HALF:(h + 1) * HALF]))
                steps.wait()
                for t in range(TT):
                    dve.bn_aggr(mv[:, t, :], stats[:, t, :, :].rearrange("p h n -> p (h n)")).then_inc(stats_ready, 1)
                dve.wait_ge(std_ready, n + 1)
                steps.done(dve.reciprocal(rstd[:, :], std[:, :]))
                steps.wait()
                for t in range(TT):
                    if t >= 2:
                        dve.wait_ge(out_ready, base + 2 * (t - 2) + 2)
                    dve.tensor_scalar(xn_of[n][:, t % 2, :], x[:, t, :], mv[:, t, 0:1], rstd[:, t:t + 1],
                                      ALU.subtract, ALU.mult).then_inc(xn_ready, 1)
                for j in range(2 * TT):
                    t, h = j // 2, j % 2
                    to = (slice(None), slice(4 * h, 4 * h + 4), slice(t * P, (t + 1) * P))
                    dve.wait_ge(ln_hi, 2 * TT * n + j + 1)
                    dve.tensor_tensor(act_lo[to], ps[:, j, :].rearrange("p (c n) -> p c n", c=4), act_hi[to],
                                      ALU.subtract).then_inc(evacuated, 1)

            dve.memset(eps[:, :], EPS).then_inc(eps_set, 1)
            dve.wait_ge(wr_hi_done, 1)
            dve.tensor_tensor(wr_lo[:, :, :], wr_raw[:, :, :], wr_hi[:, :, :], ALU.subtract).then_inc(wr_split, 1)
            norm(0, O_LN1)
            for k in range(AHEAD):
                split(k)
            dve.wait_ge(xn_ready, TT)
            dve.memset(q[:, B, :, :], 0.0)
            for k in range(U_Q, U_V):
                split(k + AHEAD)
                for j in range(2):
                    f = 2 * k + j
                    dve.wait_ge(out_ready, O_QK + f + 1)
                    if f < C:
                        dve.tensor_copy(q[:, 0:B, f, :], ps[:, f % 4, :].rearrange("p (b n) -> p b n", b=B))\
                           .then_inc(evacuated, 1)
                    else:
                        if f >= C + 2:
                            dve.wait_ge(kv_stored[f % 2], 16 * ((f - C) // 2))
                        dve.tensor_copy(kvs[:, f % 2, :], ps[:, f % 4, :]).then_inc(evacuated, 1)
            for k in range(U_V, U_KEYS0):
                split(k + AHEAD)
                g, half = (k - U_V) // 2, (k - U_V) % 2
                if half:
                    for t in range(TT):
                        n = g * TT + t
                        dve.wait_ge(out_ready, O_V + n + 1)
                        dve.wait_ge(kv_stored[n % 2], 16 * (4 + n // 2))
                        dve.tensor_copy(kvs[:, n % 2, :], ps[:, 4 * (1 - g) + t, :]).then_inc(evacuated, 1)

            def q_lo(s, b, i=0):
                dve.wait_ge(q_hi_done, s + 1 + 2 * i)
                dve.tensor_tensor(qs[:, s % 2, :, QL:P], q[:, b, :, :], qs[:, s % 2, :, 0:QL],
                                  ALU.subtract).then_inc(q_split, 1)

            def score_add(s, j, i=0):
                n = 4 * s + j
                w = HALF if j < 3 else KTAIL + QL
                at = j * HALF if j < 3 else KFULL - 1
                dve.wait_ge(lorow_ready, n + 1 + 8 * i)
                if j == 3:
                    dve.wait_ge(s_evac, n + 8 * i)
                dve.tensor_tensor(S[0:QL, s % 2, at:at + w], ps[0:QL, j, 0:w], lorow[:, j % 2, 0:w],
                                  ALU.add).then_inc(s_evac, 1)

            def row_max(s, i=0):
                dve.wait_ge(s_evac, 4 * s + 4 + 8 * i)
                steps.done(dve.tensor_reduce(mx[:, s % 2:s % 2 + 1], S[0:QL, s % 2, :], AX.X, ALU.max))
                steps.wait()
                dve.tensor_scalar(nb[:, s % 2:s % 2 + 1], mx[:, s % 2:s % 2 + 1], -SCALE, None,
                                  ALU.mult).then_inc(negmax_ready, 1)

            def ot_lo(s, b, i=0):
                dve.wait_ge(ot_hi_done, s + 1 + 2 * i)
                dve.tensor_tensor(act_lo[:, :, bass.ds(b * QL, QL)], ps[:, 6, :].rearrange("p (c n) -> p c n", c=C),
                                  act_hi[:, :, bass.ds(b * QL, QL)], ALU.subtract).then_inc(ot_split, 1)

            def step(s, i=0, loop=False, nxt=True):
                per = 2 * PER_BATCH if loop else 0
                k0 = U_KEYS0 + 7 + PER_BATCH * s
                for pos in range(0 if nxt else 7, PER_BATCH):
                    k = k0 + pos - (0 if nxt else 7)
                    split(k + AHEAD, per, i, kind_of(pos + AHEAD) if nxt or pos + AHEAD < PER_BATCH else None)
                    if pos == 1:
                        score_add(s + 1, 0, i)
                        if s > 0:
                            ot_lo(s - 1, 2 * i + (s - 1), i)
                    if pos in (3, 5):
                        score_add(s + 1, pos // 2, i)
                    if pos == 6:
                        score_add(s + 1, 3, i)
                    if pos == (6 if nxt else 7):
                        if not nxt:
                            ot_lo(s - 1, s - 1)
                        for h, (a, e) in enumerate(((0, 8), (8, NCH))):
                            dve.wait_ge(pt_hi_done, 2 * s + h + 1 + 4 * i)
                            dve.tensor_tensor(pt[:, a:e, QL:P],
                                              ps[:, 4 + h, 0:(e - a) * QL].rearrange("p (k n) -> p k n", n=QL),
                                              pt[:, a:e, 0:QL], ALU.subtract).then_inc(pt_split, 1)
                        if nxt:
                            row_max(s + 1, i)
                    if pos == 8 and nxt:
                        q_lo(s + 2, 2 * i + (s + 2), i)
                    if pos == 13:
                        dve.wait_ge(olo_ready, s + 1 + 2 * i)
                        dve.tensor_tensor(O[:, :], ps[0:QL, 6:8, :].rearrange("p a n -> p (a n)"), olo[:, :],
                                          ALU.add).then_inc(o_evac, 1)
                        steps.done(dve.reciprocal(rinv[:, s % 2:s % 2 + 1], sums[:, s % 2:s % 2 + 1]))
                        dve.wait_ge(o_evac, s + 1 + 2 * i)
                        steps.wait()
                        dve.tensor_scalar(O[:, :], O[:, :], rinv[:, s % 2:s % 2 + 1], None,
                                          ALU.mult).then_inc(o_norm, 1)

            q_lo(0, 0)
            q_lo(1, 1)
            for pos in range(7):
                split(U_KEYS0 + pos + AHEAD, kind=KEY_LAST if pos + AHEAD == 6 else None)
                if pos in (1, 3, 5):
                    score_add(0, pos // 2)
                if pos == 6:
                    score_add(0, 3)
            row_max(0)
            step(0)
            with dve.Fori(0, 3) as i:
                steps.loop(i, 4)
                step(1, i, True)
                step(2, i, True)
                steps.end(3)
            step(7, nxt=False)
            ot_lo(7, 7)

            def residual(u0, base):
                for k in range(4):
                    split(u0 + k + AHEAD)
                    if k % 2:
                        g = k // 2
                        for t in range(TT):
                            dve.wait_ge(out_ready, base + g * TT + t + 1)
                            to = x[:, t, g * HALF:(g + 1) * HALF]
                            dve.tensor_tensor(to, ps[:, 4 * (1 - g) + t, :], to, ALU.add).then_inc(evacuated, 1)
                dve.wait_ge(evacuated, base + 2 * TT)

            dve.wait_ge(x_reloaded, 16)
            residual(U_WO, O_WO)
            norm(1, O_LN2)

            dve.wait_ge(xn_ready, 2 * TT)
            cos8 = cos_t.unsqueeze(1).to_broadcast([P, 8, DH])
            sin4 = sin_t.rearrange("p (n w) -> p n w", w=2)

            def rope(g, t, i):
                n = 4 * g + t
                bank = 4 * (1 - g) + t
                dve.wait_ge(out_ready, O_QKV + n + 1 + 8 * i)
                dve.wait_ge(evacuated, O_QKV + n - 1 + 8 * i)
                a, b = rope_a[:, t % 2, :], rope_b[:, t % 2, :]
                steps.done(dve.tensor_tensor(a.rearrange("p (h d) -> p h d", d=DH),
                                             ps[:, bank, :].rearrange("p (h d) -> p h d", d=DH), cos8, ALU.mult))
                pw = ps[:, bank, :].rearrange("p (h n w) -> p h n w", n=DH // 2, w=2)
                bw = b.rearrange("p (h n w) -> p h n w", n=DH // 2, w=2)
                for w in range(2):
                    steps.done(dve.tensor_tensor(bw[:, :, :, w], pw[:, :, :, 1 - w],
                                                 sin4[:, :, w].unsqueeze(1).to_broadcast([P, 8, DH // 2]), ALU.mult))
                steps.wait()
                dve.tensor_tensor(qk[:, t, bass.ds(i * D + g * HALF, HALF)], a, b, ALU.add).then_inc(evacuated, 1)

            with dve.Fori(0, 2) as i:
                steps.loop(i, 24)
                for k in range(4):
                    split(U_QKV + k + AHEAD, RING, i)
                    if k % 2:
                        for t in range(TT):
                            rope(k // 2, t, i)
                steps.end(2)
            dve.wait_ge(x_mid_stored, 16)
            for k in range(4):
                split(U_QKV + 8 + k + AHEAD)
                if k % 2:
                    g = k // 2
                    for t in range(TT):
                        dve.wait_ge(out_ready, O_QKV + 16 + 4 * g + t + 1)
                        dve.tensor_copy(v[:, t, g * HALF:(g + 1) * HALF], ps[:, 4 * (1 - g) + t, :])\
                           .then_inc(evacuated, 1)

            def heads_scores(t):
                dve.wait_ge(hs_ready, t + 1)
                s3 = sc[:, t % 2, :].rearrange("p (h n) -> p h n", n=DH)
                dve.scalar_tensor_tensor(out=s3, in0=ps[:, 4:6, :].rearrange("p a (c n) -> p (a c) n", n=DH),
                                         scalar=HEAD_SCALE, in1=mask_t.unsqueeze(1).to_broadcast([P, H, DH]),
                                         op0=ALU.mult, op1=ALU.add).then_inc(hs_used, 1)
                dve.wait_ge(hs_used, t + 1)
                steps.done(dve.tensor_reduce(hmx, s3, AX.X, ALU.max))
                steps.wait()
                dve.tensor_tensor(s3, s3, hmx.unsqueeze(2).to_broadcast([P, H, DH]),
                                  ALU.subtract).then_inc(hs_shifted, 1)

            def heads_norm(t):
                s3 = sc[:, t % 2, :].rearrange("p (h n) -> p h n", n=DH)
                dve.wait_ge(hs_exp, t + 1)
                steps.done(dve.tensor_reduce(hsum, s3, AX.X, ALU.add))
                steps.wait()
                steps.done(dve.reciprocal(hinv, hsum))
                steps.wait()
                dve.tensor_tensor(s3, s3, hinv.unsqueeze(2).to_broadcast([P, H, DH]),
                                  ALU.mult).then_inc(hp_ready, 1)

            def heads_out(t):
                dve.wait_ge(ho_hi, t + 1)
                to = [a[:, :, t * P:(t + 1) * P].rearrange("p c (b n) -> p b c n", b=2) for a in (act_lo, act_hi)]
                dve.tensor_tensor(to[0], ps[:, 6:8, :].rearrange("p b (c n) -> p b c n", c=C), to[1],
                                  ALU.subtract).then_inc(ho_split, 1)

            heads_scores(0)
            heads_norm(0)
            for t in range(TT):
                if t + 1 < TT:
                    heads_scores(t + 1)
                    heads_norm(t + 1)
                heads_out(t)
            dve.wait_ge(x_mid_loaded, 16)
            residual(U_WOUT, O_WOUT)
            norm(2, O_LN3)

            def sm(j):
                return small[:, j, :]

            def sm3(j):
                return small[:, j, :].rearrange("p (t e) -> p t e", e=NE)

            def dep(ins):
                steps.done(ins)
                steps.wait()

            dve.wait_ge(temp_loaded, 16)
            dep(dve.reciprocal(temp[:, :], temp[:, :]))
            dve.wait_ge(logits_ready, 1)
            dve.tensor_scalar(sm(0), ps[:, 0, 0:TT * NE], temp[:, 0:1], None, ALU.mult).then_inc(z_ready, 1)
            dve.wait_ge(ez_ready, 1)
            dep(dve.tensor_scalar(sm(2), sm(1), 1.0, None, ALU.add))
            dep(dve.reciprocal(sm(3), sm(2)))
            dep(dve.tensor_scalar(sm(7), sm(3), LOWER, None, ALU.is_ge))
            dep(dve.scalar_tensor_tensor(out=sm(7), in0=sm(3), scalar=UPPER, in1=sm(7),
                                         op0=ALU.is_le, op1=ALU.mult))
            dep(dve.tensor_scalar(sm(8), sm(3), -1.0, CENTER, ALU.mult, ALU.add))
            dep(dve.tensor_scalar(sm(9), sm(3), CENTER, None, ALU.subtract))
            dve.tensor_tensor(sm(4), sm(8), sm(9), ALU.max).then_inc(dist_ready, 1)
            dve.wait_ge(edist_ready, 2)
            dep(dve.tensor_tensor(sm(5), sm(5), sm(7), ALU.mult))
            dep(dve.tensor_reduce(small[:, 10, 0:TT], sm3(5), AX.X, ALU.add))
            dep(dve.tensor_scalar(small[:, 10, TT:2 * TT], small[:, 10, 0:TT], 1e-8, None, ALU.is_lt))
            dep(dve.memset(sm(11), 0.0))
            for j in range(NE):
                each = sm3(6)[:, :, j:j + 1]
                steps.done(dve.tensor_tensor(sm3(12)[:, :, 0:j + 1], each.to_broadcast([P, TT, j + 1]),
                                             sm3(6)[:, :, 0:j + 1], ALU.is_gt))
                if j + 1 < NE:
                    steps.done(dve.tensor_tensor(sm3(12)[:, :, j + 1:NE], each.to_broadcast([P, TT, NE - 1 - j]),
                                                 sm3(6)[:, :, j + 1:NE], ALU.is_ge))
                steps.wait()
                dep(dve.tensor_tensor(sm(11), sm(11), sm(12), ALU.add))
            dep(dve.scalar_tensor_tensor(out=sm(13), in0=sm(11), scalar=2.0, in1=sm(6),
                                         op0=ALU.is_lt, op1=ALU.mult))

            def normalised(j, at):
                dep(dve.tensor_reduce(small[:, 14, at:at + TT], sm3(j), AX.X, ALU.add))
                dep(dve.tensor_scalar(small[:, 14, at:at + TT], small[:, 14, at:at + TT], 1e-8, None, ALU.max))
                dep(dve.reciprocal(small[:, 14, at + TT:at + 2 * TT], small[:, 14, at:at + TT]))
                dep(dve.tensor_tensor(sm3(j), sm3(j),
                                      small[:, 14, at + TT:at + 2 * TT].unsqueeze(2).to_broadcast([P, TT, NE]),
                                      ALU.mult))

            normalised(13, 0)
            flag = small[:, 10, TT:2 * TT].unsqueeze(2).to_broadcast([P, TT, NE])
            dep(dve.tensor_tensor(sm3(13), sm3(13), flag, ALU.mult))
            dep(dve.tensor_scalar(small[:, 10, 2 * TT:3 * TT], small[:, 10, TT:2 * TT], -1.0, 1.0, ALU.mult, ALU.add))
            dep(dve.tensor_tensor(sm3(5), sm3(5), small[:, 10, 2 * TT:3 * TT].unsqueeze(2).to_broadcast([P, TT, NE]),
                                  ALU.mult))
            dep(dve.tensor_tensor(sm(5), sm(5), sm(13), ALU.add))
            normalised(5, 2 * TT)
            dve.tensor_copy(wts[:, :, :], sm3(5)).then_inc(logits_used, 1)
            dve.wait_ge(logits_used, 1)

            def expert(e, per, last, scalar_of):
                for k in range(PER_EXPERT):
                    if not last or k + AHEAD < PER_EXPERT:
                        split(U_FFN + k + AHEAD + (0 if per else (NE - 1) * PER_EXPERT), per, e)
                    if k < 8:
                        dve.wait_ge(silu_done, 8 * e + k + 1)
                        steps.done(dve.tensor_tensor(h32[:, k % 2, :], ps[:, 5 + 2 * (k % 2), :],
                                                     silu[:, k % 2, :], ALU.mult))
                        steps.wait()
                        steps.done(dve.tensor_copy(h_hi[:, k, :], h32[:, k % 2, :]))
                        steps.wait()
                        dve.tensor_tensor(h_lo[:, k, :], h32[:, k % 2, :], h_hi[:, k, :],
                                          ALU.subtract).then_inc(evacuated, 1)
                    elif k % 2:
                        g = (k - 8) // 2
                        for t in range(TT):
                            dve.wait_ge(out_ready, O_FFN + 8 + 4 * g + t + 1 + OUT_PER_EXPERT * e)
                            to = x[:, t, g * HALF:(g + 1) * HALF]
                            dve.scalar_tensor_tensor(out=to, in0=ps[:, 4 * g + t, :], scalar=scalar_of(t), in1=to,
                                                     op0=ALU.mult, op1=ALU.add).then_inc(evacuated, 1)

            with dve.Fori(0, NE - 1) as e:
                steps.loop(e, 16)
                expert(e, PER_EXPERT, False, lambda t: wts[:, t, bass.ds(e, 1)])
                steps.end(NE - 1)
            expert(NE - 1, 0, True, lambda t: wts[:, t, NE - 1:NE])

        @block.tensor
        def _(pe):
            def unit_ready(k, per=0, i=0):
                pe.wait_ge(lo_done, k + 1 + per * i)

            def three(out, a_hi, a_lo, b_hi, b_lo, first, last):
                pe.matmul(out, a_hi, b_hi, start=first, stop=False)
                pe.matmul(out, a_hi, b_lo, start=False, stop=False)
                return pe.matmul(out, a_lo, b_hi, start=False, stop=last)

            def norm(n, base):
                if n == 0:
                    pe.wait_ge(consts_loaded, 16)
                for t in range(TT):
                    pe.wait_ge(xn_ready, TT * n + t + 1)
                    for h in range(2):
                        for c in range(4):
                            ins = pe.transpose(ps[:, 2 * t + h, c * P:(c + 1) * P],
                                               xn_of[n][:, t % 2, (4 * h + c) * P:(4 * h + c + 1) * P],
                                               ident)
                        ins.then_inc(out_ready, 1)
                pe.wait_ge(evacuated, base + 2 * TT)

            def stationary_unit(k, out, wait, per=0, i=0, used=True):
                unit_ready(k, per, i)
                for j in range(2):
                    wait(j)
                    for c in range(C):
                        at = slice(j * D + c * P, j * D + (c + 1) * P)
                        ins = three(ps[:, out(j), :], hi[:, k % RING, at], lo[:, k % RING, at],
                                    act_hi[:, c, :], act_lo[:, c, :], c == 0, c == C - 1)
                    yield ins

            def projection(u0, base, groups=2, per=0, i=0, out_per=0):
                for g in range(groups):
                    bank = 4 * (1 - g % 2)
                    for half in range(2):
                        k = u0 + 2 * g + half

                        def bank_free(t):
                            pe.wait_ge(evacuated, base + 4 * g + t - 7 + out_per * i)

                        ins = None
                        unit_ready(k, per, i)
                        for t in range(TT):
                            if half == 0:
                                bank_free(t)
                            for c in range(4):
                                cc = 4 * half + c
                                rows = slice(t * P, (t + 1) * P)
                                cols = slice(c * HALF, (c + 1) * HALF)
                                ins = three(ps[:, bank + t, :], act_hi[:, cc, rows], act_lo[:, cc, rows],
                                            hi[:, k % RING, cols], lo[:, k % RING, cols], cc == 0, cc == C - 1)
                            if half == 1:
                                ins.then_inc(out_ready, 1)
                        if half == 0:
                            ins.then_inc(unit_used, 1)

            norm(0, O_LN1)
            with pe.Fori(0, 2) as i:
                for k in range(RING):
                    def bank_free(j):
                        pe.wait_ge(evacuated, O_QK + 2 * k + j - 3 + 8 * i)
                    for j, ins in enumerate(stationary_unit(k, lambda j: (2 * k + j) % 4, bank_free, RING, i)):
                        ins.then_inc(out_ready, 1)
            projection(U_V, O_V)

            def score_block(s, u, i=0, per=0):
                k = U_KEYS0 + u if s == 0 else U_KEYS0 + 7 + PER_BATCH * (s - 1) + u
                j = u // 2
                if u == 0:
                    pe.wait_ge(q_split, s + 1 + 2 * i)
                if u % 2 == 0:
                    if s == 0:
                        pe.wait_ge(evacuated, O_V + 4 + j + 1)
                    else:
                        pe.wait_ge(s_evac, 4 * (s - 1) + j + 1 + 8 * i)
                unit_ready(k, per, i)
                n = 4 if u < 6 else C
                w = HALF if u < 6 else KTAIL + QL
                for c in range(n):
                    cc = 4 * (u % 2) + c
                    for b, buf in enumerate((hi, lo)):
                        ins = pe.matmul(ps[:, j, 0:w], qs[:, s % 2, cc, :], buf[:, k % RING, c * w:(c + 1) * w],
                                        start=(cc == 0 and b == 0), stop=(cc == C - 1 and b == 1))
                if u % 2 or u == 6:
                    ins.then_inc(s_ready, 1)
                else:
                    ins.then_inc(unit_used, 1)

            def turned(out, rows, after_wait):
                if after_wait:
                    return pe.matmul(out, rows, ident[0:QL, 0:QL], start=True, stop=True)
                return pe.transpose(out, rows, ident[0:QL, 0:QL])

            def turn_o(s, i=0):
                pe.wait_ge(o_norm, s + 1 + 2 * i)
                for c in range(C):
                    ins = turned(ps[:, 6, c * QL:(c + 1) * QL], O[:, c * P:(c + 1) * P], c == 0)
                ins.then_inc(ot_ready, 1)

            def step(s, i=0, loop=False, nxt=True):
                per = 2 * PER_BATCH if loop else 0
                k0 = U_KEYS0 + 7 + PER_BATCH * s
                if nxt:
                    score_block(s + 1, 0, i, per)
                    score_block(s + 1, 1, i, per)
                if s > 0:
                    turn_o(s - 1, i)
                if nxt:
                    for u in range(2, 7):
                        score_block(s + 1, u, i, per)
                pe.wait_ge(p_ready, s + 1 + 2 * i)
                for kc in range(NCH):
                    a = kc * P if kc < 13 else KV
                    n = P if kc < 12 else (KREM if kc == 12 else QL)
                    ins = turned(ps[0:n, 4 + kc // 8, (kc % 8) * QL:(kc % 8 + 1) * QL],
                                 S[0:QL, s % 2, a:a + n], kc == 0)
                    if kc in (7, NCH - 1):
                        ins.then_inc(pt_ready, 1)
                for u in range(7):
                    k = k0 + u + (7 if nxt else 0)
                    if u == 0:
                        pe.wait_ge(pt_split, 2 * s + 1 + 4 * i)
                        if s > 0:
                            pe.wait_ge(o_evac, s + 2 * i)
                            pe.wait_ge(ot_split, s + 2 * i)
                    if u == 4:
                        pe.wait_ge(pt_split, 2 * s + 2 + 4 * i)
                    unit_ready(k, per, i)
                    for j in range(2):
                        kc = 2 * u + j
                        n = P if kc < 12 else (KREM if kc == 12 else QL)
                        for h in range(2):
                            at = slice(j * D + h * HALF, j * D + (h + 1) * HALF)
                            for b, buf in enumerate((hi, lo)):
                                ins = pe.matmul(ps[:, 6 + h, :], pt[0:n, kc, :], buf[0:n, k % RING, at],
                                                start=(kc == 0 and b == 0), stop=(kc == NCH - 1 and b == 1))
                    if u == 6:
                        ins.then_inc(o_ready, 1)
                    else:
                        ins.then_inc(unit_used, 1)

            for u in range(7):
                score_block(0, u)
            step(0)
            with pe.Fori(0, 3) as i:
                step(1, i, True)
                step(2, i, True)
            step(7, nxt=False)
            turn_o(7)
            pe.wait_ge(ot_split, B)

            projection(U_WO, O_WO)
            norm(1, O_LN2)
            with pe.Fori(0, 3) as i:
                projection(U_QKV, O_QKV, 2, RING, i, 8)

            pe.wait_ge(evacuated, O_QKV + 24)

            def heads_front(t):
                for w in range(2):
                    for c in range(C):
                        ins = pe.transpose(ps[:, 2 * w + c // 4, (c % 4) * P:(c % 4 + 1) * P],
                                           qk[:, t, w * D + c * P:w * D + (c + 1) * P], ident)
                    ins.then_inc(tq_ready, 1)
                pe.wait_ge(tq_evac, 2 * t + 2)
                if t >= 1:
                    pe.wait_ge(hs_used, t)
                for r in range(2):
                    for c in range(C):
                        for b in range(2):
                            ins = pe.matmul(ps[b * QL:(b + 1) * QL, 4 + r, c * DH:(c + 1) * DH],
                                            qkt[r * DH:(r + 1) * DH, c, b * QL:(b + 1) * QL],
                                            qkt[r * DH:(r + 1) * DH, C + c, b * QL:(b + 1) * QL],
                                            start=True, stop=True)
                ins.then_inc(hs_ready, 1)

            def heads_back(t):
                pe.wait_ge(hp_ready, t + 1)
                for j in range(H):
                    ins = pe.transpose(ps[0:DH, j // 4, (j % 4) * P:(j % 4 + 1) * P],
                                       sc[:, t % 2, j * DH:(j + 1) * DH], ident)
                ins.then_inc(hpt_ready, 1)
                pe.wait_ge(hpt_evac, 2 * (t + 1))
                if t >= 1:
                    pe.wait_ge(ho_split, t)
                for c in range(C):
                    for b in range(2):
                        for r in range(2):
                            h = 2 * c + r
                            ins = pe.matmul(ps[r * DH:(r + 1) * DH, 6 + b, c * QL:(c + 1) * QL],
                                            v[b * QL:(b + 1) * QL, t, h * DH:(h + 1) * DH],
                                            pth[b * QL:(b + 1) * QL, r * C + c, :], start=True, stop=True)
                ins.then_inc(ho_ready, 1)

            heads_front(0)
            for t in range(TT):
                if t + 1 < TT:
                    heads_front(t + 1)
                heads_back(t)
            pe.wait_ge(ho_split, TT)
            projection(U_WOUT, O_WOUT)
            norm(2, O_LN3)

            pe.wait_ge(wr_split, 1)
            for t in range(TT):
                for c in range(C):
                    ins = three(ps[:, 0, t * NE:(t + 1) * NE], act_hi[:, c, t * P:(t + 1) * P],
                                act_lo[:, c, t * P:(t + 1) * P], wr_hi[:, c, :], wr_lo[:, c, :], c == 0, c == C - 1)
            ins.then_inc(logits_ready, 1)

            def expert(e, per):
                u0 = U_FFN + (0 if per else (NE - 1) * PER_EXPERT)
                for f in range(8):
                    def bank_free(j):
                        if j == 0:
                            pe.wait_ge(evacuated, O_FFN + (f - 2 if f == 0 else f - 1) + OUT_PER_EXPERT * e)
                    for j, ins in enumerate(stationary_unit(u0 + f, lambda j: 4 + 2 * (f % 2) + j, bank_free, per, e)):
                        pass
                    ins.then_inc(out_ready, 1)
                for g in range(2):
                    for half in range(2):
                        k = u0 + 8 + 2 * g + half
                        if g == 0:
                            pe.wait_ge(evacuated, O_FFN + 4 * (half + 1) + OUT_PER_EXPERT * e)
                        if g == 0 and half == 0:
                            pe.wait_ge(logits_used, 1)
                        unit_ready(k, per, e)
                        for t in range(TT):
                            for c in range(4):
                                cc = 4 * half + c
                                rows = slice(t * P, (t + 1) * P)
                                cols = slice(c * HALF, (c + 1) * HALF)
                                ins = three(ps[:, 4 * g + t, :], h_hi[:, cc, rows], h_lo[:, cc, rows],
                                            hi[:, k % RING, cols], lo[:, k % RING, cols], cc == 0, cc == C - 1)
                            if half == 1:
                                ins.then_inc(out_ready, 1)
                        if half == 0:
                            ins.then_inc(unit_used, 1)

            with pe.Fori(0, NE - 1) as e:
                expert(e, PER_EXPERT)
            expert(NE - 1, 0)


def kernel(**inputs):
    import numpy as np
    import concourse.bacc as _bacc
    from concourse.bass_utils import run_bass_kernel_spmd as _run

    g = {k: np.asarray(v) for k, v in inputs.items()}

    def stationary(w):
        return w.reshape(C, P, -1, P).transpose(2, 1, 0, 3).reshape(-1, P, D)

    def pairs(a, b):
        return np.stack([a, b], axis=2).reshape(-1, P, UNIT)

    def moving(w):
        return w.reshape(2, 4, P, -1, HALF).transpose(3, 0, 2, 1, 4).reshape(-1, P, UNIT)

    wq, wk = stationary(g["L0_xattn_wq"].T), stationary(g["L0_xattn_wk"].T)
    qkv = g["L0_attn_w_qkv"].reshape(4, 3, D // 4, D)
    units = [pairs(wq[0::2], wq[1::2]), pairs(wk[0::2], wk[1::2]), moving(g["L0_xattn_wv"].T),
             moving(g["L0_xattn_wo"].T)]
    units += [moving(qkv[:, n].reshape(D, D).T) for n in (0, 2, 1)]
    units.append(moving(g["L0_attn_w_out"].T))
    for e in range(NE):
        units.append(pairs(stationary(g["L0_ffn_Wg"][e]), stationary(g["L0_ffn_Wu"][e])))
        units.append(moving(g["L0_ffn_Wd"][e]))
    weights = np.concatenate(units)
    context = g["ctx_2048"]
    keys = context[:, :KFULL].reshape(B, 3, HALF, 2, 4, P).transpose(0, 1, 3, 5, 4, 2).reshape(B, 6, P, UNIT)
    tail = context[:, KFULL - 1:].reshape(B, KTAIL, C, P).transpose(0, 3, 2, 1)

    pos = np.arange(P, dtype=np.float32) % QL
    inv = (1.0 / 10000.0 ** (np.arange(0, DH, 2, dtype=np.float32) / DH)).astype(np.float32)
    ang = pos[:, None] * inv[None, :]
    consts = np.zeros((P, CONSTS), np.float32)
    consts[:, 0:DH] = np.repeat(np.cos(ang), 2, axis=1)
    consts[:, DH:2 * DH:2] = -np.sin(ang)
    consts[:, DH + 1:2 * DH:2] = np.sin(ang)
    consts[:, 2 * DH:3 * DH] = np.where(np.arange(QL)[None, :] > pos[:, None], -3.0e38, 0.0)
    consts[:, 3 * DH:] = np.eye(P)

    arrays = {
        "x_in": g["x"].reshape(TOK, D),
        "context": context,
        "keys": keys,
        "key_tail": tail,
        "weights": weights,
        "router": g["L0_ffn_Wr"].reshape(C, P, NE).transpose(1, 0, 2),
        "temperature": np.broadcast_to(g["L0_ffn_temperature"].reshape(1, 1), (P, 1)),
        "consts": consts,
    }
    arrays = {k: np.ascontiguousarray(v) for k, v in arrays.items()}
    nc = _bacc.Bacc("TRN2", target_bir_lowering=False, num_devices=1)
    args = [nc.dram_tensor(k, v.shape, F32, kind="ExternalInput").ap() for k, v in arrays.items()]
    out = nc.dram_tensor("out", (TOK, D), F32, kind="ExternalOutput").ap()
    perceiver_block(nc, *args, out)
    r = _run(nc, [arrays], core_ids=[0])
    return r.results[0]["out"].reshape(B, QL, D)
```

```python
import concourse.bass as bass
from concourse import mybir
from contextlib import ExitStack

F32 = mybir.dt.float32
F32R = mybir.dt.float32r
ALU = mybir.AluOpType
ACT = mybir.ActivationFunctionType
AX = mybir.AxisListType

P = 128
B, QL, D, KV = 8, 64, 1024, 1601
C = D // P
TOK = B * QL
TT = TOK // P
H, DH = 16, 64
NE, F = 8, 1024
HALF = 512
UNIT = 2048
RING = 4
AHEAD = RING - 1
KFULL = 3 * HALF
KREM = KV - KFULL
KTAIL = KREM + 1
KEYS = KV + QL
NCH = 14
EPS = 1e-5

U_Q, U_K, U_V = 0, 4, 8
U_KEYS0 = 12
PER_BATCH = 14
U_WO = U_KEYS0 + B * PER_BATCH
U_QKV = U_WO + 4
U_WOUT = U_QKV + 12
U_FFN = U_WOUT + 4
PER_EXPERT = 12
W_FFN = U_FFN - B * PER_BATCH
O_LN1 = 0
O_QK = O_LN1 + 8
O_V = O_QK + 16
O_WO = O_V + 8
O_LN2 = O_WO + 8
O_QKV = O_LN2 + 8
O_WOUT = O_QKV + 24
O_LN3 = O_WOUT + 8
O_FFN = O_LN3 + 8

CAP = 256
NT = CAP // P
ITEMS = 2 * NE
assert 2 * CAP >= TOK and NT * P == CAP

ROPE = 3 * DH
ROUTE = CAP + NE
SCALE = 1.0 / 32.0
HEAD_SCALE = 0.125
CENTER = 0.36787944117144233
LOWER = 0.21231792754821915
UPPER = 0.5


def released():
    silent, table = 0, []

    def unit(sem, value):
        nonlocal silent
        if sem is None:
            silent += 1
            sem, value = "unit_used", silent
        table.append((sem, value))

    def projection(base, groups):
        for g in range(groups):
            unit(None, 0)
            unit("out_ready", base + 4 * (g + 1))

    for k in range(8):
        unit("out_ready", O_QK + 2 * (k + 1))
    projection(O_V, 2)
    for s in range(B + 1):
        if s < B:
            for u in range(7):
                unit(*(("s_ready", 4 * s + (u + 1) // 2 + (u == 6)) if u % 2 or u == 6 else (None, 0)))
        if s > 0:
            for u in range(7):
                unit(*(("o_ready", s) if u == 6 else (None, 0)))
    projection(O_WO, 2)
    projection(O_QKV, 6)
    projection(O_WOUT, 2)
    for e in range(NE):
        for f in range(8):
            unit("gu_ready", 8 * e + f + 1)
        for g in range(2):
            unit(None, 0)
            unit("y_ready", 4 * e + 2 * (g + 1))
    return table


class Steps:

    def __init__(self, engine, sem):
        self.engine, self.sem, self.n, self.k, self.i, self.per = engine, sem, 0, 0, 0, 0

    def done(self, ins):
        ins.then_inc(self.sem, 1)
        self.k += 1

    def wait(self):
        self.engine.wait_ge(self.sem, self.n + self.k + self.per * self.i)

    def loop(self, i, per):
        self.n, self.k, self.i, self.per = self.n + self.k, 0, i, per

    def end(self, turns):
        assert self.k == self.per, (self.k, self.per)
        self.n, self.k, self.i, self.per = self.n + self.per * turns, 0, 0, 0


def perceiver_block(nc, x_d, ctx_d, keys_d, tail_d, w_d, wr_d, temp_d, ident_d, rope_d, route_d, count_d, out_d):
    with ExitStack() as ctx:
        def sb(name, shape, dt=F32):
            return ctx.enter_context(nc.sbuf_tensor(name, shape, dt))

        def sem(name):
            return ctx.enter_context(nc.semaphore(name))

        new_k_d = nc.dram_tensor("new_keys_t", (P, C, TOK), F32).ap()
        x_mid_d = nc.dram_tensor("x_mid", (P, TT * D), F32).ap()
        new_v_d = nc.dram_tensor("new_values", (TOK, D), F32).ap()

        ps = ctx.enter_context(nc.psum_tensor("ps", [P, 8, HALF], F32))
        raw = sb("raw", [P, RING, UNIT])
        hi = sb("hi", [P, RING, UNIT], F32R)
        lo = sb("lo", [P, RING, UNIT], F32R)
        xq = sb("xq", [P, (B + 1) * C * QL])
        act_hi = sb("act_hi", [P, C, TOK], F32R)
        act_lo = sb("act_lo", [P, C, TOK], F32R)
        ident = sb("ident", [P, P])
        ident_r = sb("ident_r", [P, P], F32R)
        ident = ident[:, :]
        wr_hi = sb("wr_hi", [P, C, NE], F32R)
        wr_lo = sb("wr_lo", [P, C, NE], F32R)
        eps = sb("eps", [P, 1])
        stats = sb("stats", [P, TT, 2, 6])
        mv = sb("mv", [P, TT, 2])
        std = sb("std", [P, TT])
        rstd = sb("rstd", [P, TT])
        small = sb("small", [P, 15, TT * NE])
        item_w = sb("item_w", [P, TT, ITEMS])
        item_slot = sb("item_slot", [P, TT, ITEMS])
        meta = sb("meta", [P, 1 + NE], mybir.dt.int32)
        x = xq[:, 0:TT * D].rearrange("p (t d) -> p t d", t=TT)
        q = xq[:, :].rearrange("p (b c n) -> p b c n", b=B + 1, c=C)

        x_loaded = [sem(f"x_loaded{t}") for t in range(TT)]
        x_reloaded = sem("x_reloaded")
        x_mid_stored = sem("x_mid_stored")
        x_mid_loaded = sem("x_mid_loaded")
        consts_loaded = sem("consts_loaded")
        router_loaded = sem("router_loaded")
        temp_loaded = sem("temp_loaded")
        landed = [sem(f"landed{s}") for s in range(RING)]
        new_landed = sem("new_landed")
        hi_done = sem("hi_done")
        lo_done = sem("lo_done")
        unit_used = sem("unit_used")
        out_ready = sem("out_ready")
        evacuated = sem("evacuated")
        dve_step = sem("dve_step")
        eps_set = sem("eps_set")
        stats_ready = sem("stats_ready")
        std_ready = sem("std_ready")
        xn_ready = sem("xn_ready")
        ln_hi = sem("ln_hi")
        kv_stored = [sem(f"kv_stored{s}") for s in range(2)]
        q_hi_done = sem("q_hi_done")
        q_split = sem("q_split")
        s_ready = sem("s_ready")
        lorow_ready = sem("lorow_ready")
        s_evac = sem("s_evac")
        negmax_ready = sem("negmax_ready")
        p_ready = sem("p_ready")
        pt_ready = sem("pt_ready")
        pt_hi_done = sem("pt_hi_done")
        pt_split = sem("pt_split")
        o_ready = sem("o_ready")
        olo_ready = sem("olo_ready")
        o_evac = sem("o_evac")
        o_norm = sem("o_norm")
        ot_ready = sem("ot_ready")
        ot_hi_done = sem("ot_hi_done")
        ot_split = sem("ot_split")
        tq_ready = sem("tq_ready")
        tq_evac = sem("tq_evac")
        hs_ready = sem("hs_ready")
        hs_used = sem("hs_used")
        hs_shifted = sem("hs_shifted")
        hs_exp = sem("hs_exp")
        hp_ready = sem("hp_ready")
        hpt_ready = sem("hpt_ready")
        hpt_evac = sem("hpt_evac")
        ho_ready = sem("ho_ready")
        ho_hi = sem("ho_hi")
        ho_split = sem("ho_split")
        wr_hi_done = sem("wr_hi_done")
        wr_split = sem("wr_split")
        logits_ready = sem("logits_ready")
        logits_used = sem("logits_used")
        z_ready = sem("z_ready")
        ez_ready = sem("ez_ready")
        dist_ready = sem("dist_ready")
        edist_ready = sem("edist_ready")
        silu_done = sem("silu_done")
        ident_r_set = sem("ident_r_set")
        rope_loaded = sem("rope_loaded")
        route_loaded = sem("route_loaded")
        count_loaded = sem("count_loaded")
        member_ready = sem("member_ready")
        rank_ready = sem("rank_ready")
        x_tok_hi_done = sem("x_tok_hi_done")
        x_tok_split = sem("x_tok_split")
        sel_built = sem("sel_built")
        selt_ready = sem("selt_ready")
        selt_done = sem("selt_done")
        xg_ready = sem("xg_ready")
        xg_done = sem("xg_done")
        gu_ready = sem("gu_ready")
        h_split = sem("h_split")
        y_ready = sem("y_ready")
        y_hi_done = sem("y_hi_done")
        y_split = sem("y_split")
        sc_ready = sem("sc_ready")
        sc_done = sem("sc_done")
        meta_ready = sem("meta_ready")
        out_stored = sem("out_stored")

        with ExitStack() as phase:
            def pb(name, shape, dt=F32):
                return phase.enter_context(nc.sbuf_tensor(name, shape, dt))

            qs = pb("qs", [P, 2, C, P], F32R)
            pt = pb("pt", [P, NCH, P], F32R)
            S = pb("scores", [P, 2, KEYS])
            lorow = pb("lorow", [QL, 2, HALF])
            olo = pb("olo", [QL, D])
            O = pb("attended", [QL, D])
            cols = pb("cols", [QL, 4, 2])
            mx, nb, sums, rinv = (cols[:, j, :] for j in range(4))
            kvs = pb("kvs", [P, 2, HALF])
            xn1 = S[:, :, 0:D]
            wr_raw = pb("wr_raw", [P, C, NE])
            temp = small[:, 14, 31:32]
        with ExitStack() as phase:
            qk = pb("qk", [P, TT, 2 * D])
            sc = pb("head_scores", [P, 2, D])
            qkt = pb("qkt", [P, 2 * C, P])
            pth = pb("pth", [P, H, QL])
            heads = pb("heads", [P, 3, H])
            rope_c = pb("rope_c", [P, ROPE])
            cos_t, sin_t, mask_t = (rope_c[:, j * DH:(j + 1) * DH] for j in range(3))
            hmx, hsum, hinv = (heads[:, j, :] for j in range(3))
            rope_a, rope_b = sc[:, 0, :].rearrange("p (s n) -> p s n", s=2), sc[:, 1, :].rearrange("p (s n) -> p s n", s=2)
            xn2 = sc[:, :, :]
        with ExitStack() as phase:
            x_tok_hi = pb("x_tok_hi", [P, TT, D], F32R)
            x_tok_lo = pb("x_tok_lo", [P, TT, D], F32R)
            h_hi = pb("h_hi", [P, C, CAP], F32R)
            h_lo = pb("h_lo", [P, C, CAP], F32R)
            sel = pb("sel", [P, TT, CAP], F32R)
            with nc.sbuf_tensor("count_c", [P, 2 * P], F32) as count_c:
                pass
            earlier, ones = count_c[:, 0:P], count_c[:, P:2 * P]
            selt = pb("selt", [P, NT, TOK], F32R)
            route_c = pb("route_c", [P, ROUTE])
            places, expert_ids = route_c[:, 0:CAP], route_c[:, CAP:]
        xn3 = xn2
        silu = xq[:, TT * D:TT * D + 2 * CAP].rearrange("p (s n) -> p s n", s=2)
        xg = act_hi
        y = act_lo[:, :, :].rearrange("p (h n a) b -> p h n (a b)", h=2, n=NT)
        xn_of = (xn1, xn2, xn3)
        v = x

        free = released()
        release = {"gu_ready": gu_ready, "y_ready": y_ready, "out_ready": out_ready, "unit_used": unit_used, "s_ready": s_ready, "o_ready": o_ready}
        assert len(free) == U_FFN + NE * PER_EXPERT

        block = ctx.enter_context(nc.Block())

        @block.sync
        def _(sp):
            def load(k, src, per=0, i=0, dst=None):
                if k >= RING:
                    sp.wait_ge(lo_done, k - RING + 1 + per * i)
                sp.dma_start(raw[:, k % RING, :] if dst is None else dst, src).then_inc(landed[k % RING], 16)

            def load_keys(k, b, per=0, i=0, first=False):
                for u in range(6):
                    load(k + u, keys_d[b, u], per, i)
                view = raw[:, (k + 6) % RING, 0:C * (KTAIL + QL)].rearrange("p (c n) -> p c n", c=C)
                load(k + 6, tail_d[b], per, i, view[:, :, 0:KTAIL])
                if first:
                    for s in range(2):
                        sp.wait_ge(kv_stored[s], 16 * 8)
                sp.dma_start(view[:, :, KTAIL:], new_k_d[:, :, bass.ds(b * QL, QL)]).then_inc(new_landed, 16)

            def load_values(k, b, per=0, i=0):
                for u in range(6):
                    load(k + u, ctx_d[b, 2 * P * u:2 * P * (u + 1), :].rearrange("(j p) d -> p j d", p=P), per, i,
                         raw[:, (k + u) % RING, :].rearrange("p (j d) -> p j d", j=2))
                load(k + 6, ctx_d[b, KFULL:KV, :], per, i, raw[0:KREM, (k + 6) % RING, 0:D])
                sp.dma_start(raw[0:QL, (k + 6) % RING, D:2 * D],
                             new_v_d[bass.ds(b * QL, QL), :]).then_inc(new_landed, 16)

            for t in range(TT):
                sp.dma_start(x[:, t, :], x_d[t * P:(t + 1) * P, :]).then_inc(x_loaded[t], 16)
                if t == 0:
                    sp.dma_start(ident, ident_d).then_inc(consts_loaded, 16)
            for k in range(RING):
                load(k, w_d[k])
            sp.dma_start(wr_raw[:, :, :], wr_d).then_inc(router_loaded, 16)
            sp.dma_start(temp, temp_d).then_inc(temp_loaded, 16)
            with sp.Fori(0, 2) as i:
                for k in range(RING):
                    load(RING + k, w_d[4 * i + RING + k], RING, i)
            load_keys(U_KEYS0, 0, first=True)
            k0 = U_KEYS0 + 7
            load_keys(k0, 1)
            load_values(k0 + 7, 0)
            with sp.Fori(0, 3) as i:
                for s in range(2):
                    k = k0 + PER_BATCH * (1 + s)
                    load_keys(k, 2 * i + (s + 2), 2 * PER_BATCH, i)
                    load_values(k + 7, 2 * i + (s + 1), 2 * PER_BATCH, i)
            load_values(k0 + 7 * PER_BATCH, B - 1)
            with sp.Fori(0, (U_FFN + NE * PER_EXPERT - U_WO) // RING) as i:
                for k in range(RING):
                    load(U_WO + k, w_d[4 * i + (U_KEYS0 + k)], RING, i)
            sp.wait_ge(meta_ready, 1)
            more = sp.value_load(meta[0:1, 0:1], min_val=0, max_val=NE)
            with sp.If(more > 0):
                with sp.Fori(0, more) as j:
                    e = sp.value_load(meta[0:1, bass.ds(j + 1, 1)], min_val=0, max_val=NE - 1)
                    for k in range(PER_EXPERT):
                        load(U_FFN + NE * PER_EXPERT + k, w_d[PER_EXPERT * e + (W_FFN + k)], PER_EXPERT, j)
            sp.wait_ge(sc_done, 8 * more + (8 * NE + 1))
            sp.dma_start(out_d.rearrange("(t p) d -> p t d", p=P), x[:, :, :]).then_inc(out_stored, 16)
            sp.wait_ge(out_stored, 16)

        @block.gpsimd
        def _(pool):
            for f in range(C):
                pool.wait_ge(evacuated, O_QK + C + f + 1)
                pool.dma_start(new_k_d[:, f, :], kvs[:, f % 2, :]).then_inc(kv_stored[f % 2], 16)
            for n in range(8):
                g, t = n // TT, n % TT
                pool.wait_ge(evacuated, O_V + n + 1)
                pool.dma_start(new_v_d[t * P:(t + 1) * P, g * HALF:(g + 1) * HALF],
                               kvs[:, n % 2, :]).then_inc(kv_stored[n % 2], 16)
            pool.wait_ge(q_split, B + 1)
            pool.dma_start(x[:, :, :], x_d.rearrange("(t p) d -> p t d", p=P)).then_inc(x_reloaded, 16)
            pool.wait_ge(ot_split, B)
            pool.dma_start(rope_c[:, :], rope_d).then_inc(rope_loaded, 16)
            pool.wait_ge(xn_ready, 2 * TT)
            pool.dma_start(x_mid_d, xq[:, 0:TT * D]).then_inc(x_mid_stored, 16)
            pool.wait_ge(ho_ready, TT)
            pool.wait_ge(x_mid_stored, 16)
            pool.dma_start(xq[:, 0:TT * D], x_mid_d).then_inc(x_mid_loaded, 16)
            pool.wait_ge(ho_split, TT)
            pool.dma_start(route_c[:, :], route_d).then_inc(route_loaded, 16)
            pool.dma_start(count_c[:, :], count_d).then_inc(count_loaded, 16)

        SC_BANK = (4, 5, 0, 1)
        Y_BANK = (6, 2)
        KEY_LAST, VALUE_LAST = "keys", "values"

        def part(buf, k, kind):
            if kind == KEY_LAST:
                return buf[:, k % RING, 0:C * (KTAIL + QL)]
            if kind == VALUE_LAST:
                return buf[0:KREM, k % RING, :]
            return buf[:, k % RING, :]

        def kind_of(pos):
            return {6: KEY_LAST, 13: VALUE_LAST}.get(pos % PER_BATCH)

        @block.scalar
        def _(act):
            def split(k, per=0, i=0, kind=None, used=None):
                act.wait_ge(landed[k % RING], 16 * (per // RING) * i + 16 * (k // RING + 1))
                if kind:
                    b2 = (k - U_KEYS0 - 6) // 7
                    act.wait_ge(new_landed, 16 * (b2 + 1) + 16 * (per // 7) * i)
                if used:
                    act.wait_ge(*used)
                elif k >= RING:
                    name, value = free[k - RING + per]
                    grows = free[k - RING + 2 * per][1] - value
                    act.wait_ge(release[name], grows * i + (value - grows) if per else value)
                act.activation(part(hi, k, kind), part(raw, k, kind), ACT.Copy).then_inc(hi_done, 1)

            def norm(n, base):
                act.wait_ge(stats_ready, TT * (n + 1))
                act.activation(std[:, :], mv[:, :, 1], ACT.Sqrt, bias=eps[:, 0:1]).then_inc(std_ready, 1)
                if n == 2:
                    for t in range(TT):
                        act.wait_ge(xn_ready, TT * n + t + 1)
                        act.activation(x_tok_hi[:, t, :], xn_of[n][:, t % 2, :], ACT.Copy).then_inc(x_tok_hi_done, 1)
                for j in range(2 * TT):
                    t, h = j // 2, j % 2
                    act.wait_ge(out_ready, base + j + 1)
                    act.activation(act_hi[:, 4 * h:4 * h + 4, t * P:(t + 1) * P],
                                   ps[:, j, :].rearrange("p (c n) -> p c n", c=4), ACT.Copy).then_inc(ln_hi, 1)

            act.wait_ge(router_loaded, 16)
            act.activation(wr_hi[:, :, :], wr_raw[:, :, :], ACT.Copy).then_inc(wr_hi_done, 1)
            act.wait_ge(eps_set, 1)
            act.wait_ge(consts_loaded, 16)
            act.activation(ident_r[:, :], ident, ACT.Copy).then_inc(ident_r_set, 1)
            for k in range(AHEAD):
                split(k)
            norm(0, O_LN1)
            for k in range(U_Q, U_KEYS0):
                split(k + AHEAD)

            def q_hi(s, b, i=0):
                if s >= 2:
                    act.wait_ge(s_ready, 4 * (s - 1) + 8 * i)
                act.activation(qs[:, s % 2, :, 0:QL], q[:, b, :, :], ACT.Copy).then_inc(q_hi_done, 1)

            def score_rows(s, j, i=0):
                n = 4 * s + j
                w = HALF if j < 3 else KTAIL + QL
                act.wait_ge(s_ready, n + 1 + 8 * i)
                if n >= 2:
                    act.wait_ge(s_evac, n - 1 + 8 * i)
                act.activation(lorow[:, j % 2, 0:w], ps[QL:P, j, 0:w], ACT.Copy).then_inc(lorow_ready, 1)

            def exps(s, i=0):
                act.wait_ge(negmax_ready, s + 1 + 2 * i)
                act.activation(S[0:QL, s % 2, :], S[0:QL, s % 2, :], ACT.Exp, bias=nb[:, s % 2:s % 2 + 1], scale=SCALE,
                               accum_out=sums[:, s % 2:s % 2 + 1]).then_inc(p_ready, 1)

            def ot_hi(s, b, i=0):
                act.wait_ge(ot_ready, s + 1 + 2 * i)
                act.activation(act_hi[:, :, bass.ds(b * QL, QL)], ps[:, 6, :].rearrange("p (c n) -> p c n", c=C),
                               ACT.Copy).then_inc(ot_hi_done, 1)

            def step(s, i=0, loop=False, nxt=True):
                per = 2 * PER_BATCH if loop else 0
                k0 = U_KEYS0 + 7 + PER_BATCH * s
                for pos in range(0 if nxt else 7, PER_BATCH):
                    k = k0 + pos - (0 if nxt else 7)
                    split(k + AHEAD, per, i, kind_of(pos + AHEAD) if nxt or pos + AHEAD < PER_BATCH else None)
                    if pos == 1:
                        score_rows(s + 1, 0, i)
                        if s > 0:
                            ot_hi(s - 1, 2 * i + (s - 1), i)
                    if pos in (3, 5):
                        score_rows(s + 1, pos // 2, i)
                    if pos == 6:
                        score_rows(s + 1, 3, i)
                    if pos == (6 if nxt else 7):
                        if not nxt:
                            ot_hi(s - 1, s - 1)
                        for h, (a, e) in enumerate(((0, 8), (8, NCH))):
                            act.wait_ge(pt_ready, 2 * s + h + 1 + 4 * i)
                            act.activation(pt[:, a:e, 0:QL],
                                           ps[:, 4 + h, 0:(e - a) * QL].rearrange("p (k n) -> p k n", n=QL),
                                           ACT.Copy).then_inc(pt_hi_done, 1)
                        if nxt:
                            exps(s + 1, i)
                    if pos == 8 and nxt:
                        q_hi(s + 2, 2 * i + (s + 2), i)
                    if pos == 13:
                        act.wait_ge(o_ready, s + 1 + 2 * i)
                        act.activation(olo[:, :], ps[QL:P, 6:8, :].rearrange("p a n -> p (a n)"),
                                       ACT.Copy).then_inc(olo_ready, 1)

            act.wait_ge(evacuated, O_QK + C)
            q_hi(0, 0)
            q_hi(1, 1)
            for pos in range(7):
                split(U_KEYS0 + pos + AHEAD, kind=KEY_LAST if pos + AHEAD == 6 else None)
                if pos in (1, 3, 5, 6):
                    score_rows(0, (pos + 1) // 2 - (pos < 6) if pos < 6 else 3)
            exps(0)
            step(0)
            with act.Fori(0, 3) as i:
                step(1, i, True)
                step(2, i, True)
            step(7, nxt=False)
            ot_hi(7, 7)

            for k in range(U_WO, U_QKV):
                split(k + AHEAD)
            norm(1, O_LN2)
            with act.Fori(0, 3) as i:
                for k in range(RING):
                    split(U_QKV + k + AHEAD, RING, i)

            def heads_t(t):
                for w in range(2):
                    act.wait_ge(tq_ready, 2 * t + w + 1)
                    act.activation(qkt[:, C * w:C * (w + 1), :].rearrange("p c n -> p (c n)"),
                                   ps[:, 2 * w:2 * w + 2, :].rearrange("p a n -> p (a n)"),
                                   ACT.Copy).then_inc(tq_evac, 1)

            def heads_exp(t):
                act.wait_ge(hs_shifted, t + 1)
                act.activation(sc[:, t % 2, :], sc[:, t % 2, :], ACT.Exp).then_inc(hs_exp, 1)

            heads_t(0)
            heads_exp(0)
            for t in range(TT):
                if t + 1 < TT:
                    heads_t(t + 1)
                    heads_exp(t + 1)
                act.wait_ge(hpt_ready, t + 1)
                for b in range(2):
                    act.activation(pth[b * QL:(b + 1) * QL, :, :],
                                   ps[0:QL, 0:4, :].rearrange("p a (j n) -> p (a j) n", n=P)[:, :, b * QL:(b + 1) * QL],
                                   ACT.Copy).then_inc(hpt_evac, 1)
                act.wait_ge(ho_ready, t + 1)
                act.activation(act_hi[:, :, t * P:(t + 1) * P].rearrange("p c (b n) -> p b c n", b=2),
                               ps[:, 6:8, :].rearrange("p b (c n) -> p b c n", c=C), ACT.Copy).then_inc(ho_hi, 1)

            for k in range(U_WOUT, U_FFN):
                split(k + AHEAD)
            norm(2, O_LN3)

            act.wait_ge(z_ready, 1)
            act.activation(small[:, 1, :], small[:, 0, :], ACT.Exp, scale=-1.0).then_inc(ez_ready, 1)
            act.wait_ge(dist_ready, 1)
            act.activation(small[:, 5, :], small[:, 4, :], ACT.Exp, scale=-1.0 / 0.1).then_inc(edist_ready, 1)
            act.activation(small[:, 6, :], small[:, 4, :], ACT.Exp, scale=-1.0 / 0.3).then_inc(edist_ready, 1)

            def gathered(e):
                for c in range(C):
                    act.wait_ge(xg_ready, C * e + (c + 1))
                    act.activation(xg[:, c, :], ps[:, 2 + c % 4, :], ACT.Copy).then_inc(xg_done, 1)

            def item(e, u0, first, more):
                if first:
                    for k in range(AHEAD):
                        split(u0 + k, PER_EXPERT, e)
                    gathered(e)
                for n in range(NT):
                    act.wait_ge(selt_ready, NT * e + (n + 1))
                    act.activation(selt[:, n, :], ps[:, 6 + n, :], ACT.Copy).then_inc(selt_done, 1)
                for k in range(PER_EXPERT):
                    if more or k + AHEAD < PER_EXPERT:
                        split(u0 + k + AHEAD, PER_EXPERT, e, used=(gu_ready, 8 * e + 1) if k == 0 else None)
                    if k < 8:
                        act.wait_ge(gu_ready, 8 * e + (k + 1))
                        act.activation(silu[:, k % 2, :], ps[:, k % 2, 0:CAP], ACT.Silu).then_inc(silu_done, 1)
                    if k == 7 and more:
                        gathered(e + 1)
                    if k in (9, 11):
                        g = (k - 9) // 2
                        for n in range(NT):
                            act.wait_ge(y_ready, 4 * e + (2 * g + n + 1))
                            act.activation(y[:, 0, n, g * HALF:(g + 1) * HALF], ps[:, Y_BANK[g] + n, :],
                                           ACT.Copy).then_inc(y_hi_done, 1)

            gathered(0)
            with act.Fori(0, NE - 1) as e:
                item(e, U_FFN, False, True)
            item(NE - 1, U_FFN, False, False)
            act.wait_ge(meta_ready, 1)
            more = act.value_load(meta[0:1, 0:1], min_val=0, max_val=NE)
            with act.If(more > 0):
                with act.Fori(0, more) as j:
                    item(j + NE, U_FFN, True, False)

        @block.vector
        def _(dve):
            steps = Steps(dve, dve_step)

            def split(k, per=0, i=0, kind=None):
                dve.wait_ge(hi_done, k + 1 + per * i)
                dve.tensor_tensor(part(lo, k, kind), part(raw, k, kind), part(hi, k, kind),
                                  ALU.subtract).then_inc(lo_done, 1)

            def tok_lo(t):
                dve.wait_ge(x_tok_hi_done, t + 1)
                dve.tensor_tensor(x_tok_lo[:, t, :], xn3[:, t % 2, :], x_tok_hi[:, t, :],
                                  ALU.subtract).then_inc(x_tok_split, 1)

            def norm(n, base):
                for t in range(TT):
                    if n == 0:
                        dve.wait_ge(x_loaded[t], 16)
                    for h in range(2):
                        steps.done(dve.bn_stats(stats[:, t, h, :], x[:, t, h * HALF:(h + 1) * HALF]))
                steps.wait()
                for t in range(TT):
                    dve.bn_aggr(mv[:, t, :], stats[:, t, :, :].rearrange("p h n -> p (h n)")).then_inc(stats_ready, 1)
                dve.wait_ge(std_ready, n + 1)
                steps.done(dve.reciprocal(rstd[:, :], std[:, :]))
                steps.wait()
                for t in range(TT):
                    if n == 2 and t >= 2:
                        tok_lo(t - 2)
                        dve.wait_ge(x_tok_split, t - 1)
                    if t >= 2:
                        dve.wait_ge(out_ready, base + 2 * (t - 2) + 2)
                    dve.tensor_scalar(xn_of[n][:, t % 2, :], x[:, t, :], mv[:, t, 0:1], rstd[:, t:t + 1],
                                      ALU.subtract, ALU.mult).then_inc(xn_ready, 1)
                if n == 2:
                    tok_lo(2)
                    tok_lo(3)
                for j in range(2 * TT):
                    t, h = j // 2, j % 2
                    to = (slice(None), slice(4 * h, 4 * h + 4), slice(t * P, (t + 1) * P))
                    dve.wait_ge(ln_hi, 2 * TT * n + j + 1)
                    dve.tensor_tensor(act_lo[to], ps[:, j, :].rearrange("p (c n) -> p c n", c=4), act_hi[to],
                                      ALU.subtract).then_inc(evacuated, 1)

            dve.memset(eps[:, :], EPS).then_inc(eps_set, 1)
            dve.wait_ge(wr_hi_done, 1)
            dve.tensor_tensor(wr_lo[:, :, :], wr_raw[:, :, :], wr_hi[:, :, :], ALU.subtract).then_inc(wr_split, 1)
            norm(0, O_LN1)
            for k in range(AHEAD):
                split(k)
            dve.wait_ge(xn_ready, TT)
            dve.memset(q[:, B, :, :], 0.0)
            for k in range(U_Q, U_V):
                split(k + AHEAD)
                for j in range(2):
                    f = 2 * k + j
                    dve.wait_ge(out_ready, O_QK + f + 1)
                    if f < C:
                        dve.tensor_copy(q[:, 0:B, f, :], ps[:, f % 4, :].rearrange("p (b n) -> p b n", b=B))\
                           .then_inc(evacuated, 1)
                    else:
                        if f >= C + 2:
                            dve.wait_ge(kv_stored[f % 2], 16 * ((f - C) // 2))
                        dve.tensor_copy(kvs[:, f % 2, :], ps[:, f % 4, :]).then_inc(evacuated, 1)
            for k in range(U_V, U_KEYS0):
                split(k + AHEAD)
                g, half = (k - U_V) // 2, (k - U_V) % 2
                if half:
                    for t in range(TT):
                        n = g * TT + t
                        dve.wait_ge(out_ready, O_V + n + 1)
                        dve.wait_ge(kv_stored[n % 2], 16 * (4 + n // 2))
                        dve.tensor_copy(kvs[:, n % 2, :], ps[:, 4 * (1 - g) + t, :]).then_inc(evacuated, 1)

            def q_lo(s, b, i=0):
                dve.wait_ge(q_hi_done, s + 1 + 2 * i)
                dve.tensor_tensor(qs[:, s % 2, :, QL:P], q[:, b, :, :], qs[:, s % 2, :, 0:QL],
                                  ALU.subtract).then_inc(q_split, 1)

            def score_add(s, j, i=0):
                n = 4 * s + j
                w = HALF if j < 3 else KTAIL + QL
                at = j * HALF if j < 3 else KFULL - 1
                dve.wait_ge(lorow_ready, n + 1 + 8 * i)
                if j == 3:
                    dve.wait_ge(s_evac, n + 8 * i)
                dve.tensor_tensor(S[0:QL, s % 2, at:at + w], ps[0:QL, j, 0:w], lorow[:, j % 2, 0:w],
                                  ALU.add).then_inc(s_evac, 1)

            def row_max(s, i=0):
                dve.wait_ge(s_evac, 4 * s + 4 + 8 * i)
                steps.done(dve.tensor_reduce(mx[:, s % 2:s % 2 + 1], S[0:QL, s % 2, :], AX.X, ALU.max))
                steps.wait()
                dve.tensor_scalar(nb[:, s % 2:s % 2 + 1], mx[:, s % 2:s % 2 + 1], -SCALE, None,
                                  ALU.mult).then_inc(negmax_ready, 1)

            def ot_lo(s, b, i=0):
                dve.wait_ge(ot_hi_done, s + 1 + 2 * i)
                dve.tensor_tensor(act_lo[:, :, bass.ds(b * QL, QL)], ps[:, 6, :].rearrange("p (c n) -> p c n", c=C),
                                  act_hi[:, :, bass.ds(b * QL, QL)], ALU.subtract).then_inc(ot_split, 1)

            def step(s, i=0, loop=False, nxt=True):
                per = 2 * PER_BATCH if loop else 0
                k0 = U_KEYS0 + 7 + PER_BATCH * s
                for pos in range(0 if nxt else 7, PER_BATCH):
                    k = k0 + pos - (0 if nxt else 7)
                    split(k + AHEAD, per, i, kind_of(pos + AHEAD) if nxt or pos + AHEAD < PER_BATCH else None)
                    if pos == 1:
                        score_add(s + 1, 0, i)
                        if s > 0:
                            ot_lo(s - 1, 2 * i + (s - 1), i)
                    if pos in (3, 5):
                        score_add(s + 1, pos // 2, i)
                    if pos == 6:
                        score_add(s + 1, 3, i)
                    if pos == (6 if nxt else 7):
                        if not nxt:
                            ot_lo(s - 1, s - 1)
                        for h, (a, e) in enumerate(((0, 8), (8, NCH))):
                            dve.wait_ge(pt_hi_done, 2 * s + h + 1 + 4 * i)
                            dve.tensor_tensor(pt[:, a:e, QL:P],
                                              ps[:, 4 + h, 0:(e - a) * QL].rearrange("p (k n) -> p k n", n=QL),
                                              pt[:, a:e, 0:QL], ALU.subtract).then_inc(pt_split, 1)
                        if nxt:
                            row_max(s + 1, i)
                    if pos == 8 and nxt:
                        q_lo(s + 2, 2 * i + (s + 2), i)
                    if pos == 13:
                        dve.wait_ge(olo_ready, s + 1 + 2 * i)
                        dve.tensor_tensor(O[:, :], ps[0:QL, 6:8, :].rearrange("p a n -> p (a n)"), olo[:, :],
                                          ALU.add).then_inc(o_evac, 1)
                        steps.done(dve.reciprocal(rinv[:, s % 2:s % 2 + 1], sums[:, s % 2:s % 2 + 1]))
                        dve.wait_ge(o_evac, s + 1 + 2 * i)
                        steps.wait()
                        dve.tensor_scalar(O[:, :], O[:, :], rinv[:, s % 2:s % 2 + 1], None,
                                          ALU.mult).then_inc(o_norm, 1)

            q_lo(0, 0)
            q_lo(1, 1)
            for pos in range(7):
                split(U_KEYS0 + pos + AHEAD, kind=KEY_LAST if pos + AHEAD == 6 else None)
                if pos in (1, 3, 5):
                    score_add(0, pos // 2)
                if pos == 6:
                    score_add(0, 3)
            row_max(0)
            step(0)
            with dve.Fori(0, 3) as i:
                steps.loop(i, 4)
                step(1, i, True)
                step(2, i, True)
                steps.end(3)
            step(7, nxt=False)
            ot_lo(7, 7)

            def residual(u0, base):
                for k in range(4):
                    split(u0 + k + AHEAD)
                    if k % 2:
                        g = k // 2
                        for t in range(TT):
                            dve.wait_ge(out_ready, base + g * TT + t + 1)
                            to = x[:, t, g * HALF:(g + 1) * HALF]
                            dve.tensor_tensor(to, ps[:, 4 * (1 - g) + t, :], to, ALU.add).then_inc(evacuated, 1)
                dve.wait_ge(evacuated, base + 2 * TT)

            dve.wait_ge(x_reloaded, 16)
            residual(U_WO, O_WO)
            norm(1, O_LN2)

            dve.wait_ge(rope_loaded, 16)
            dve.wait_ge(xn_ready, 2 * TT)
            cos8 = cos_t.unsqueeze(1).to_broadcast([P, 8, DH])
            sin4 = sin_t.rearrange("p (n w) -> p n w", w=2)

            def rope(g, t, i):
                n = 4 * g + t
                bank = 4 * (1 - g) + t
                dve.wait_ge(out_ready, O_QKV + n + 1 + 8 * i)
                dve.wait_ge(evacuated, O_QKV + n - 1 + 8 * i)
                a, b = rope_a[:, t % 2, :], rope_b[:, t % 2, :]
                steps.done(dve.tensor_tensor(a.rearrange("p (h d) -> p h d", d=DH),
                                             ps[:, bank, :].rearrange("p (h d) -> p h d", d=DH), cos8, ALU.mult))
                pw = ps[:, bank, :].rearrange("p (h n w) -> p h n w", n=DH // 2, w=2)
                bw = b.rearrange("p (h n w) -> p h n w", n=DH // 2, w=2)
                for w in range(2):
                    steps.done(dve.tensor_tensor(bw[:, :, :, w], pw[:, :, :, 1 - w],
                                                 sin4[:, :, w].unsqueeze(1).to_broadcast([P, 8, DH // 2]), ALU.mult))
                steps.wait()
                dve.tensor_tensor(qk[:, t, bass.ds(i * D + g * HALF, HALF)], a, b, ALU.add).then_inc(evacuated, 1)

            with dve.Fori(0, 2) as i:
                steps.loop(i, 24)
                for k in range(4):
                    split(U_QKV + k + AHEAD, RING, i)
                    if k % 2:
                        for t in range(TT):
                            rope(k // 2, t, i)
                steps.end(2)
            dve.wait_ge(x_mid_stored, 16)
            for k in range(4):
                split(U_QKV + 8 + k + AHEAD)
                if k % 2:
                    g = k // 2
                    for t in range(TT):
                        dve.wait_ge(out_ready, O_QKV + 16 + 4 * g + t + 1)
                        dve.tensor_copy(v[:, t, g * HALF:(g + 1) * HALF], ps[:, 4 * (1 - g) + t, :])\
                           .then_inc(evacuated, 1)

            def heads_scores(t):
                dve.wait_ge(hs_ready, t + 1)
                s3 = sc[:, t % 2, :].rearrange("p (h n) -> p h n", n=DH)
                dve.scalar_tensor_tensor(out=s3, in0=ps[:, 4:6, :].rearrange("p a (c n) -> p (a c) n", n=DH),
                                         scalar=HEAD_SCALE, in1=mask_t.unsqueeze(1).to_broadcast([P, H, DH]),
                                         op0=ALU.mult, op1=ALU.add).then_inc(hs_used, 1)
                dve.wait_ge(hs_used, t + 1)
                steps.done(dve.tensor_reduce(hmx, s3, AX.X, ALU.max))
                steps.wait()
                dve.tensor_tensor(s3, s3, hmx.unsqueeze(2).to_broadcast([P, H, DH]),
                                  ALU.subtract).then_inc(hs_shifted, 1)

            def heads_norm(t):
                s3 = sc[:, t % 2, :].rearrange("p (h n) -> p h n", n=DH)
                dve.wait_ge(hs_exp, t + 1)
                steps.done(dve.tensor_reduce(hsum, s3, AX.X, ALU.add))
                steps.wait()
                steps.done(dve.reciprocal(hinv, hsum))
                steps.wait()
                dve.tensor_tensor(s3, s3, hinv.unsqueeze(2).to_broadcast([P, H, DH]),
                                  ALU.mult).then_inc(hp_ready, 1)

            def heads_out(t):
                dve.wait_ge(ho_hi, t + 1)
                to = [a[:, :, t * P:(t + 1) * P].rearrange("p c (b n) -> p b c n", b=2) for a in (act_lo, act_hi)]
                dve.tensor_tensor(to[0], ps[:, 6:8, :].rearrange("p b (c n) -> p b c n", c=C), to[1],
                                  ALU.subtract).then_inc(ho_split, 1)

            heads_scores(0)
            heads_norm(0)
            for t in range(TT):
                if t + 1 < TT:
                    heads_scores(t + 1)
                    heads_norm(t + 1)
                heads_out(t)
            dve.wait_ge(x_mid_loaded, 16)
            residual(U_WOUT, O_WOUT)
            norm(2, O_LN3)

            def sm(j):
                return small[:, j, :]

            def sm3(j):
                return small[:, j, :].rearrange("p (t e) -> p t e", e=NE)

            def dep(ins):
                steps.done(ins)
                steps.wait()

            dve.wait_ge(temp_loaded, 16)
            dep(dve.reciprocal(temp, temp))
            dve.wait_ge(logits_ready, 1)
            dve.tensor_scalar(sm(0), ps[:, 0, 0:TT * NE], temp, None, ALU.mult).then_inc(z_ready, 1)
            dve.wait_ge(ez_ready, 1)
            dep(dve.tensor_scalar(sm(2), sm(1), 1.0, None, ALU.add))
            dep(dve.reciprocal(sm(3), sm(2)))
            dep(dve.tensor_scalar(sm(7), sm(3), LOWER, None, ALU.is_ge))
            dep(dve.scalar_tensor_tensor(out=sm(7), in0=sm(3), scalar=UPPER, in1=sm(7),
                                         op0=ALU.is_le, op1=ALU.mult))
            dep(dve.tensor_scalar(sm(8), sm(3), -1.0, CENTER, ALU.mult, ALU.add))
            dep(dve.tensor_scalar(sm(9), sm(3), CENTER, None, ALU.subtract))
            dve.tensor_tensor(sm(4), sm(8), sm(9), ALU.max).then_inc(dist_ready, 1)
            dve.wait_ge(edist_ready, 2)
            dep(dve.tensor_tensor(sm(5), sm(5), sm(7), ALU.mult))
            dep(dve.tensor_reduce(small[:, 10, 0:TT], sm3(5), AX.X, ALU.add))
            dep(dve.tensor_scalar(small[:, 10, TT:2 * TT], small[:, 10, 0:TT], 1e-8, None, ALU.is_lt))
            dep(dve.memset(sm(11), 0.0))
            for j in range(NE):
                each = sm3(6)[:, :, j:j + 1]
                steps.done(dve.tensor_tensor(sm3(12)[:, :, 0:j + 1], each.to_broadcast([P, TT, j + 1]),
                                             sm3(6)[:, :, 0:j + 1], ALU.is_gt))
                if j + 1 < NE:
                    steps.done(dve.tensor_tensor(sm3(12)[:, :, j + 1:NE], each.to_broadcast([P, TT, NE - 1 - j]),
                                                 sm3(6)[:, :, j + 1:NE], ALU.is_ge))
                steps.wait()
                dep(dve.tensor_tensor(sm(11), sm(11), sm(12), ALU.add))
            dep(dve.scalar_tensor_tensor(out=sm(13), in0=sm(11), scalar=2.0, in1=sm(6),
                                         op0=ALU.is_lt, op1=ALU.mult))

            def normalised(j, at):
                dep(dve.tensor_reduce(small[:, 14, at:at + TT], sm3(j), AX.X, ALU.add))
                dep(dve.tensor_scalar(small[:, 14, at:at + TT], small[:, 14, at:at + TT], 1e-8, None, ALU.max))
                dep(dve.reciprocal(small[:, 14, at + TT:at + 2 * TT], small[:, 14, at:at + TT]))
                dep(dve.tensor_tensor(sm3(j), sm3(j),
                                      small[:, 14, at + TT:at + 2 * TT].unsqueeze(2).to_broadcast([P, TT, NE]),
                                      ALU.mult))

            normalised(13, 0)
            flag = small[:, 10, TT:2 * TT].unsqueeze(2).to_broadcast([P, TT, NE])
            dep(dve.tensor_tensor(sm3(13), sm3(13), flag, ALU.mult))
            dep(dve.tensor_scalar(small[:, 10, 2 * TT:3 * TT], small[:, 10, TT:2 * TT], -1.0, 1.0, ALU.mult, ALU.add))
            dep(dve.tensor_tensor(sm3(5), sm3(5), small[:, 10, 2 * TT:3 * TT].unsqueeze(2).to_broadcast([P, TT, NE]),
                                  ALU.mult))
            dep(dve.tensor_tensor(sm(5), sm(5), sm(13), ALU.add))
            normalised(5, 2 * TT)
            dve.wait_ge(edist_ready, 2)
            dve.tensor_scalar(sm(0), sm(5), 0.0, None, ALU.is_gt).then_inc(member_ready, 1)
            dep(dve.tensor_copy(item_w[:, :, 0:NE], sm3(5)))
            dve.wait_ge(rank_ready, 1)
            dep(dve.scalar_tensor_tensor(out=sm(1), in0=ps[:, 1, 0:TT * NE], scalar=1.0, in1=sm(0),
                                         op0=ALU.add, op1=ALU.mult))
            dep(dve.tensor_scalar(item_slot[:, :, 0:NE], sm3(1), 1.0, None, ALU.subtract))
            dve.tensor_copy(small[:, 2, 0:NE], ps[:, 1, TT * NE:(TT + 1) * NE]).then_inc(sc_done, 1)
            dve.wait_ge(sc_done, 1)

            dve.wait_ge(route_loaded, 16)

            def build_sel(slot_of):
                for t in range(TT):
                    dve.tensor_scalar(sel[:, t, :], places, slot_of(t), None, ALU.is_equal).then_inc(sel_built, 1)

            build_sel(lambda t: item_slot[:, t, 0:1])

            count, has, number = (small[:, 2, j * NE:(j + 1) * NE] for j in range(3))
            dep(dve.tensor_scalar(has, count, float(CAP), None, ALU.is_gt))
            dep(dve.memset(number[:, 0:1], 0.0))
            for e in range(NE - 1):
                dep(dve.tensor_tensor(number[:, e + 1:e + 2], number[:, e:e + 1], has[:, e:e + 1], ALU.add))
            one = small[:, 6:8, :].rearrange("p a (x e) -> p (a x) e", e=NE)
            for j in range(NE):
                steps.done(dve.scalar_tensor_tensor(out=one[:, j, :], in0=number, scalar=float(j), in1=has,
                                                    op0=ALU.is_equal, op1=ALU.mult))
            steps.wait()
            over = small[:, 3, :].rearrange("p (t e) -> p t e", e=NE)
            dep(dve.tensor_scalar(over, item_slot[:, :, 0:NE], float(CAP), None, ALU.subtract))
            both = small[:, 8:10, :].rearrange("p a (x e) -> p (a x) e", e=NE)
            for t in range(TT):
                for src, to in ((over, item_slot), (sm3(5), item_w)):
                    dep(dve.tensor_tensor(both, one, src[:, t:t + 1, :].to_broadcast([P, NE, NE]), ALU.mult))
                    dep(dve.tensor_reduce(to[:, t, NE:ITEMS], both, AX.X, ALU.add))
            dep(dve.tensor_tensor(both, one, expert_ids.unsqueeze(1).to_broadcast([P, NE, NE]), ALU.mult))
            dep(dve.tensor_reduce(small[:, 10, 1:NE + 1], both, AX.X, ALU.add))
            dep(dve.tensor_reduce(small[:, 10, 0:1], has, AX.X, ALU.add))
            dve.tensor_copy(meta[:, :], small[:, 10, 0:NE + 1]).then_inc(meta_ready, 1)
            dve.wait_ge(meta_ready, 1)

            def item(e, u0, first, more):
                at = lambda a, t, n: a[:, t, bass.ds(e + n, 1)]
                if first:
                    for k in range(AHEAD):
                        split(u0 + k, PER_EXPERT, e)
                    dve.wait_ge(selt_ready, NT * e)
                    build_sel(lambda t: at(item_slot, t, 0))
                for k in range(PER_EXPERT):
                    if more or k + AHEAD < PER_EXPERT:
                        split(u0 + k + AHEAD, PER_EXPERT, e)
                    if k < 8:
                        dve.wait_ge(silu_done, 8 * e + (k + 1))
                        steps.done(dve.tensor_tensor(silu[:, k % 2, :], ps[:, k % 2, CAP:2 * CAP],
                                                     silu[:, k % 2, :], ALU.mult))
                        steps.wait()
                        steps.done(dve.tensor_copy(h_hi[:, k, :], silu[:, k % 2, :]))
                        steps.wait()
                        dve.tensor_tensor(h_lo[:, k, :], silu[:, k % 2, :], h_hi[:, k, :],
                                          ALU.subtract).then_inc(h_split, 1)
                    if k == 1 and more:
                        dve.wait_ge(selt_ready, NT * e + NT)
                        build_sel(lambda t: at(item_slot, t, 1))
                    if k in (9, 11):
                        g = (k - 9) // 2
                        cols = slice(g * HALF, (g + 1) * HALF)
                        for n in range(NT):
                            dve.wait_ge(y_hi_done, 4 * e + (2 * g + n + 1))
                            dve.tensor_tensor(y[:, 1, n, cols], ps[:, Y_BANK[g] + n, :], y[:, 0, n, cols],
                                              ALU.subtract).then_inc(y_split, 1)
                for g in range(2):
                    for t in range(TT):
                        dve.wait_ge(sc_ready, 8 * e + (4 * g + t + 1))
                        to = x[:, t, g * HALF:(g + 1) * HALF]
                        dve.scalar_tensor_tensor(out=to, in0=ps[:, SC_BANK[t], :], scalar=at(item_w, t, 0), in1=to,
                                                 op0=ALU.mult, op1=ALU.add).then_inc(sc_done, 1)

            with dve.Fori(0, NE - 1) as e:
                steps.loop(e, 16)
                item(e, U_FFN, False, True)
                steps.end(NE - 1)
            item(NE - 1, U_FFN, False, False)
            more = dve.value_load(meta[0:1, 0:1], min_val=0, max_val=NE)
            with dve.If(more > 0):
                with dve.Fori(0, more) as j:
                    steps.loop(j, 16)
                    item(j + NE, U_FFN, True, False)
                    steps.end(0)

        @block.tensor
        def _(pe):
            def unit_ready(k, per=0, i=0):
                pe.wait_ge(lo_done, k + 1 + per * i)

            def three(out, a_hi, a_lo, b_hi, b_lo, first, last):
                pe.matmul(out, a_hi, b_hi, start=first, stop=False)
                pe.matmul(out, a_hi, b_lo, start=False, stop=False)
                return pe.matmul(out, a_lo, b_hi, start=False, stop=last)

            def norm(n, base):
                if n == 0:
                    pe.wait_ge(consts_loaded, 16)
                for t in range(TT):
                    pe.wait_ge(xn_ready, TT * n + t + 1)
                    for h in range(2):
                        for c in range(4):
                            ins = pe.transpose(ps[:, 2 * t + h, c * P:(c + 1) * P],
                                               xn_of[n][:, t % 2, (4 * h + c) * P:(4 * h + c + 1) * P],
                                               ident)
                        ins.then_inc(out_ready, 1)
                pe.wait_ge(evacuated, base + 2 * TT)

            def stationary_unit(k, out, wait, per=0, i=0, used=True):
                unit_ready(k, per, i)
                for j in range(2):
                    wait(j)
                    for c in range(C):
                        at = slice(j * D + c * P, j * D + (c + 1) * P)
                        ins = three(ps[:, out(j), :], hi[:, k % RING, at], lo[:, k % RING, at],
                                    act_hi[:, c, :], act_lo[:, c, :], c == 0, c == C - 1)
                    yield ins

            def projection(u0, base, groups=2, per=0, i=0, out_per=0):
                for g in range(groups):
                    bank = 4 * (1 - g % 2)
                    for half in range(2):
                        k = u0 + 2 * g + half

                        def bank_free(t):
                            pe.wait_ge(evacuated, base + 4 * g + t - 7 + out_per * i)

                        ins = None
                        unit_ready(k, per, i)
                        for t in range(TT):
                            if half == 0:
                                bank_free(t)
                            for c in range(4):
                                cc = 4 * half + c
                                rows = slice(t * P, (t + 1) * P)
                                cols = slice(c * HALF, (c + 1) * HALF)
                                ins = three(ps[:, bank + t, :], act_hi[:, cc, rows], act_lo[:, cc, rows],
                                            hi[:, k % RING, cols], lo[:, k % RING, cols], cc == 0, cc == C - 1)
                            if half == 1:
                                ins.then_inc(out_ready, 1)
                        if half == 0:
                            ins.then_inc(unit_used, 1)

            norm(0, O_LN1)
            with pe.Fori(0, 2) as i:
                for k in range(RING):
                    def bank_free(j):
                        pe.wait_ge(evacuated, O_QK + 2 * k + j - 3 + 8 * i)
                    for j, ins in enumerate(stationary_unit(k, lambda j: (2 * k + j) % 4, bank_free, RING, i)):
                        ins.then_inc(out_ready, 1)
            projection(U_V, O_V)

            def score_block(s, u, i=0, per=0):
                k = U_KEYS0 + u if s == 0 else U_KEYS0 + 7 + PER_BATCH * (s - 1) + u
                j = u // 2
                if u == 0:
                    pe.wait_ge(q_split, s + 1 + 2 * i)
                if u % 2 == 0:
                    if s == 0:
                        pe.wait_ge(evacuated, O_V + 4 + j + 1)
                    else:
                        pe.wait_ge(s_evac, 4 * (s - 1) + j + 1 + 8 * i)
                unit_ready(k, per, i)
                n = 4 if u < 6 else C
                w = HALF if u < 6 else KTAIL + QL
                for c in range(n):
                    cc = 4 * (u % 2) + c
                    for b, buf in enumerate((hi, lo)):
                        ins = pe.matmul(ps[:, j, 0:w], qs[:, s % 2, cc, :], buf[:, k % RING, c * w:(c + 1) * w],
                                        start=(cc == 0 and b == 0), stop=(cc == C - 1 and b == 1))
                if u % 2 or u == 6:
                    ins.then_inc(s_ready, 1)
                else:
                    ins.then_inc(unit_used, 1)

            def turned(out, rows, after_wait):
                if after_wait:
                    return pe.matmul(out, rows, ident[0:QL, 0:QL], start=True, stop=True)
                return pe.transpose(out, rows, ident[0:QL, 0:QL])

            def turn_o(s, i=0):
                pe.wait_ge(o_norm, s + 1 + 2 * i)
                for c in range(C):
                    ins = turned(ps[:, 6, c * QL:(c + 1) * QL], O[:, c * P:(c + 1) * P], c == 0)
                ins.then_inc(ot_ready, 1)

            def step(s, i=0, loop=False, nxt=True):
                per = 2 * PER_BATCH if loop else 0
                k0 = U_KEYS0 + 7 + PER_BATCH * s
                if nxt:
                    score_block(s + 1, 0, i, per)
                    score_block(s + 1, 1, i, per)
                if s > 0:
                    turn_o(s - 1, i)
                if nxt:
                    for u in range(2, 7):
                        score_block(s + 1, u, i, per)
                pe.wait_ge(p_ready, s + 1 + 2 * i)
                for kc in range(NCH):
                    a = kc * P if kc < 13 else KV
                    n = P if kc < 12 else (KREM if kc == 12 else QL)
                    ins = turned(ps[0:n, 4 + kc // 8, (kc % 8) * QL:(kc % 8 + 1) * QL],
                                 S[0:QL, s % 2, a:a + n], kc == 0)
                    if kc in (7, NCH - 1):
                        ins.then_inc(pt_ready, 1)
                for u in range(7):
                    k = k0 + u + (7 if nxt else 0)
                    if u == 0:
                        pe.wait_ge(pt_split, 2 * s + 1 + 4 * i)
                        if s > 0:
                            pe.wait_ge(o_evac, s + 2 * i)
                            pe.wait_ge(ot_split, s + 2 * i)
                    if u == 4:
                        pe.wait_ge(pt_split, 2 * s + 2 + 4 * i)
                    unit_ready(k, per, i)
                    for j in range(2):
                        kc = 2 * u + j
                        n = P if kc < 12 else (KREM if kc == 12 else QL)
                        for h in range(2):
                            at = slice(j * D + h * HALF, j * D + (h + 1) * HALF)
                            for b, buf in enumerate((hi, lo)):
                                ins = pe.matmul(ps[:, 6 + h, :], pt[0:n, kc, :], buf[0:n, k % RING, at],
                                                start=(kc == 0 and b == 0), stop=(kc == NCH - 1 and b == 1))
                    if u == 6:
                        ins.then_inc(o_ready, 1)
                    else:
                        ins.then_inc(unit_used, 1)

            for u in range(7):
                score_block(0, u)
            step(0)
            with pe.Fori(0, 3) as i:
                step(1, i, True)
                step(2, i, True)
            step(7, nxt=False)
            turn_o(7)
            pe.wait_ge(ot_split, B)

            projection(U_WO, O_WO)
            norm(1, O_LN2)
            with pe.Fori(0, 3) as i:
                projection(U_QKV, O_QKV, 2, RING, i, 8)

            pe.wait_ge(evacuated, O_QKV + 24)

            def heads_front(t):
                for w in range(2):
                    for c in range(C):
                        ins = pe.transpose(ps[:, 2 * w + c // 4, (c % 4) * P:(c % 4 + 1) * P],
                                           qk[:, t, w * D + c * P:w * D + (c + 1) * P], ident)
                    ins.then_inc(tq_ready, 1)
                pe.wait_ge(tq_evac, 2 * t + 2)
                if t >= 1:
                    pe.wait_ge(hs_used, t)
                for r in range(2):
                    for c in range(C):
                        for b in range(2):
                            ins = pe.matmul(ps[b * QL:(b + 1) * QL, 4 + r, c * DH:(c + 1) * DH],
                                            qkt[r * DH:(r + 1) * DH, c, b * QL:(b + 1) * QL],
                                            qkt[r * DH:(r + 1) * DH, C + c, b * QL:(b + 1) * QL],
                                            start=True, stop=True)
                ins.then_inc(hs_ready, 1)

            def heads_back(t):
                pe.wait_ge(hp_ready, t + 1)
                for j in range(H):
                    ins = pe.transpose(ps[0:DH, j // 4, (j % 4) * P:(j % 4 + 1) * P],
                                       sc[:, t % 2, j * DH:(j + 1) * DH], ident)
                ins.then_inc(hpt_ready, 1)
                pe.wait_ge(hpt_evac, 2 * (t + 1))
                if t >= 1:
                    pe.wait_ge(ho_split, t)
                for c in range(C):
                    for b in range(2):
                        for r in range(2):
                            h = 2 * c + r
                            ins = pe.matmul(ps[r * DH:(r + 1) * DH, 6 + b, c * QL:(c + 1) * QL],
                                            v[b * QL:(b + 1) * QL, t, h * DH:(h + 1) * DH],
                                            pth[b * QL:(b + 1) * QL, r * C + c, :], start=True, stop=True)
                ins.then_inc(ho_ready, 1)

            heads_front(0)
            for t in range(TT):
                if t + 1 < TT:
                    heads_front(t + 1)
                heads_back(t)
            pe.wait_ge(ho_split, TT)
            projection(U_WOUT, O_WOUT)
            norm(2, O_LN3)

            pe.wait_ge(wr_split, 1)
            for t in range(TT):
                for c in range(C):
                    ins = three(ps[:, 0, t * NE:(t + 1) * NE], act_hi[:, c, t * P:(t + 1) * P],
                                act_lo[:, c, t * P:(t + 1) * P], wr_hi[:, c, :], wr_lo[:, c, :], c == 0, c == C - 1)
            ins.then_inc(logits_ready, 1)

            pe.wait_ge(member_ready, 1)
            pe.wait_ge(count_loaded, 16)
            for t in range(TT + 1):
                for u in range(min(t + 1, TT)):
                    ins = pe.matmul(ps[:, 1, t * NE:(t + 1) * NE], earlier if u == t else ones,
                                    small[:, 0, u * NE:(u + 1) * NE], start=(u == 0), stop=(u == min(t, TT - 1)))
            ins.then_inc(rank_ready, 1)

            def gather(e):
                for c in range(C):
                    if c == 0:
                        pe.wait_ge(sel_built, TT * e + TT)
                    if c >= 4:
                        pe.wait_ge(xg_done, C * e + (c - 3))
                    for h, src in enumerate((x_tok_hi, x_tok_lo)):
                        for t in range(TT):
                            ins = pe.matmul(ps[:, 2 + c % 4, h * CAP:(h + 1) * CAP], src[:, t, c * P:(c + 1) * P],
                                            sel[:, t, :], start=(t == 0), stop=(t == TT - 1))
                    ins.then_inc(xg_ready, 1)

            def item(e, u0, first, more):
                if first:
                    pe.wait_ge(sc_done, 8 * e + 1)
                    gather(e)
                for n in range(NT):
                    for t in range(TT):
                        ins = pe.matmul(ps[:, 6 + n, t * P:(t + 1) * P], sel[:, t, n * P:(n + 1) * P], ident_r[:, :],
                                        start=True, stop=True)
                    ins.then_inc(selt_ready, 1)
                pe.wait_ge(xg_done, C * e + C)
                for f in range(8):
                    k = u0 + f
                    unit_ready(k, PER_EXPERT, e)
                    if f >= 2:
                        pe.wait_ge(h_split, 8 * e + (f - 1))
                    elif f == 0:
                        pe.wait_ge(sc_done, 8 * e + 1)
                    for j in range(2):
                        for c in range(C):
                            at = slice(j * D + c * P, j * D + (c + 1) * P)
                            ins = three(ps[:, f % 2, j * CAP:(j + 1) * CAP], hi[:, k % RING, at], lo[:, k % RING, at],
                                        xg[:, c, 0:CAP], xg[:, c, CAP:2 * CAP], c == 0, c == C - 1)
                    ins.then_inc(gu_ready, 1)
                if more:
                    gather(e + 1)
                for g in range(2):
                    for half in range(2):
                        k = u0 + 8 + 2 * g + half
                        if g == 0:
                            pe.wait_ge(h_split, 8 * e + 4 * (half + 1))
                            if half == 0:
                                pe.wait_ge(selt_done, NT * e + NT)
                        elif half == 0 and more:
                            pe.wait_ge(xg_done, C * e + 2 * C)
                        unit_ready(k, PER_EXPERT, e)
                        for n in range(NT):
                            for c in range(4):
                                cc = 4 * half + c
                                rows = slice(n * P, (n + 1) * P)
                                cols = slice(c * HALF, (c + 1) * HALF)
                                ins = three(ps[:, Y_BANK[g] + n, :], h_hi[:, cc, rows], h_lo[:, cc, rows],
                                            hi[:, k % RING, cols], lo[:, k % RING, cols], cc == 0, cc == C - 1)
                            if half == 1:
                                ins.then_inc(y_ready, 1)
                        if half == 0:
                            ins.then_inc(unit_used, 1)
                for g in range(2):
                    pe.wait_ge(y_split, 4 * e + (2 * g + 2))
                    for t in range(TT):
                        if g == 1:
                            pe.wait_ge(sc_done, 8 * e + (t + 2))
                        for n in range(NT):
                            for h in range(2):
                                ins = pe.matmul(ps[:, SC_BANK[t], :], selt[:, n, t * P:(t + 1) * P],
                                                y[:, h, n, g * HALF:(g + 1) * HALF],
                                                start=(n == 0 and h == 0), stop=(n == NT - 1 and h == 1))
                        ins.then_inc(sc_ready, 1)

            pe.wait_ge(x_tok_split, TT)
            pe.wait_ge(ident_r_set, 1)
            gather(0)
            with pe.Fori(0, NE - 1) as e:
                item(e, U_FFN, False, True)
            item(NE - 1, U_FFN, False, False)
            pe.wait_ge(meta_ready, 1)
            more = pe.value_load(meta[0:1, 0:1], min_val=0, max_val=NE)
            with pe.If(more > 0):
                with pe.Fori(0, more) as j:
                    item(j + NE, U_FFN, True, False)


def kernel(**inputs):
    import numpy as np
    import concourse.bacc as _bacc
    from concourse.bass_utils import run_bass_kernel_spmd as _run

    g = {k: np.asarray(v) for k, v in inputs.items()}

    def stationary(w):
        return w.reshape(C, P, -1, P).transpose(2, 1, 0, 3).reshape(-1, P, D)

    def pairs(a, b):
        return np.stack([a, b], axis=2).reshape(-1, P, UNIT)

    def moving(w):
        return w.reshape(2, 4, P, -1, HALF).transpose(3, 0, 2, 1, 4).reshape(-1, P, UNIT)

    wq, wk = stationary(g["L0_xattn_wq"].T), stationary(g["L0_xattn_wk"].T)
    qkv = g["L0_attn_w_qkv"].reshape(4, 3, D // 4, D)
    units = [pairs(wq[0::2], wq[1::2]), pairs(wk[0::2], wk[1::2]), moving(g["L0_xattn_wv"].T),
             moving(g["L0_xattn_wo"].T)]
    units += [moving(qkv[:, n].reshape(D, D).T) for n in (0, 2, 1)]
    units.append(moving(g["L0_attn_w_out"].T))
    for e in range(NE):
        units.append(pairs(stationary(g["L0_ffn_Wg"][e]), stationary(g["L0_ffn_Wu"][e])))
        units.append(moving(g["L0_ffn_Wd"][e]))
    weights = np.concatenate(units)
    context = g["ctx_2048"]
    keys = context[:, :KFULL].reshape(B, 3, HALF, 2, 4, P).transpose(0, 1, 3, 5, 4, 2).reshape(B, 6, P, UNIT)
    tail = context[:, KFULL - 1:].reshape(B, KTAIL, C, P).transpose(0, 3, 2, 1)

    pos = np.arange(P, dtype=np.float32) % QL
    inv = (1.0 / 10000.0 ** (np.arange(0, DH, 2, dtype=np.float32) / DH)).astype(np.float32)
    ang = pos[:, None] * inv[None, :]
    rope = np.zeros((P, ROPE), np.float32)
    rope[:, 0:DH] = np.repeat(np.cos(ang), 2, axis=1)
    rope[:, DH:2 * DH:2] = -np.sin(ang)
    rope[:, DH + 1:2 * DH:2] = np.sin(ang)
    rope[:, 2 * DH:3 * DH] = np.where(np.arange(QL)[None, :] > pos[:, None], -3.0e38, 0.0)
    route = np.zeros((P, ROUTE), np.float32)
    route[:, 0:CAP] = np.arange(CAP)
    route[:, CAP:] = np.arange(NE)
    count = np.ones((P, 2 * P), np.float32)
    count[:, 0:P] = np.arange(P)[:, None] < np.arange(P)[None, :]

    arrays = {
        "x_in": g["x"].reshape(TOK, D),
        "context": context,
        "keys": keys,
        "key_tail": tail,
        "weights": weights,
        "router": g["L0_ffn_Wr"].reshape(C, P, NE).transpose(1, 0, 2),
        "temperature": np.broadcast_to(g["L0_ffn_temperature"].reshape(1, 1), (P, 1)),
        "identity": np.eye(P, dtype=np.float32),
        "rope": rope,
        "route": route,
        "count": count,
    }
    arrays = {k: np.ascontiguousarray(v) for k, v in arrays.items()}
    nc = _bacc.Bacc("TRN2", target_bir_lowering=False, num_devices=1)
    args = [nc.dram_tensor(k, v.shape, F32, kind="ExternalInput").ap() for k, v in arrays.items()]
    out = nc.dram_tensor("out", (TOK, D), F32, kind="ExternalOutput").ap()
    perceiver_block(nc, *args, out)
    r = _run(nc, [arrays], core_ids=[0])
    return r.results[0]["out"].reshape(B, QL, D)
```

```python
import concourse.bass as bass
from concourse import mybir
from contextlib import ExitStack

F32 = mybir.dt.float32
F32R = mybir.dt.float32r
ALU = mybir.AluOpType
ACT = mybir.ActivationFunctionType
AX = mybir.AxisListType

P = 128
B, QL, D, KV = 8, 64, 1024, 1601
C = D // P
TOK = B * QL
TT = TOK // P
H, DH = 16, 64
NE, F = 8, 1024
HALF = 512
UNIT = 2048
RING = 4
AHEAD = RING - 1
KFULL = 3 * HALF
KREM = KV - KFULL
KTAIL = KREM + 1
KEYS = KV + QL
NCH = 14
EPS = 1e-5

U_Q, U_K, U_V = 0, 4, 8
U_KEYS0 = 12
PER_BATCH = 14
U_WO = U_KEYS0 + B * PER_BATCH
U_QKV = U_WO + 4
U_WOUT = U_QKV + 12
U_FFN = U_WOUT + 4
PER_EXPERT = 12
W_FFN = U_FFN - B * PER_BATCH
O_LN1 = 0
O_QK = O_LN1 + 8
O_V = O_QK + 16
O_WO = O_V + 8
O_LN2 = O_WO + 8
O_QKV = O_LN2 + 8
O_WOUT = O_QKV + 24
O_LN3 = O_WOUT + 8
O_FFN = O_LN3 + 8

CAP = 256
NT = CAP // P
TPH = TT // NT
HTOK = TOK // NT
ITEMS = 2 * NE
assert NT * P == CAP and 2 * P >= HTOK

ROPE = 3 * DH
ROUTE = NT * CAP + NE + NE * NE
NO_PLACE = -1000.0
SCALE = 1.0 / 32.0
HEAD_SCALE = 0.125
CENTER = 0.36787944117144233
LOWER = 0.21231792754821915
UPPER = 0.5


def released():
    silent, table = 0, []

    def unit(sem, value):
        nonlocal silent
        if sem is None:
            silent += 1
            sem, value = "unit_used", silent
        table.append((sem, value))

    def projection(base, groups):
        for g in range(groups):
            unit(None, 0)
            unit("out_ready", base + 4 * (g + 1))

    for k in range(8):
        unit("out_ready", O_QK + 2 * (k + 1))
    projection(O_V, 2)
    for s in range(B + 1):
        if s < B:
            for u in range(7):
                unit(*(("s_ready", 4 * s + (u + 1) // 2 + (u == 6)) if u % 2 or u == 6 else (None, 0)))
        if s > 0:
            for u in range(7):
                unit(*(("o_ready", s) if u == 6 else (None, 0)))
    projection(O_WO, 2)
    projection(O_QKV, 6)
    projection(O_WOUT, 2)
    for e in range(NE):
        for f in range(8):
            unit("gu_ready", 8 * e + f + 1)
        for g in range(2):
            unit(None, 0)
            unit("y_ready", 4 * e + 2 * (g + 1))
    return table


class Steps:

    def __init__(self, engine, sem):
        self.engine, self.sem, self.n, self.k, self.i, self.per = engine, sem, 0, 0, 0, 0

    def done(self, ins):
        ins.then_inc(self.sem, 1)
        self.k += 1

    def wait(self):
        self.engine.wait_ge(self.sem, self.n + self.k + self.per * self.i)

    def loop(self, i, per):
        self.n, self.k, self.i, self.per = self.n + self.k, 0, i, per

    def end(self, turns):
        assert self.k == self.per, (self.k, self.per)
        self.n, self.k, self.i, self.per = self.n + self.per * turns, 0, 0, 0


def perceiver_block(nc, x_d, ctx_d, keys_d, tail_d, w_d, wr_d, temp_d, ident_d, rope_d, route_d, count_d, out_d):
    with ExitStack() as ctx:
        def sb(name, shape, dt=F32):
            return ctx.enter_context(nc.sbuf_tensor(name, shape, dt))

        def sem(name):
            return ctx.enter_context(nc.semaphore(name))

        new_k_d = nc.dram_tensor("new_keys_t", (P, C, TOK), F32).ap()
        x_mid_d = nc.dram_tensor("x_mid", (P, TT * D), F32).ap()
        new_v_d = nc.dram_tensor("new_values", (TOK, D), F32).ap()

        ps = ctx.enter_context(nc.psum_tensor("ps", [P, 8, HALF], F32))
        raw = sb("raw", [P, RING, UNIT])
        hi = sb("hi", [P, RING, UNIT], F32R)
        lo = sb("lo", [P, RING, UNIT], F32R)
        xq = sb("xq", [P, (B + 1) * C * QL])
        act_hi = sb("act_hi", [P, C, TOK], F32R)
        act_lo = sb("act_lo", [P, C, TOK], F32R)
        ident = sb("ident", [P, P])
        ident_r = sb("ident_r", [P, P], F32R)
        ident = ident[:, :]
        wr_hi = sb("wr_hi", [P, C, NE], F32R)
        wr_lo = sb("wr_lo", [P, C, NE], F32R)
        eps = sb("eps", [P, 1])
        stats = sb("stats", [P, TT, 2, 6])
        mv = sb("mv", [P, TT, 2])
        std = sb("std", [P, TT])
        rstd = sb("rstd", [P, TT])
        small = sb("small", [P, 15, TT * NE])
        item_w = sb("item_w", [P, TT, ITEMS])
        item_slot = sb("item_slot", [P, TT, ITEMS])
        meta = sb("meta", [P, 1 + NE], mybir.dt.int32)
        x = xq[:, 0:TT * D].rearrange("p (t d) -> p t d", t=TT)
        q = xq[:, :].rearrange("p (b c n) -> p b c n", b=B + 1, c=C)

        x_loaded = [sem(f"x_loaded{t}") for t in range(TT)]
        x_reloaded = sem("x_reloaded")
        x_mid_stored = sem("x_mid_stored")
        x_mid_loaded = sem("x_mid_loaded")
        ident_loaded = sem("ident_loaded")
        router_loaded = sem("router_loaded")
        temp_loaded = sem("temp_loaded")
        landed = [sem(f"landed{s}") for s in range(RING)]
        new_landed = sem("new_landed")
        hi_done = sem("hi_done")
        lo_done = sem("lo_done")
        unit_used = sem("unit_used")
        out_ready = sem("out_ready")
        evacuated = sem("evacuated")
        dve_step = sem("dve_step")
        eps_set = sem("eps_set")
        stats_ready = sem("stats_ready")
        std_ready = sem("std_ready")
        xn_ready = sem("xn_ready")
        ln_hi = sem("ln_hi")
        kv_stored = [sem(f"kv_stored{s}") for s in range(2)]
        q_hi_done = sem("q_hi_done")
        q_split = sem("q_split")
        s_ready = sem("s_ready")
        lorow_ready = sem("lorow_ready")
        s_evac = sem("s_evac")
        negmax_ready = sem("negmax_ready")
        p_ready = sem("p_ready")
        pt_ready = sem("pt_ready")
        pt_hi_done = sem("pt_hi_done")
        pt_split = sem("pt_split")
        o_ready = sem("o_ready")
        olo_ready = sem("olo_ready")
        o_evac = sem("o_evac")
        o_norm = sem("o_norm")
        ot_ready = sem("ot_ready")
        ot_hi_done = sem("ot_hi_done")
        ot_split = sem("ot_split")
        tq_ready = sem("tq_ready")
        tq_evac = sem("tq_evac")
        hs_ready = sem("hs_ready")
        hs_used = sem("hs_used")
        hs_shifted = sem("hs_shifted")
        hs_exp = sem("hs_exp")
        hp_ready = sem("hp_ready")
        hpt_ready = sem("hpt_ready")
        hpt_evac = sem("hpt_evac")
        ho_ready = sem("ho_ready")
        ho_hi = sem("ho_hi")
        ho_split = sem("ho_split")
        wr_hi_done = sem("wr_hi_done")
        wr_split = sem("wr_split")
        logits_ready = sem("logits_ready")
        logits_out = sem("logits_out")
        logits_turned = sem("logits_turned")
        z_ready = sem("z_ready")
        ez_ready = sem("ez_ready")
        dist_ready = sem("dist_ready")
        edist_ready = sem("edist_ready")
        silu_done = sem("silu_done")
        ident_r_set = sem("ident_r_set")
        rope_loaded = sem("rope_loaded")
        route_loaded = sem("route_loaded")
        count_loaded = sem("count_loaded")
        member_ready = sem("member_ready")
        rank_ready = sem("rank_ready")
        counts_ready = sem("counts_ready")
        x_tok_hi_done = sem("x_tok_hi_done")
        x_tok_split = sem("x_tok_split")
        sel_built = sem("sel_built")
        selt_ready = sem("selt_ready")
        selt_done = sem("selt_done")
        xg_ready = sem("xg_ready")
        xg_done = sem("xg_done")
        gu_ready = sem("gu_ready")
        h_split = sem("h_split")
        y_ready = sem("y_ready")
        y_hi_done = sem("y_hi_done")
        y_split = sem("y_split")
        sc_ready = sem("sc_ready")
        sc_done = sem("sc_done")
        meta_ready = sem("meta_ready")
        out_stored = [sem(f"out_stored{t}") for t in range(TT + 1)]

        with ExitStack() as phase:
            def pb(name, shape, dt=F32):
                return phase.enter_context(nc.sbuf_tensor(name, shape, dt))

            qs = pb("qs", [P, 2, C, P], F32R)
            pt = pb("pt", [P, NCH, P], F32R)
            S = pb("scores", [P, 2, KEYS])
            lorow = pb("lorow", [QL, 2, HALF])
            olo = pb("olo", [QL, D])
            O = pb("attended", [QL, D])
            cols = pb("cols", [QL, 4, 2])
            mx, nb, sums, rinv = (cols[:, j, :] for j in range(4))
            kvs = pb("kvs", [P, 2, HALF])
            xn1 = S[:, :, 0:D]
            wr_raw = pb("wr_raw", [P, C, NE])
            temp = small[:, 14, 31:32]
        with ExitStack() as phase:
            qk = pb("qk", [P, TT, 2 * D])
            sc = pb("head_scores", [P, 2, D])
            qkt = pb("qkt", [P, 2 * C, P])
            pth = pb("pth", [P, H, QL])
            heads = pb("heads", [P, 3, H])
            rope_c = pb("rope_c", [P, ROPE])
            cos_t, sin_t, mask_t = (rope_c[:, j * DH:(j + 1) * DH] for j in range(3))
            hmx, hsum, hinv = (heads[:, j, :] for j in range(3))
            rope_a, rope_b = sc[:, 0, :].rearrange("p (s n) -> p s n", s=2), sc[:, 1, :].rearrange("p (s n) -> p s n", s=2)
            xn2 = sc[:, :, :]
        with ExitStack() as phase:
            x_tok_hi = pb("x_tok_hi", [P, TT, D], F32R)
            x_tok_lo = pb("x_tok_lo", [P, TT, D], F32R)
            h_hi = pb("h_hi", [P, C, CAP], F32R)
            h_lo = pb("h_lo", [P, C, CAP], F32R)
            sel = pb("sel", [P, TT, CAP], F32R)
            with nc.sbuf_tensor("count_c", [P, 2 * P], F32) as count_c:
                pass
            earlier, ones = count_c[:, 0:P], count_c[:, P:2 * P]
            selt = pb("selt", [P, NT, HTOK], F32R)
            route_c = pb("route_c", [P, ROUTE])
            places = route_c[:, 0:NT * CAP].rearrange("p (n a) -> p n a", n=NT)
            expert_ids = route_c[:, NT * CAP:NT * CAP + NE]
            earlier_expert = route_c[:, NT * CAP + NE:]
        logits_t = xq[0:NE, TT * D:TT * D + TOK]
        silu = xq[:, TT * D:TT * D + 2 * CAP].rearrange("p (s n) -> p s n", s=2)
        xg = act_hi
        y = act_lo[:, :, :].rearrange("p (h n a) b -> p h n (a b)", h=2, n=NT)

        def xn_rows(n, t):
            if n == 2 and t >= 2:
                return qkt[:, :, :].rearrange("p (s c) n -> p s (c n)", s=2)[:, t - 2, :]
            return (xn1 if n == 0 else xn2)[:, t % 2, :]

        v = x

        free = released()
        release = {"gu_ready": gu_ready, "y_ready": y_ready, "out_ready": out_ready, "unit_used": unit_used,
                   "s_ready": s_ready, "o_ready": o_ready}
        assert len(free) == U_FFN + NE * PER_EXPERT

        block = ctx.enter_context(nc.Block())

        @block.sync
        def _(sp):
            def load(k, src, per=0, i=0, dst=None):
                if k >= RING:
                    sp.wait_ge(lo_done, k - RING + 1 + per * i)
                sp.dma_start(raw[:, k % RING, :] if dst is None else dst, src).then_inc(landed[k % RING], 16)

            def load_keys(k, b, per=0, i=0, first=False):
                for u in range(6):
                    load(k + u, keys_d[b, u], per, i)
                view = raw[:, (k + 6) % RING, 0:C * (KTAIL + QL)].rearrange("p (c n) -> p c n", c=C)
                load(k + 6, tail_d[b], per, i, view[:, :, 0:KTAIL])
                if first:
                    for s in range(2):
                        sp.wait_ge(kv_stored[s], 16 * 8)
                sp.dma_start(view[:, :, KTAIL:], new_k_d[:, :, bass.ds(b * QL, QL)]).then_inc(new_landed, 16)

            def load_values(k, b, per=0, i=0):
                for u in range(6):
                    load(k + u, ctx_d[b, 2 * P * u:2 * P * (u + 1), :].rearrange("(j p) d -> p j d", p=P), per, i,
                         raw[:, (k + u) % RING, :].rearrange("p (j d) -> p j d", j=2))
                load(k + 6, ctx_d[b, KFULL:KV, :], per, i, raw[0:KREM, (k + 6) % RING, 0:D])
                sp.dma_start(raw[0:QL, (k + 6) % RING, D:2 * D],
                             new_v_d[bass.ds(b * QL, QL), :]).then_inc(new_landed, 16)

            for t in range(TT):
                sp.dma_start(x[:, t, :], x_d[t * P:(t + 1) * P, :]).then_inc(x_loaded[t], 16)
                if t == 0:
                    sp.dma_start(ident, ident_d).then_inc(ident_loaded, 16)
            for k in range(RING):
                load(k, w_d[k])
            sp.dma_start(wr_raw[:, :, :], wr_d).then_inc(router_loaded, 16)
            sp.dma_start(temp, temp_d).then_inc(temp_loaded, 16)
            with sp.Fori(0, 2) as i:
                for k in range(RING):
                    load(RING + k, w_d[4 * i + RING + k], RING, i)
            load_keys(U_KEYS0, 0, first=True)
            k0 = U_KEYS0 + 7
            load_keys(k0, 1)
            load_values(k0 + 7, 0)
            with sp.Fori(0, 3) as i:
                for s in range(2):
                    k = k0 + PER_BATCH * (1 + s)
                    load_keys(k, 2 * i + (s + 2), 2 * PER_BATCH, i)
                    load_values(k + 7, 2 * i + (s + 1), 2 * PER_BATCH, i)
            load_values(k0 + 7 * PER_BATCH, B - 1)
            with sp.Fori(0, (U_FFN + NE * PER_EXPERT - U_WO) // RING) as i:
                for k in range(RING):
                    load(U_WO + k, w_d[4 * i + (U_KEYS0 + k)], RING, i)
            sp.wait_ge(meta_ready, 1)
            more = sp.value_load(meta[0:1, 0:1], min_val=0, max_val=NE)
            with sp.If(more > 0):
                with sp.Fori(0, more) as j:
                    e = sp.value_load(meta[0:1, bass.ds(j + 1, 1)], min_val=0, max_val=NE - 1)
                    for k in range(PER_EXPERT):
                        load(U_FFN + NE * PER_EXPERT + k, w_d[PER_EXPERT * e + (W_FFN + k)], PER_EXPERT, j)
            out_t = out_d.rearrange("(t p) d -> p t d", p=P)
            sp.wait_ge(sc_done, 8 * more + (8 * NE + 1 - TT))
            sp.dma_start(out_t[:, :, 0:HALF], x[:, :, 0:HALF]).then_inc(out_stored[TT], 16)
            for t in range(TT):
                sp.wait_ge(sc_done, 8 * more + (8 * NE + 1 - TT + t + 1))
                sp.dma_start(out_t[:, t, HALF:], x[:, t, HALF:]).then_inc(out_stored[t], 16)
            for t in range(TT + 1):
                sp.wait_ge(out_stored[t], 16)

        @block.gpsimd
        def _(pool):
            for f in range(C):
                pool.wait_ge(evacuated, O_QK + C + f + 1)
                pool.dma_start(new_k_d[:, f, :], kvs[:, f % 2, :]).then_inc(kv_stored[f % 2], 16)
            for n in range(8):
                g, t = n // TT, n % TT
                pool.wait_ge(evacuated, O_V + n + 1)
                pool.dma_start(new_v_d[t * P:(t + 1) * P, g * HALF:(g + 1) * HALF],
                               kvs[:, n % 2, :]).then_inc(kv_stored[n % 2], 16)
            pool.wait_ge(q_split, B + 1)
            pool.wait_ge(o_ready, B)
            pool.dma_start(x[:, :, :], x_d.rearrange("(t p) d -> p t d", p=P)).then_inc(x_reloaded, 16)
            pool.wait_ge(ot_split, B)
            pool.dma_start(rope_c[:, :], rope_d).then_inc(rope_loaded, 16)
            pool.wait_ge(xn_ready, 2 * TT)
            pool.dma_start(x_mid_d, xq[:, 0:TT * D]).then_inc(x_mid_stored, 16)
            pool.wait_ge(ho_ready, TT)
            pool.wait_ge(x_mid_stored, 16)
            pool.dma_start(xq[:, 0:TT * D], x_mid_d).then_inc(x_mid_loaded, 16)
            pool.wait_ge(ho_split, TT)
            pool.dma_start(route_c[:, :], route_d).then_inc(route_loaded, 16)
            pool.dma_start(count_c[:, :], count_d).then_inc(count_loaded, 16)

        SC_BANK = (4, 5, 6, 7)
        Y_BANK = (6, 2)
        LN_BANK = (4, 0, 4)
        KEY_LAST, VALUE_LAST = "keys", "values"

        def part(buf, k, kind):
            if kind == KEY_LAST:
                return buf[:, k % RING, 0:C * (KTAIL + QL)]
            if kind == VALUE_LAST:
                return buf[0:KREM, k % RING, :]
            return buf[:, k % RING, :]

        def kind_of(pos):
            return {6: KEY_LAST, 13: VALUE_LAST}.get(pos % PER_BATCH)

        @block.scalar
        def _(act):
            def split(k, per=0, i=0, kind=None, used=None):
                act.wait_ge(landed[k % RING], 16 * (per // RING) * i + 16 * (k // RING + 1))
                if kind:
                    b2 = (k - U_KEYS0 - 6) // 7
                    act.wait_ge(new_landed, 16 * (b2 + 1) + 16 * (per // 7) * i)
                if used:
                    act.wait_ge(*used)
                elif k >= RING:
                    name, value = free[k - RING + per]
                    grows = free[k - RING + 2 * per][1] - value
                    act.wait_ge(release[name], grows * i + (value - grows) if per else value)
                act.activation(part(hi, k, kind), part(raw, k, kind), ACT.Copy).then_inc(hi_done, 1)

            def norm(n, base, after=lambda t: None):
                def rows_hi(t):
                    if n == 2:
                        act.wait_ge(xn_ready, TT * n + t + 1)
                        act.activation(x_tok_hi[:, t, :], xn_rows(n, t), ACT.Copy).then_inc(x_tok_hi_done, 1)

                for t in range(TT):
                    act.wait_ge(stats_ready, TT * n + t + 1)
                    act.activation(std[:, t:t + 1], mv[:, t, 1:2], ACT.Sqrt, bias=eps[:, 0:1]).then_inc(std_ready, 1)
                    if t in (1, 2):
                        rows_hi(t - 1)
                for j in range(2 * TT):
                    t, h = j // 2, j % 2
                    act.wait_ge(out_ready, base + j + 1)
                    act.activation(act_hi[:, 4 * h:4 * h + 4, t * P:(t + 1) * P],
                                   ps[:, LN_BANK[n] + j % 4, :].rearrange("p (c n) -> p c n", c=4),
                                   ACT.Copy).then_inc(ln_hi, 1)
                    if j in (1, 3):
                        rows_hi(2 + j // 2)
                    if h:
                        after(t)

            def first_units(t):
                if t > 0:
                    split(t - 1)

            act.wait_ge(eps_set, 1)
            norm(0, O_LN1, first_units)
            act.wait_ge(ident_loaded, 16)
            act.activation(ident_r[:, :], ident, ACT.Copy).then_inc(ident_r_set, 1)
            act.wait_ge(router_loaded, 16)
            act.activation(wr_hi[:, :, :], wr_raw[:, :, :], ACT.Copy).then_inc(wr_hi_done, 1)
            for k in range(U_Q, U_KEYS0):
                split(k + AHEAD)

            def q_hi(s, b, i=0):
                if s >= 2:
                    act.wait_ge(s_ready, 4 * (s - 1) + 8 * i)
                act.activation(qs[:, s % 2, :, 0:QL], q[:, b, :, :], ACT.Copy).then_inc(q_hi_done, 1)

            def score_rows(s, j, i=0):
                n = 4 * s + j
                w = HALF if j < 3 else KTAIL + QL
                act.wait_ge(s_ready, n + 1 + 8 * i)
                if n >= 2:
                    act.wait_ge(s_evac, n - 1 + 8 * i)
                act.activation(lorow[:, j % 2, 0:w], ps[QL:P, j, 0:w], ACT.Copy).then_inc(lorow_ready, 1)

            def exps(s, i=0):
                act.wait_ge(negmax_ready, s + 1 + 2 * i)
                act.activation(S[0:QL, s % 2, :], S[0:QL, s % 2, :], ACT.Exp, bias=nb[:, s % 2:s % 2 + 1], scale=SCALE,
                               accum_out=sums[:, s % 2:s % 2 + 1]).then_inc(p_ready, 1)

            def ot_hi(s, b, i=0):
                act.wait_ge(ot_ready, s + 1 + 2 * i)
                act.activation(act_hi[:, :, bass.ds(b * QL, QL)], ps[:, 6, :].rearrange("p (c n) -> p c n", c=C),
                               ACT.Copy).then_inc(ot_hi_done, 1)

            def step(s, i=0, loop=False, nxt=True):
                per = 2 * PER_BATCH if loop else 0
                k0 = U_KEYS0 + 7 + PER_BATCH * s
                for pos in range(0 if nxt else 7, PER_BATCH):
                    k = k0 + pos - (0 if nxt else 7)
                    if pos < PER_BATCH - 1 or nxt:
                        split(k + AHEAD, per, i, kind_of(pos + AHEAD) if nxt or pos + AHEAD < PER_BATCH else None)
                    if pos == 1:
                        score_rows(s + 1, 0, i)
                        if s > 0:
                            ot_hi(s - 1, 2 * i + (s - 1), i)
                    if pos in (3, 5):
                        score_rows(s + 1, pos // 2, i)
                    if pos == 6:
                        score_rows(s + 1, 3, i)
                    if pos == (4 if nxt else 7):
                        if not nxt:
                            ot_hi(s - 1, s - 1)
                        for h, (a, e) in enumerate(((0, 8), (8, NCH))):
                            act.wait_ge(pt_ready, 2 * s + h + 1 + 4 * i)
                            act.activation(pt[:, a:e, 0:QL],
                                           ps[:, 4 + h, 0:(e - a) * QL].rearrange("p (k n) -> p k n", n=QL),
                                           ACT.Copy).then_inc(pt_hi_done, 1)
                    if pos == 10 and nxt:
                        exps(s + 1, i)
                    if pos == 8 and nxt:
                        q_hi(s + 2, 2 * i + (s + 2), i)
                    if pos == 13:
                        act.wait_ge(o_ready, s + 1 + 2 * i)
                        act.activation(olo[:, :], ps[QL:P, 6:8, :].rearrange("p a n -> p (a n)"),
                                       ACT.Copy).then_inc(olo_ready, 1)
                if not nxt:
                    split(k + AHEAD)

            act.wait_ge(evacuated, O_QK + C)
            q_hi(0, 0)
            q_hi(1, 1)
            for pos in range(7):
                split(U_KEYS0 + pos + AHEAD, kind=KEY_LAST if pos + AHEAD == 6 else None)
                if pos in (1, 3, 5, 6):
                    score_rows(0, (pos + 1) // 2 - (pos < 6) if pos < 6 else 3)
            exps(0)
            step(0)
            with act.Fori(0, 3) as i:
                step(1, i, True)
                step(2, i, True)
            step(7, nxt=False)
            ot_hi(7, 7)

            for k in range(U_WO, U_QKV):
                split(k + AHEAD)
            norm(1, O_LN2)
            with act.Fori(0, 3) as i:
                for k in range(RING):
                    split(U_QKV + k + AHEAD, RING, i)

            def heads_t(t):
                for w in range(2):
                    act.wait_ge(tq_ready, 2 * t + w + 1)
                    act.activation(qkt[:, C * w:C * (w + 1), :].rearrange("p c n -> p (c n)"),
                                   ps[:, 2 * w:2 * w + 2, :].rearrange("p a n -> p (a n)"),
                                   ACT.Copy).then_inc(tq_evac, 1)

            def heads_exp(t):
                act.wait_ge(hs_shifted, t + 1)
                act.activation(sc[:, t % 2, :], sc[:, t % 2, :], ACT.Exp).then_inc(hs_exp, 1)

            act.activation(small[:, 14, 30:31], eps[:, :], ACT.Exp)
            heads_t(0)
            heads_t(1)
            heads_exp(0)
            for t in range(TT):
                act.wait_ge(hpt_ready, t + 1)
                for a in range(2):
                    for b in range(2):
                        heads_a = pth[b * QL:(b + 1) * QL, :, :].rearrange("p (m a) n -> p m a n", a=2)[:, :, a, :]
                        act.activation(heads_a, ps[a * QL:(a + 1) * QL, 0:2, :].rearrange("p k (j n) -> p (k j) n", n=P)
                                       [:, :, b * QL:(b + 1) * QL], ACT.Copy).then_inc(hpt_evac, 1)
                if t + 1 < TT:
                    heads_exp(t + 1)
                act.wait_ge(ho_ready, t + 1)
                act.activation(act_hi[:, :, t * P:(t + 1) * P].rearrange("p c (b n) -> p b c n", b=2),
                               ps[:, 6:8, :].rearrange("p b (c n) -> p b c n", c=C), ACT.Copy).then_inc(ho_hi, 1)
                if t + 2 < TT:
                    heads_t(t + 2)

            for k in range(U_WOUT, U_FFN):
                split(k + AHEAD)
            norm(2, O_LN3)

            act.activation(small[:, 14, 29:30], eps[:, :], ACT.Exp)
            act.wait_ge(logits_ready, 1)
            act.activation(logits_t, ps[0:NE, 0, 0:TOK], ACT.Copy).then_inc(logits_out, 1)
            act.wait_ge(z_ready, 1)
            act.activation(small[:, 1, :], small[:, 0, :], ACT.Exp, scale=-1.0).then_inc(ez_ready, 1)
            act.wait_ge(dist_ready, 1)
            act.activation(small[:, 5, :], small[:, 4, :], ACT.Exp, scale=-1.0 / 0.1).then_inc(edist_ready, 1)
            act.activation(small[:, 6, :], small[:, 4, :], ACT.Exp, scale=-1.0 / 0.3).then_inc(edist_ready, 1)

            def gathered(e):
                for c in range(C):
                    act.wait_ge(xg_ready, C * e + (c + 1))
                    act.activation(xg[:, c, :], ps[:, 2 + c % 4, :], ACT.Copy).then_inc(xg_done, 1)

            def item(e, u0, first, more):
                if first:
                    for k in range(AHEAD):
                        split(u0 + k, PER_EXPERT, e)
                    gathered(e)
                for k in range(PER_EXPERT):
                    if more or k + AHEAD < PER_EXPERT:
                        split(u0 + k + AHEAD, PER_EXPERT, e, used=(gu_ready, 8 * e + 1) if k == 0 else None)
                    if k < 8:
                        act.wait_ge(gu_ready, 8 * e + (k + 1))
                        act.activation(silu[:, k % 2, :], ps[:, k % 2, 0:CAP], ACT.Silu).then_inc(silu_done, 1)
                    if k == 1:
                        for n in range(NT):
                            act.wait_ge(selt_ready, NT * e + (n + 1))
                            act.activation(selt[:, n, :], ps[:, 6 + n, 0:HTOK], ACT.Copy).then_inc(selt_done, 1)
                    if k == 7 and more:
                        gathered(e + 1)
                    if k in (9, 11):
                        g = (k - 9) // 2
                        for n in range(NT):
                            act.wait_ge(y_ready, 4 * e + (2 * g + n + 1))
                            act.activation(y[:, 0, n, g * HALF:(g + 1) * HALF], ps[:, Y_BANK[g] + n, :],
                                           ACT.Copy).then_inc(y_hi_done, 1)

            gathered(0)
            with act.Fori(0, NE - 1) as e:
                item(e, U_FFN, False, True)
            item(NE - 1, U_FFN, False, False)
            act.wait_ge(meta_ready, 1)
            more = act.value_load(meta[0:1, 0:1], min_val=0, max_val=NE)
            with act.If(more > 0):
                with act.Fori(0, more) as j:
                    item(j + NE, U_FFN, True, False)

        @block.vector
        def _(dve):
            steps = Steps(dve, dve_step)

            def split(k, per=0, i=0, kind=None):
                dve.wait_ge(hi_done, k + 1 + per * i)
                dve.tensor_tensor(part(lo, k, kind), part(raw, k, kind), part(hi, k, kind),
                                  ALU.subtract).then_inc(lo_done, 1)

            def tok_lo(t):
                dve.wait_ge(x_tok_hi_done, t + 1)
                dve.tensor_tensor(x_tok_lo[:, t, :], xn_rows(2, t), x_tok_hi[:, t, :],
                                  ALU.subtract).then_inc(x_tok_split, 1)

            def norm(n, base, rows, after=lambda t: None):
                def normalise(t):
                    dve.wait_ge(std_ready, TT * n + t + 1)
                    steps.done(dve.reciprocal(rstd[:, t:t + 1], std[:, t:t + 1]))
                    steps.wait()
                    if t >= 2 and n < 2:
                        dve.wait_ge(out_ready, base + 2 * (t - 2) + 2)
                    dve.tensor_scalar(xn_rows(n, t), x[:, t, :], mv[:, t, 0:1], rstd[:, t:t + 1],
                                      ALU.subtract, ALU.mult).then_inc(xn_ready, 1)

                def transposed_lo(t):
                    for h in range(2):
                        j = 2 * t + h
                        to = (slice(None), slice(4 * h, 4 * h + 4), slice(t * P, (t + 1) * P))
                        dve.wait_ge(ln_hi, 2 * TT * n + j + 1)
                        dve.tensor_tensor(act_lo[to], ps[:, LN_BANK[n] + j % 4, :].rearrange("p (c n) -> p c n", c=4),
                                          act_hi[to], ALU.subtract).then_inc(evacuated, 1)

                for t in range(TT):
                    rows(t)
                    for h in range(2):
                        steps.done(dve.bn_stats(stats[:, t, h, :], x[:, t, h * HALF:(h + 1) * HALF]))
                    steps.wait()
                    dve.bn_aggr(mv[:, t, :], stats[:, t, :, :].rearrange("p h n -> p (h n)")).then_inc(stats_ready, 1)
                    if t in (1, 2) or (n == 2 and t == 3):
                        normalise(t - 1)
                if n == 2:
                    normalise(3)
                for t in range(TT):
                    transposed_lo(t)
                    if n < 2 and t < 2:
                        normalise(2 + t)
                    after(t)
                if n == 2:
                    for t in range(TT):
                        tok_lo(t)

            dve.memset(eps[:, :], EPS).then_inc(eps_set, 1)
            def first_units(t):
                if t > 0:
                    split(t - 1)

            norm(0, O_LN1, lambda t: dve.wait_ge(x_loaded[t], 16), first_units)
            dve.wait_ge(wr_hi_done, 1)
            dve.tensor_tensor(wr_lo[:, :, :], wr_raw[:, :, :], wr_hi[:, :, :], ALU.subtract).then_inc(wr_split, 1)
            dve.wait_ge(xn_ready, TT)
            dve.memset(q[:, B, :, :], 0.0)
            for k in range(U_Q, U_V):
                split(k + AHEAD)
                for j in range(2):
                    f = 2 * k + j
                    dve.wait_ge(out_ready, O_QK + f + 1)
                    if f < C:
                        dve.tensor_copy(q[:, 0:B, f, :], ps[:, f % 4, :].rearrange("p (b n) -> p b n", b=B))\
                           .then_inc(evacuated, 1)
                    else:
                        if f >= C + 2:
                            dve.wait_ge(kv_stored[f % 2], 16 * ((f - C) // 2))
                        dve.tensor_copy(kvs[:, f % 2, :], ps[:, f % 4, :]).then_inc(evacuated, 1)
            for k in range(U_V, U_KEYS0):
                split(k + AHEAD)
                g, half = (k - U_V) // 2, (k - U_V) % 2
                if half:
                    for t in range(TT):
                        n = g * TT + t
                        dve.wait_ge(out_ready, O_V + n + 1)
                        dve.wait_ge(kv_stored[n % 2], 16 * (4 + n // 2))
                        dve.tensor_copy(kvs[:, n % 2, :], ps[:, 4 * (1 - g) + t, :]).then_inc(evacuated, 1)

            def q_lo(s, b, i=0):
                dve.wait_ge(q_hi_done, s + 1 + 2 * i)
                dve.tensor_tensor(qs[:, s % 2, :, QL:P], q[:, b, :, :], qs[:, s % 2, :, 0:QL],
                                  ALU.subtract).then_inc(q_split, 1)

            def score_add(s, j, i=0):
                n = 4 * s + j
                w = HALF if j < 3 else KTAIL + QL
                at = j * HALF if j < 3 else KFULL - 1
                dve.wait_ge(lorow_ready, n + 1 + 8 * i)
                if j == 3:
                    dve.wait_ge(s_evac, n + 8 * i)
                dve.tensor_tensor(S[0:QL, s % 2, at:at + w], ps[0:QL, j, 0:w], lorow[:, j % 2, 0:w],
                                  ALU.add).then_inc(s_evac, 1)

            def row_max(s, i=0):
                dve.wait_ge(s_evac, 4 * s + 4 + 8 * i)
                steps.done(dve.tensor_reduce(mx[:, s % 2:s % 2 + 1], S[0:QL, s % 2, :], AX.X, ALU.max))
                steps.wait()
                dve.tensor_scalar(nb[:, s % 2:s % 2 + 1], mx[:, s % 2:s % 2 + 1], -SCALE, None,
                                  ALU.mult).then_inc(negmax_ready, 1)

            def ot_lo(s, b, i=0):
                dve.wait_ge(ot_hi_done, s + 1 + 2 * i)
                dve.tensor_tensor(act_lo[:, :, bass.ds(b * QL, QL)], ps[:, 6, :].rearrange("p (c n) -> p c n", c=C),
                                  act_hi[:, :, bass.ds(b * QL, QL)], ALU.subtract).then_inc(ot_split, 1)

            def step(s, i=0, loop=False, nxt=True):
                per = 2 * PER_BATCH if loop else 0
                k0 = U_KEYS0 + 7 + PER_BATCH * s
                for pos in range(0 if nxt else 7, PER_BATCH):
                    k = k0 + pos - (0 if nxt else 7)
                    if pos < PER_BATCH - 1 or nxt:
                        split(k + AHEAD, per, i, kind_of(pos + AHEAD) if nxt or pos + AHEAD < PER_BATCH else None)
                    if pos == 1:
                        score_add(s + 1, 0, i)
                        if s > 0:
                            ot_lo(s - 1, 2 * i + (s - 1), i)
                    if pos in (3, 5):
                        score_add(s + 1, pos // 2, i)
                    if pos == 6:
                        score_add(s + 1, 3, i)
                    if pos == (4 if nxt else 7):
                        if not nxt:
                            ot_lo(s - 1, s - 1)
                        for h, (a, e) in enumerate(((0, 8), (8, NCH))):
                            dve.wait_ge(pt_hi_done, 2 * s + h + 1 + 4 * i)
                            dve.tensor_tensor(pt[:, a:e, QL:P],
                                              ps[:, 4 + h, 0:(e - a) * QL].rearrange("p (k n) -> p k n", n=QL),
                                              pt[:, a:e, 0:QL], ALU.subtract).then_inc(pt_split, 1)
                    if pos == 8 and nxt:
                        row_max(s + 1, i)
                    if pos == 8 and nxt:
                        q_lo(s + 2, 2 * i + (s + 2), i)
                    if pos == 13:
                        dve.wait_ge(olo_ready, s + 1 + 2 * i)
                        dve.tensor_tensor(O[:, :], ps[0:QL, 6:8, :].rearrange("p a n -> p (a n)"), olo[:, :],
                                          ALU.add).then_inc(o_evac, 1)
                        steps.done(dve.reciprocal(rinv[:, s % 2:s % 2 + 1], sums[:, s % 2:s % 2 + 1]))
                        dve.wait_ge(o_evac, s + 1 + 2 * i)
                        steps.wait()
                        dve.tensor_scalar(O[:, :], O[:, :], rinv[:, s % 2:s % 2 + 1], None,
                                          ALU.mult).then_inc(o_norm, 1)
                if not nxt:
                    split(k + AHEAD)

            q_lo(0, 0)
            q_lo(1, 1)
            for pos in range(7):
                split(U_KEYS0 + pos + AHEAD, kind=KEY_LAST if pos + AHEAD == 6 else None)
                if pos in (1, 3, 5):
                    score_add(0, pos // 2)
                if pos == 6:
                    score_add(0, 3)
            row_max(0)
            step(0)
            with dve.Fori(0, 3) as i:
                steps.loop(i, 4)
                step(1, i, True)
                step(2, i, True)
                steps.end(3)
            step(7, nxt=False)
            ot_lo(7, 7)

            def residual(u0, base, first_bank, n, ln_base):
                def add(g, t):
                    dve.wait_ge(out_ready, base + g * TT + t + 1)
                    to = x[:, t, g * HALF:(g + 1) * HALF]
                    dve.tensor_tensor(to, ps[:, (first_bank + 4 * g) % 8 + t, :], to, ALU.add).then_inc(evacuated, 1)

                def rows(t):
                    add(1, t)
                    dve.wait_ge(evacuated, base + TT + t + 1)

                for k in range(4):
                    split(u0 + k + AHEAD)
                    if k == 1:
                        for t in range(TT):
                            add(0, t)
                norm(n, ln_base, rows)

            dve.wait_ge(x_reloaded, 16)
            residual(U_WO, O_WO, 0, 1, O_LN2)

            dve.wait_ge(rope_loaded, 16)
            dve.wait_ge(xn_ready, 2 * TT)
            cos8 = cos_t.unsqueeze(1).to_broadcast([P, 8, DH])
            sin4 = sin_t.rearrange("p (n w) -> p n w", w=2)

            def rope(g, t, i):
                n = 4 * g + t
                bank = 4 * (1 - g) + t
                dve.wait_ge(out_ready, O_QKV + n + 1 + 8 * i)
                dve.wait_ge(evacuated, O_QKV + n - 1 + 8 * i)
                a, b = rope_a[:, t % 2, :], rope_b[:, t % 2, :]
                steps.done(dve.tensor_tensor(a.rearrange("p (h d) -> p h d", d=DH),
                                             ps[:, bank, :].rearrange("p (h d) -> p h d", d=DH), cos8, ALU.mult))
                pw = ps[:, bank, :].rearrange("p (h n w) -> p h n w", n=DH // 2, w=2)
                bw = b.rearrange("p (h n w) -> p h n w", n=DH // 2, w=2)
                for w in range(2):
                    steps.done(dve.tensor_tensor(bw[:, :, :, w], pw[:, :, :, 1 - w],
                                                 sin4[:, :, w].unsqueeze(1).to_broadcast([P, 8, DH // 2]), ALU.mult))
                steps.wait()
                dve.tensor_tensor(qk[:, t, bass.ds(i * D + g * HALF, HALF)], a, b, ALU.add).then_inc(evacuated, 1)

            with dve.Fori(0, 2) as i:
                steps.loop(i, 24)
                for k in range(4):
                    split(U_QKV + k + AHEAD, RING, i)
                    if k % 2:
                        for t in range(TT):
                            rope(k // 2, t, i)
                steps.end(2)
            dve.wait_ge(x_mid_stored, 16)
            for k in range(4):
                split(U_QKV + 8 + k + AHEAD)
                if k % 2:
                    g = k // 2
                    for t in range(TT):
                        dve.wait_ge(out_ready, O_QKV + 16 + 4 * g + t + 1)
                        dve.tensor_copy(v[:, t, g * HALF:(g + 1) * HALF], ps[:, 4 * (1 - g) + t, :])\
                           .then_inc(evacuated, 1)

            def heads_scores(t):
                dve.wait_ge(hs_ready, t + 1)
                s3 = sc[:, t % 2, :].rearrange("p (h n) -> p h n", n=DH)
                dve.scalar_tensor_tensor(out=s3, in0=ps[:, 4:6, :].rearrange("p a (c n) -> p (a c) n", n=DH),
                                         scalar=HEAD_SCALE, in1=mask_t.unsqueeze(1).to_broadcast([P, H, DH]),
                                         op0=ALU.mult, op1=ALU.add).then_inc(hs_used, 1)
                dve.wait_ge(hs_used, t + 1)
                steps.done(dve.tensor_reduce(hmx, s3, AX.X, ALU.max))
                steps.wait()
                dve.tensor_tensor(s3, s3, hmx.unsqueeze(2).to_broadcast([P, H, DH]),
                                  ALU.subtract).then_inc(hs_shifted, 1)

            def heads_norm(t):
                s3 = sc[:, t % 2, :].rearrange("p (h n) -> p h n", n=DH)
                dve.wait_ge(hs_exp, t + 1)
                steps.done(dve.tensor_reduce(hsum, s3, AX.X, ALU.add))
                steps.wait()
                steps.done(dve.reciprocal(hinv, hsum))
                steps.wait()
                dve.tensor_tensor(s3, s3, hinv.unsqueeze(2).to_broadcast([P, H, DH]),
                                  ALU.mult).then_inc(hp_ready, 1)

            def heads_out(t):
                dve.wait_ge(ho_hi, t + 1)
                to = [a[:, :, t * P:(t + 1) * P].rearrange("p c (b n) -> p b c n", b=2) for a in (act_lo, act_hi)]
                dve.tensor_tensor(to[0], ps[:, 6:8, :].rearrange("p b (c n) -> p b c n", c=C), to[1],
                                  ALU.subtract).then_inc(ho_split, 1)

            heads_scores(0)
            heads_norm(0)
            for t in range(TT):
                if t + 1 < TT:
                    heads_scores(t + 1)
                    heads_norm(t + 1)
                heads_out(t)
            dve.wait_ge(x_mid_loaded, 16)
            residual(U_WOUT, O_WOUT, 4, 2, O_LN3)

            def sm(j):
                return small[:, j, :]

            def sm3(j):
                return small[:, j, :].rearrange("p (t e) -> p t e", e=NE)

            def dep(ins):
                steps.done(ins)
                steps.wait()

            dve.wait_ge(route_loaded, 16)
            dve.wait_ge(temp_loaded, 16)
            dep(dve.reciprocal(temp, temp))
            dve.wait_ge(logits_turned, 1)
            dve.tensor_scalar(sm(0), ps[:, 1, 0:TT * NE], temp, None, ALU.mult).then_inc(z_ready, 1)
            dve.wait_ge(ez_ready, 1)
            dep(dve.tensor_scalar(sm(2), sm(1), 1.0, None, ALU.add))
            dep(dve.reciprocal(sm(3), sm(2)))
            dep(dve.tensor_scalar(sm(7), sm(3), LOWER, None, ALU.is_ge))
            dep(dve.scalar_tensor_tensor(out=sm(7), in0=sm(3), scalar=UPPER, in1=sm(7),
                                         op0=ALU.is_le, op1=ALU.mult))
            dep(dve.tensor_scalar(sm(8), sm(3), -1.0, CENTER, ALU.mult, ALU.add))
            dep(dve.tensor_scalar(sm(9), sm(3), CENTER, None, ALU.subtract))
            dve.tensor_tensor(sm(4), sm(8), sm(9), ALU.max).then_inc(dist_ready, 1)
            dve.wait_ge(edist_ready, 2)
            dep(dve.tensor_tensor(sm(5), sm(5), sm(7), ALU.mult))
            dep(dve.tensor_reduce(small[:, 10, 0:TT], sm3(5), AX.X, ALU.add))
            dep(dve.tensor_scalar(small[:, 10, TT:2 * TT], small[:, 10, 0:TT], 1e-8, None, ALU.is_lt))
            larger, equal = (silu[:, j, :].rearrange("p (t e j) -> p t e j", e=NE, j=NE) for j in range(2))
            other = sm3(6).unsqueeze(2).to_broadcast([P, TT, NE, NE])
            own = sm3(6).unsqueeze(3).to_broadcast([P, TT, NE, NE])
            steps.done(dve.tensor_tensor(larger, other, own, ALU.is_gt))
            dep(dve.tensor_tensor(equal, other, own, ALU.is_ge))
            dep(dve.tensor_tensor(equal, equal, earlier_expert.rearrange("p (e j) -> p e j", j=NE).unsqueeze(1)
                                  .to_broadcast([P, TT, NE, NE]), ALU.mult))
            dep(dve.tensor_tensor(larger, larger, equal, ALU.max))
            dep(dve.tensor_reduce(sm3(11), larger, AX.X, ALU.add))
            dep(dve.scalar_tensor_tensor(out=sm(13), in0=sm(11), scalar=2.0, in1=sm(6),
                                         op0=ALU.is_lt, op1=ALU.mult))

            def normalised(j, at):
                dep(dve.tensor_reduce(small[:, 14, at:at + TT], sm3(j), AX.X, ALU.add))
                dep(dve.tensor_scalar(small[:, 14, at:at + TT], small[:, 14, at:at + TT], 1e-8, None, ALU.max))
                dep(dve.reciprocal(small[:, 14, at + TT:at + 2 * TT], small[:, 14, at:at + TT]))
                dep(dve.tensor_tensor(sm3(j), sm3(j),
                                      small[:, 14, at + TT:at + 2 * TT].unsqueeze(2).to_broadcast([P, TT, NE]),
                                      ALU.mult))

            normalised(13, 0)
            flag = small[:, 10, TT:2 * TT].unsqueeze(2).to_broadcast([P, TT, NE])
            dep(dve.tensor_tensor(sm3(13), sm3(13), flag, ALU.mult))
            dep(dve.tensor_scalar(small[:, 10, 2 * TT:3 * TT], small[:, 10, TT:2 * TT], -1.0, 1.0, ALU.mult, ALU.add))
            dep(dve.tensor_tensor(sm3(5), sm3(5), small[:, 10, 2 * TT:3 * TT].unsqueeze(2).to_broadcast([P, TT, NE]),
                                  ALU.mult))
            dep(dve.tensor_tensor(sm(5), sm(5), sm(13), ALU.add))
            normalised(5, 2 * TT)
            dve.wait_ge(edist_ready, 2)
            dve.tensor_scalar(sm(0), sm(5), 0.0, None, ALU.is_gt).then_inc(member_ready, 1)
            dep(dve.tensor_copy(item_w[:, :, 0:NE], sm3(5)))
            dve.wait_ge(rank_ready, 1)
            dep(dve.scalar_tensor_tensor(out=sm(1), in0=ps[:, 0, 0:TT * NE], scalar=1.0, in1=sm(0),
                                         op0=ALU.add, op1=ALU.mult))
            dep(dve.tensor_scalar(item_slot[:, :, 0:NE], sm3(1), 1.0, None, ALU.subtract))

            def build_sel(slot_of):
                for t in range(TT):
                    dve.tensor_scalar(sel[:, t, :], places[:, t // TPH, :], slot_of(t), None,
                                      ALU.is_equal).then_inc(sel_built, 1)

            build_sel(lambda t: item_slot[:, t, 0:1])

            dve.wait_ge(counts_ready, 1)
            dve.tensor_copy(small[:, 2, 0:2 * NE], ps[:, 1, 0:NT * NE]).then_inc(sc_done, 1)
            dve.wait_ge(sc_done, 1)
            count0, count1, has = (small[:, 2, j * NE:(j + 1) * NE] for j in range(3))
            number = count0
            dep(dve.tensor_tensor(has, count0, count1, ALU.max))
            dep(dve.tensor_scalar(has, has, float(P), None, ALU.is_gt))
            dep(dve.memset(number[:, 0:1], 0.0))
            for e in range(NE - 1):
                dep(dve.tensor_tensor(number[:, e + 1:e + 2], number[:, e:e + 1], has[:, e:e + 1], ALU.add))
            one = small[:, 6:8, :].rearrange("p a (x e) -> p (a x) e", e=NE)
            for j in range(NE):
                steps.done(dve.scalar_tensor_tensor(out=one[:, j, :], in0=number, scalar=float(j), in1=has,
                                                    op0=ALU.is_equal, op1=ALU.mult))
            steps.wait()
            over = small[:, 3, :].rearrange("p (t e) -> p t e", e=NE)
            dep(dve.tensor_scalar(over, item_slot[:, :, 0:NE], float(P), None, ALU.subtract))
            both = small[:, 8:10, :].rearrange("p a (x e) -> p (a x) e", e=NE)
            for t in range(TT):
                for src, to in ((over, item_slot), (sm3(5), item_w)):
                    dep(dve.tensor_tensor(both, one, src[:, t:t + 1, :].to_broadcast([P, NE, NE]), ALU.mult))
                    dep(dve.tensor_reduce(to[:, t, NE:ITEMS], both, AX.X, ALU.add))
            dep(dve.tensor_tensor(both, one, expert_ids.unsqueeze(1).to_broadcast([P, NE, NE]), ALU.mult))
            dep(dve.tensor_reduce(small[:, 10, 1:NE + 1], both, AX.X, ALU.add))
            dep(dve.tensor_reduce(small[:, 10, 0:1], has, AX.X, ALU.add))
            dve.tensor_copy(meta[:, :], small[:, 10, 0:NE + 1]).then_inc(meta_ready, 1)
            dve.wait_ge(meta_ready, 1)

            def item(e, u0, first, more):
                at = lambda a, t, n: a[:, t, bass.ds(e + n, 1)]

                def add_sums(g):
                    for t in range(TT):
                        dve.wait_ge(sc_ready, 8 * e + (4 * g + t + 1))
                        to = x[:, t, g * HALF:(g + 1) * HALF]
                        dve.scalar_tensor_tensor(out=to, in0=ps[:, SC_BANK[t], :], scalar=at(item_w, t, 0), in1=to,
                                                 op0=ALU.mult, op1=ALU.add).then_inc(sc_done, 1)

                if first:
                    for k in range(AHEAD):
                        split(u0 + k, PER_EXPERT, e)
                    dve.wait_ge(selt_ready, NT * e)
                    build_sel(lambda t: at(item_slot, t, 0))
                for k in range(PER_EXPERT):
                    if more or k + AHEAD < PER_EXPERT:
                        split(u0 + k + AHEAD, PER_EXPERT, e)
                    if k < 8:
                        dve.wait_ge(silu_done, 8 * e + (k + 1))
                        steps.done(dve.tensor_tensor(silu[:, k % 2, :], ps[:, k % 2, CAP:2 * CAP],
                                                     silu[:, k % 2, :], ALU.mult))
                        steps.wait()
                        steps.done(dve.tensor_copy(h_hi[:, k, :], silu[:, k % 2, :]))
                        steps.wait()
                        dve.tensor_tensor(h_lo[:, k, :], silu[:, k % 2, :], h_hi[:, k, :],
                                          ALU.subtract).then_inc(h_split, 1)
                    if k == 3 and more:
                        dve.wait_ge(selt_ready, NT * e + NT)
                        build_sel(lambda t: at(item_slot, t, 1))
                    if k in (9, 11):
                        g = (k - 9) // 2
                        cols = slice(g * HALF, (g + 1) * HALF)
                        for n in range(NT):
                            dve.wait_ge(y_hi_done, 4 * e + (2 * g + n + 1))
                            dve.tensor_tensor(y[:, 1, n, cols], ps[:, Y_BANK[g] + n, :], y[:, 0, n, cols],
                                              ALU.subtract).then_inc(y_split, 1)
                    if k >= 10:
                        add_sums(k - 10)

            with dve.Fori(0, NE - 1) as e:
                steps.loop(e, 16)
                item(e, U_FFN, False, True)
                steps.end(NE - 1)
            item(NE - 1, U_FFN, False, False)
            more = dve.value_load(meta[0:1, 0:1], min_val=0, max_val=NE)
            with dve.If(more > 0):
                with dve.Fori(0, more) as j:
                    steps.loop(j, 16)
                    item(j + NE, U_FFN, True, False)
                    steps.end(0)

        @block.tensor
        def _(pe):
            def unit_ready(k, per=0, i=0):
                pe.wait_ge(lo_done, k + 1 + per * i)

            def three(out, a_hi, a_lo, b_hi, b_lo, first, last):
                pe.matmul(out, a_hi, b_hi, start=first, stop=False)
                pe.matmul(out, a_hi, b_lo, start=False, stop=False)
                return pe.matmul(out, a_lo, b_hi, start=False, stop=last)

            def norm(n, base, t):
                if n == 0 and t == 0:
                    pe.wait_ge(ident_loaded, 16)
                pe.wait_ge(xn_ready, TT * n + t + 1)
                for h in range(2):
                    j = 2 * t + h
                    if j >= 4 or n > 0:
                        pe.wait_ge(evacuated, base + j - 3 if j >= 4 else base - TT)
                    for c in range(4):
                        ins = pe.transpose(ps[:, LN_BANK[n] + j % 4, c * P:(c + 1) * P],
                                           xn_rows(n, t)[:, (4 * h + c) * P:(4 * h + c + 1) * P], ident)
                    ins.then_inc(out_ready, 1)

            def stationary_unit(k, out, wait, per=0, i=0):
                unit_ready(k, per, i)
                for j in range(2):
                    wait(j)
                    for c in range(C):
                        at = slice(j * D + c * P, j * D + (c + 1) * P)
                        ins = three(ps[:, out(j), :], hi[:, k % RING, at], lo[:, k % RING, at],
                                    act_hi[:, c, :], act_lo[:, c, :], c == 0, c == C - 1)
                    yield ins

            def projection(u0, base, first_bank=4, per=0, i=0, out_per=0, before=lambda half, t: None):
                for g in range(2):
                    bank = (first_bank + 4 * g) % 8
                    for half in range(2):
                        k = u0 + 2 * g + half
                        ins = None
                        unit_ready(k, per, i)
                        for t in range(TT):
                            if g == 0:
                                before(half, t)
                            if half == 0:
                                pe.wait_ge(evacuated, base + 4 * g + t - 7 + out_per * i)
                            for c in range(4):
                                cc = 4 * half + c
                                rows = slice(t * P, (t + 1) * P)
                                cols = slice(c * HALF, (c + 1) * HALF)
                                ins = three(ps[:, bank + t, :], act_hi[:, cc, rows], act_lo[:, cc, rows],
                                            hi[:, k % RING, cols], lo[:, k % RING, cols], cc == 0, cc == C - 1)
                            if half == 1:
                                ins.then_inc(out_ready, 1)
                        if half == 0:
                            ins.then_inc(unit_used, 1)

            for t in range(TT):
                norm(0, O_LN1, t)
            pe.wait_ge(evacuated, O_LN1 + 2 * TT)
            with pe.Fori(0, 2) as i:
                for k in range(RING):
                    def bank_free(j):
                        pe.wait_ge(evacuated, O_QK + 2 * k + j - 3 + 8 * i)
                    for j, ins in enumerate(stationary_unit(k, lambda j: (2 * k + j) % 4, bank_free, RING, i)):
                        ins.then_inc(out_ready, 1)
            projection(U_V, O_V)

            def score_block(s, u, i=0, per=0):
                k = U_KEYS0 + u if s == 0 else U_KEYS0 + 7 + PER_BATCH * (s - 1) + u
                j = u // 2
                if u == 0:
                    pe.wait_ge(q_split, s + 1 + 2 * i)
                if u % 2 == 0:
                    if s == 0:
                        pe.wait_ge(evacuated, O_V + 4 + j + 1)
                    else:
                        pe.wait_ge(s_evac, 4 * (s - 1) + j + 1 + 8 * i)
                unit_ready(k, per, i)
                n = 4 if u < 6 else C
                w = HALF if u < 6 else KTAIL + QL
                for c in range(n):
                    cc = 4 * (u % 2) + c
                    for b, buf in enumerate((hi, lo)):
                        ins = pe.matmul(ps[:, j, 0:w], qs[:, s % 2, cc, :], buf[:, k % RING, c * w:(c + 1) * w],
                                        start=(cc == 0 and b == 0), stop=(cc == C - 1 and b == 1))
                if u % 2 or u == 6:
                    ins.then_inc(s_ready, 1)
                else:
                    ins.then_inc(unit_used, 1)

            def turned(out, rows, after_wait):
                if after_wait:
                    return pe.matmul(out, rows, ident[0:QL, 0:QL], start=True, stop=True)
                return pe.transpose(out, rows, ident[0:QL, 0:QL])

            def turn_o(s, i=0):
                pe.wait_ge(o_norm, s + 1 + 2 * i)
                for c in range(C):
                    ins = turned(ps[:, 6, c * QL:(c + 1) * QL], O[:, c * P:(c + 1) * P], c == 0)
                ins.then_inc(ot_ready, 1)

            def step(s, i=0, loop=False, nxt=True):
                per = 2 * PER_BATCH if loop else 0
                k0 = U_KEYS0 + 7 + PER_BATCH * s
                if nxt:
                    score_block(s + 1, 0, i, per)
                    score_block(s + 1, 1, i, per)
                if s > 0:
                    turn_o(s - 1, i)
                if nxt:
                    for u in range(2, 4):
                        score_block(s + 1, u, i, per)
                pe.wait_ge(p_ready, s + 1 + 2 * i)
                for kc in range(NCH):
                    a = kc * P if kc < 13 else KV
                    n = P if kc < 12 else (KREM if kc == 12 else QL)
                    ins = turned(ps[0:n, 4 + kc // 8, (kc % 8) * QL:(kc % 8 + 1) * QL],
                                 S[0:QL, s % 2, a:a + n], kc == 0)
                    if kc in (7, NCH - 1):
                        ins.then_inc(pt_ready, 1)
                if nxt:
                    for u in range(4, 7):
                        score_block(s + 1, u, i, per)
                for u in range(7):
                    k = k0 + u + (7 if nxt else 0)
                    if u == 0:
                        pe.wait_ge(pt_split, 2 * s + 1 + 4 * i)
                        if s > 0:
                            pe.wait_ge(o_evac, s + 2 * i)
                            pe.wait_ge(ot_split, s + 2 * i)
                    if u == 4:
                        pe.wait_ge(pt_split, 2 * s + 2 + 4 * i)
                    unit_ready(k, per, i)
                    for j in range(2):
                        kc = 2 * u + j
                        n = P if kc < 12 else (KREM if kc == 12 else QL)
                        for h in range(2):
                            at = slice(j * D + h * HALF, j * D + (h + 1) * HALF)
                            for b, buf in enumerate((hi, lo)):
                                ins = pe.matmul(ps[:, 6 + h, :], pt[0:n, kc, :], buf[0:n, k % RING, at],
                                                start=(kc == 0 and b == 0), stop=(kc == NCH - 1 and b == 1))
                    if u == 6:
                        ins.then_inc(o_ready, 1)
                    else:
                        ins.then_inc(unit_used, 1)

            for u in range(7):
                score_block(0, u)
            step(0)
            with pe.Fori(0, 3) as i:
                step(1, i, True)
                step(2, i, True)
            step(7, nxt=False)

            def before_wo(half, t):
                if half == 0 and t == 0:
                    pe.wait_ge(ot_split, B - 2)
                    pe.wait_ge(s_evac, 4 * B)
                elif half == 0 and t == 2:
                    turn_o(7)
                elif half == 0 and t == 3:
                    pe.wait_ge(ot_split, B)

            projection(U_WO, O_WO, 0, before=before_wo)

            def before_qkv(half, t):
                pe.wait_ge(evacuated, O_LN2 + 2 * t + half + 1)
                if half == 0 and t < 2:
                    norm(1, O_LN2, t + 2)

            norm(1, O_LN2, 0)
            norm(1, O_LN2, 1)
            projection(U_QKV, O_QKV, before=before_qkv)
            with pe.Fori(1, 3) as i:
                projection(U_QKV, O_QKV, 4, RING, i, 8)

            pe.wait_ge(evacuated, O_QKV + 24)

            def heads_front(t):
                for w in range(2):
                    for c in range(C):
                        ins = pe.transpose(ps[:, 2 * w + c // 4, (c % 4) * P:(c % 4 + 1) * P],
                                           qk[:, t, w * D + c * P:w * D + (c + 1) * P], ident)
                    ins.then_inc(tq_ready, 1)
                pe.wait_ge(tq_evac, 2 * t + 2)
                if t >= 1:
                    pe.wait_ge(hs_used, t)
                for r in range(2):
                    for c in range(C):
                        for b in range(2):
                            ins = pe.matmul(ps[b * QL:(b + 1) * QL, 4 + r, c * DH:(c + 1) * DH],
                                            qkt[r * DH:(r + 1) * DH, c, b * QL:(b + 1) * QL],
                                            qkt[r * DH:(r + 1) * DH, C + c, b * QL:(b + 1) * QL],
                                            start=True, stop=True)
                ins.then_inc(hs_ready, 1)

            def heads_back(t):
                pe.wait_ge(hp_ready, t + 1)
                for m in range(H // 2):
                    ins = pe.transpose(ps[:, m // 4, (m % 4) * P:(m % 4 + 1) * P],
                                       sc[:, t % 2, m * P:(m + 1) * P], ident)
                ins.then_inc(hpt_ready, 1)
                pe.wait_ge(hpt_evac, 4 * (t + 1))
                if t >= 1:
                    pe.wait_ge(ho_split, t)
                for c in range(C):
                    for b in range(2):
                        for r in range(2):
                            h = 2 * c + r
                            ins = pe.matmul(ps[r * DH:(r + 1) * DH, 6 + b, c * QL:(c + 1) * QL],
                                            v[b * QL:(b + 1) * QL, t, h * DH:(h + 1) * DH],
                                            pth[b * QL:(b + 1) * QL, r * C + c, :], start=True, stop=True)
                ins.then_inc(ho_ready, 1)

            heads_front(0)
            for t in range(TT):
                if t + 1 < TT:
                    heads_front(t + 1)
                heads_back(t)
            pe.wait_ge(ho_split, TT)
            projection(U_WOUT, O_WOUT)
            for t in range(TT):
                norm(2, O_LN3, t)

            pe.wait_ge(wr_split, 1)
            for n in range(NT):
                pe.wait_ge(evacuated, O_LN3 + 2 * TPH * (n + 1))
                cols = slice(n * HTOK, (n + 1) * HTOK)
                for c in range(C):
                    ins = three(ps[0:NE, 0, cols], wr_hi[:, c, :], wr_lo[:, c, :], act_hi[:, c, cols],
                                act_lo[:, c, cols], c == 0, c == C - 1)
            ins.then_inc(logits_ready, 1)
            pe.wait_ge(logits_out, 1)
            for t in range(TT):
                ins = pe.matmul(ps[:, 1, t * NE:(t + 1) * NE], logits_t[:, t * P:(t + 1) * P], ident[0:NE, 0:NE],
                                start=True, stop=True)
            ins.then_inc(logits_turned, 1)

            pe.wait_ge(member_ready, 1)
            pe.wait_ge(count_loaded, 16)
            member = small[:, 0, :].rearrange("p (t e) -> p t e", e=NE)
            ins = pe.matmul(ps[:, 0, 0:TT * NE], earlier, small[:, 0, :], start=True, stop=False)
            for n in range(NT):
                for t in range(1, TPH):
                    for u in range(t):
                        tt = n * TPH + t
                        ins = pe.matmul(ps[:, 0, tt * NE:(tt + 1) * NE], ones, member[:, n * TPH + u, :],
                                        start=False, stop=(n == NT - 1 and t == TPH - 1 and u == t - 1))
            ins.then_inc(rank_ready, 1)
            for n in range(NT):
                for u in range(TPH):
                    ins = pe.matmul(ps[:, 1, n * NE:(n + 1) * NE], ones, member[:, n * TPH + u, :],
                                    start=(u == 0), stop=(u == TPH - 1))
            ins.then_inc(counts_ready, 1)

            def gather(e):
                for c in range(C):
                    if c == 0:
                        pe.wait_ge(sel_built, TT * e + TT)
                    if c >= 4:
                        pe.wait_ge(xg_done, C * e + (c - 3))
                    for h, src in enumerate((x_tok_hi, x_tok_lo)):
                        for t in range(TT):
                            ins = pe.matmul(ps[:, 2 + c % 4, h * CAP:(h + 1) * CAP], src[:, t, c * P:(c + 1) * P],
                                            sel[:, t, :], start=(t == 0), stop=(t == TT - 1))
                    ins.then_inc(xg_ready, 1)

            def item(e, u0, first, more):
                if first:
                    pe.wait_ge(sc_done, 8 * e + 1)
                    gather(e)

                def turn_selection():
                    for n in range(NT):
                        for t in range(TPH):
                            ins = pe.matmul(ps[:, 6 + n, t * P:(t + 1) * P], sel[:, TPH * n + t, n * P:(n + 1) * P],
                                            ident_r[:, :], start=True, stop=True)
                        ins.then_inc(selt_ready, 1)

                def sums(g):
                    for t in range(TT):
                        if t % TPH == 0:
                            pe.wait_ge(y_split, 4 * e + (2 * g + t // TPH + 1))
                        if g == 1:
                            pe.wait_ge(sc_done, 8 * e + (t + 2))
                        n, u = t // TPH, t % TPH
                        for h in range(2):
                            ins = pe.matmul(ps[:, SC_BANK[t], :], selt[:, n, u * P:(u + 1) * P],
                                            y[:, h, n, g * HALF:(g + 1) * HALF], start=(h == 0), stop=(h == 1))
                        ins.then_inc(sc_ready, 1)

                pe.wait_ge(xg_done, C * e + C)
                for f in range(8):
                    k = u0 + f
                    unit_ready(k, PER_EXPERT, e)
                    if f >= 2:
                        pe.wait_ge(h_split, 8 * e + (f - 1))
                    elif f == 0:
                        pe.wait_ge(sc_done, 1)
                    for j in range(2):
                        for c in range(C):
                            at = slice(j * D + c * P, j * D + (c + 1) * P)
                            ins = three(ps[:, f % 2, j * CAP:(j + 1) * CAP], hi[:, k % RING, at], lo[:, k % RING, at],
                                        xg[:, c, 0:CAP], xg[:, c, CAP:2 * CAP], c == 0, c == C - 1)
                    ins.then_inc(gu_ready, 1)
                    if f == 1:
                        pe.wait_ge(sc_done, 8 * e + 1)
                        turn_selection()
                if more:
                    gather(e + 1)
                for g in range(2):
                    for half in range(2):
                        k = u0 + 8 + 2 * g + half
                        if g == 0:
                            pe.wait_ge(h_split, 8 * e + 4 * (half + 1))
                            if half == 0:
                                pe.wait_ge(selt_done, NT * e + NT)
                        elif half == 0 and more:
                            pe.wait_ge(xg_done, C * e + 2 * C)
                        if g == 1 and half == 1:
                            sums(0)
                        unit_ready(k, PER_EXPERT, e)
                        for n in range(NT):
                            for c in range(4):
                                cc = 4 * half + c
                                rows = slice(n * P, (n + 1) * P)
                                cols = slice(c * HALF, (c + 1) * HALF)
                                ins = three(ps[:, Y_BANK[g] + n, :], h_hi[:, cc, rows], h_lo[:, cc, rows],
                                            hi[:, k % RING, cols], lo[:, k % RING, cols], cc == 0, cc == C - 1)
                            if half == 1:
                                ins.then_inc(y_ready, 1)
                        if half == 0:
                            ins.then_inc(unit_used, 1)
                sums(1)

            pe.wait_ge(x_tok_split, TT)
            pe.wait_ge(ident_r_set, 1)
            gather(0)
            with pe.Fori(0, NE - 1) as e:
                item(e, U_FFN, False, True)
            item(NE - 1, U_FFN, False, False)
            pe.wait_ge(meta_ready, 1)
            more = pe.value_load(meta[0:1, 0:1], min_val=0, max_val=NE)
            with pe.If(more > 0):
                with pe.Fori(0, more) as j:
                    item(j + NE, U_FFN, True, False)


def kernel(**inputs):
    import numpy as np
    import concourse.bacc as _bacc
    from concourse.bass_utils import run_bass_kernel_spmd as _run

    g = {k: np.asarray(v) for k, v in inputs.items()}

    def stationary(w):
        return w.reshape(C, P, -1, P).transpose(2, 1, 0, 3).reshape(-1, P, D)

    def pairs(a, b):
        return np.stack([a, b], axis=2).reshape(-1, P, UNIT)

    def moving(w):
        return w.reshape(2, 4, P, -1, HALF).transpose(3, 0, 2, 1, 4).reshape(-1, P, UNIT)

    wq, wk = stationary(g["L0_xattn_wq"].T), stationary(g["L0_xattn_wk"].T)
    qkv = g["L0_attn_w_qkv"].reshape(4, 3, D // 4, D)
    units = [pairs(wq[0::2], wq[1::2]), pairs(wk[0::2], wk[1::2]), moving(g["L0_xattn_wv"].T),
             moving(g["L0_xattn_wo"].T)]
    units += [moving(qkv[:, n].reshape(D, D).T) for n in (0, 2, 1)]
    units.append(moving(g["L0_attn_w_out"].T))
    for e in range(NE):
        units.append(pairs(stationary(g["L0_ffn_Wg"][e]), stationary(g["L0_ffn_Wu"][e])))
        units.append(moving(g["L0_ffn_Wd"][e]))
    weights = np.concatenate(units)
    context = g["ctx_2048"]
    keys = context[:, :KFULL].reshape(B, 3, HALF, 2, 4, P).transpose(0, 1, 3, 5, 4, 2).reshape(B, 6, P, UNIT)
    tail = context[:, KFULL - 1:].reshape(B, KTAIL, C, P).transpose(0, 3, 2, 1)

    pos = np.arange(P, dtype=np.float32) % QL
    inv = (1.0 / 10000.0 ** (np.arange(0, DH, 2, dtype=np.float32) / DH)).astype(np.float32)
    ang = pos[:, None] * inv[None, :]
    rope = np.zeros((P, ROPE), np.float32)
    rope[:, 0:DH] = np.repeat(np.cos(ang), 2, axis=1)
    rope[:, DH:2 * DH:2] = -np.sin(ang)
    rope[:, DH + 1:2 * DH:2] = np.sin(ang)
    rope[:, 2 * DH:3 * DH] = np.where(np.arange(QL)[None, :] > pos[:, None], -3.0e38, 0.0)
    route = np.zeros((P, ROUTE), np.float32)
    route[:, 0:NT * CAP] = NO_PLACE
    for n in range(NT):
        route[:, n * CAP + n * P:n * CAP + (n + 1) * P] = np.arange(P)
    route[:, NT * CAP:NT * CAP + NE] = np.arange(NE)
    route[:, NT * CAP + NE:] = (np.arange(NE)[None, :] < np.arange(NE)[:, None]).reshape(-1)
    count = np.ones((P, 2 * P), np.float32)
    count[:, 0:P] = np.arange(P)[:, None] < np.arange(P)[None, :]

    arrays = {
        "x_in": g["x"].reshape(TOK, D),
        "context": context,
        "keys": keys,
        "key_tail": tail,
        "weights": weights,
        "router": g["L0_ffn_Wr"].reshape(C, P, NE).transpose(1, 0, 2),
        "temperature": np.broadcast_to(g["L0_ffn_temperature"].reshape(1, 1), (P, 1)),
        "identity": np.eye(P, dtype=np.float32),
        "rope": rope,
        "route": route,
        "count": count,
    }
    arrays = {k: np.ascontiguousarray(v) for k, v in arrays.items()}
    nc = _bacc.Bacc("TRN2", target_bir_lowering=False, num_devices=1)
    args = [nc.dram_tensor(k, v.shape, F32, kind="ExternalInput").ap() for k, v in arrays.items()]
    out = nc.dram_tensor("out", (TOK, D), F32, kind="ExternalOutput").ap()
    perceiver_block(nc, *args, out)
    r = _run(nc, [arrays], core_ids=[0])
    return r.results[0]["out"].reshape(B, QL, D)
```
